# Optimizing a Trainium2 kernel written in Bass

```python
import numpy as np
import jax
import jax.numpy as jnp

def _softmax(x, axis=-1):
    return jax.nn.softmax(x, axis=axis)

def _gelu(x):
    return jax.nn.gelu(x, approximate=True)

def _silu(x):
    return jax.nn.silu(x)

def _sigmoid(x):
    return jax.nn.sigmoid(x)

def _layernorm(x, axis=-1, eps=1e-05):
    m = jnp.mean(x, axis=axis, keepdims=True)
    v = jnp.var(x, axis=axis, keepdims=True)
    return (x - m) / jnp.sqrt(v + eps)

def _scatter_add(tgt, idx, src, axis=0):
    return tgt.at[idx].add(src)

def _segment_sum(src, seg, n):
    return jax.ops.segment_sum(src, seg, n)
kernel_name = 'mk_sandwich_d2_jaxref_r8_2efd0b'

def setup_inputs(seed: int=0):
    np.random.seed(seed)
    _w = jnp.asarray

    def _L0_attn_setup():
        import jax, jax.numpy as jnp
        import numpy as np
        B, S, E = (2, 256, 128)
        H = 16
        D = E // H
        key = jax.random.key(seed)
        ks = jax.random.split(key, 11)
        s = 1.0 / np.sqrt(E)
        return {'x': jax.random.normal(ks[0], (B, S, E), dtype=jnp.float32), 'Wq': jax.random.uniform(ks[1], (E, E), jnp.float32, -s, s), 'bq': jnp.zeros((E,), jnp.float32), 'Wk': jax.random.uniform(ks[2], (E, E), jnp.float32, -s, s), 'bk': jnp.zeros((E,), jnp.float32), 'Wv': jax.random.uniform(ks[3], (E, E), jnp.float32, -s, s), 'bv': jnp.zeros((E,), jnp.float32), 'Wo': jax.random.uniform(ks[4], (E, E), jnp.float32, -s, s), 'bo': jnp.zeros((E,), jnp.float32), 'J_attn': jax.random.normal(ks[5], (H, D, D), jnp.float32) * 0.02, 'lambda_attn': jnp.float32(0.5)}
    _L0_attn_in = _L0_attn_setup()

    def _L0_ffn_setup():
        import jax, jax.numpy as jnp
        import numpy as np
        TOPK = 8
        NUM_EXPERTS = 64
        FFN = 384
        CAPACITY = 160

        def _swiglu(x, w1, w2):
            h = x @ w1.T
            x1, x2 = jnp.split(h, 2, axis=-1)
            return x1 * jax.nn.silu(x2) @ w2.T
        key = jax.random.key(seed)
        ks = jax.random.split(key, 6)
        B, S, H = (1, 64, 128)
        scale = 0.02
        return {'hidden_states': jax.random.normal(ks[0], (B, S, H), jnp.float32), 'wg': jax.random.normal(ks[1], (NUM_EXPERTS, H), jnp.float32) * scale, 'shared_w1': jax.random.normal(ks[2], (2 * FFN, H), jnp.float32) * scale, 'shared_w2': jax.random.normal(ks[3], (H, FFN), jnp.float32) * scale, 'expert_w1': jax.random.normal(ks[4], (NUM_EXPERTS, 2 * FFN, H), jnp.float32) * scale, 'expert_w2': jax.random.normal(ks[5], (NUM_EXPERTS, H, FFN), jnp.float32) * scale}
    _L0_ffn_in = _L0_ffn_setup()

    def _L1_attn_setup():
        import jax, jax.numpy as jnp
        import numpy as np
        from jax import lax
        D_MODEL = 128
        D_STATE = 16
        D_CONV = 4
        EXPAND = 2
        D_INNER = EXPAND * D_MODEL
        DT_RANK = (D_MODEL + 15) // 16
        B, L = (2, 256)
        EPS = 1e-05

        def _layernorm(x, g, b):
            mu = jnp.mean(x, axis=-1, keepdims=True)
            var = jnp.mean(jnp.square(x - mu), axis=-1, keepdims=True)
            return (x - mu) * lax.rsqrt(var + EPS) * g + b

        def _causal_dwconv(u, w, b):
            din, dc = w.shape
            up = jnp.pad(u, ((0, 0), (dc - 1, 0), (0, 0)))
            k = w.T[:, None, :]
            out = lax.conv_general_dilated(up, k, (1,), 'VALID', dimension_numbers=('NWC', 'WIO', 'NWC'), feature_group_count=din)
            return out + b

        def _mamba(h, in_proj_w, conv_w, conv_b, x_proj_w, dt_w, dt_b, A_log, D, out_proj_w):
            xz = h @ in_proj_w
            u, z = jnp.split(xz, 2, axis=-1)
            u = jax.nn.silu(_causal_dwconv(u, conv_w, conv_b))
            x_dbl = u @ x_proj_w
            dt, Bm, Cm = jnp.split(x_dbl, [DT_RANK, DT_RANK + D_STATE], axis=-1)
            delta = jax.nn.softplus(dt @ dt_w + dt_b)
            A = -jnp.exp(A_log)
            dA = jnp.exp(jnp.einsum('bld,dn->bldn', delta, A))
            dBu = jnp.einsum('bld,bln,bld->bldn', delta, Bm, u)

            def step(hst, inp):
                dA_t, dBu_t, C_t = inp
                hst = dA_t * hst + dBu_t
                y = jnp.einsum('bdn,bn->bd', hst, C_t)
                return (hst, y)
            h0 = jnp.zeros((u.shape[0], D_INNER, D_STATE), u.dtype)
            _, ys = lax.scan(step, h0, (dA.transpose(1, 0, 2, 3), dBu.transpose(1, 0, 2, 3), Cm.transpose(1, 0, 2)))
            y = ys.transpose(1, 0, 2) + u * D
            y = y * jax.nn.silu(z)
            return y @ out_proj_w
        key = jax.random.key(seed)
        ks = jax.random.split(key, 12)
        s = 0.02
        inp = {'x': jax.random.normal(ks[0], (B, L, D_MODEL), jnp.float32), 'ln_g': jnp.ones((D_MODEL,), jnp.float32), 'ln_b': jnp.zeros((D_MODEL,), jnp.float32), 'sq_w': jax.random.normal(ks[1], (D_MODEL, D_MODEL), jnp.float32) * s, 'sq_b': jnp.zeros((D_MODEL,), jnp.float32), 'srw_w': jax.random.normal(ks[2], (D_MODEL, D_MODEL), jnp.float32) * s, 'srw_b': jnp.zeros((D_MODEL,), jnp.float32), 'res_scale': jnp.ones((1,), jnp.float32), 'in_proj_w': jax.random.normal(ks[3], (D_MODEL, 2 * D_INNER), jnp.float32) * s, 'conv_w': jax.random.normal(ks[4], (D_INNER, D_CONV), jnp.float32) * 0.1, 'conv_b': jnp.zeros((D_INNER,), jnp.float32), 'x_proj_w': jax.random.normal(ks[5], (D_INNER, DT_RANK + 2 * D_STATE), jnp.float32) * s, 'dt_w': jax.random.normal(ks[6], (DT_RANK, D_INNER), jnp.float32) * s, 'dt_b': jnp.full((D_INNER,), -4.6, jnp.float32), 'A_log': jnp.log(jnp.broadcast_to(jnp.arange(1, D_STATE + 1, dtype=jnp.float32), (D_INNER, D_STATE))), 'D': jnp.ones((D_INNER,), jnp.float32), 'out_proj_w': jax.random.normal(ks[7], (D_INNER, D_MODEL), jnp.float32) * s}
        return inp
    _L1_attn_in = _L1_attn_setup()

    def _L1_ffn_setup():
        import jax, jax.numpy as jnp
        import numpy as np
        ALPHA = 2.0
        TOP_K = 2
        key = jax.random.key(seed)
        ks = jax.random.split(key, 8)
        B, S, D, H, E = (2, 256, 128, 512, 8)
        Er = E - 1
        s_in = 1.0 / np.sqrt(D)
        s_hid = 1.0 / np.sqrt(H)
        return {'x': jax.random.normal(ks[0], (B, S, D), dtype=jnp.float32), 'router_w': jax.random.normal(ks[1], (D, E), dtype=jnp.float32) * s_in, 'up_w': jax.random.normal(ks[2], (Er, D, H), dtype=jnp.float32) * s_in, 'gate_w': jax.random.normal(ks[3], (Er, D, H), dtype=jnp.float32) * s_in, 'down_w': jax.random.normal(ks[4], (Er, H, D), dtype=jnp.float32) * s_hid * 0.1, 'shared_up_w': jax.random.normal(ks[5], (D, H), dtype=jnp.float32) * s_in, 'shared_gate_w': jax.random.normal(ks[6], (D, H), dtype=jnp.float32) * s_in, 'shared_down_w': jax.random.normal(ks[7], (H, D), dtype=jnp.float32) * s_hid * 0.1}
    _L1_ffn_in = _L1_ffn_setup()
    _d = {'L0_attn_x': _L0_attn_in['x'], 'L0_attn_Wq': _L0_attn_in['Wq'], 'L0_attn_bq': _L0_attn_in['bq'], 'L0_attn_Wk': _L0_attn_in['Wk'], 'L0_attn_bk': _L0_attn_in['bk'], 'L0_attn_Wv': _L0_attn_in['Wv'], 'L0_attn_bv': _L0_attn_in['bv'], 'L0_attn_Wo': _L0_attn_in['Wo'], 'L0_attn_bo': _L0_attn_in['bo'], 'L0_attn_J_attn': _L0_attn_in['J_attn'], 'L0_attn_lambda_attn': _L0_attn_in['lambda_attn'], 'L0_ffn_wg': _L0_ffn_in['wg'], 'L0_ffn_shared_w1': _L0_ffn_in['shared_w1'], 'L0_ffn_shared_w2': _L0_ffn_in['shared_w2'], 'L0_ffn_expert_w1': _L0_ffn_in['expert_w1'], 'L0_ffn_expert_w2': _L0_ffn_in['expert_w2'], 'L1_attn_ln_g': _L1_attn_in['ln_g'], 'L1_attn_ln_b': _L1_attn_in['ln_b'], 'L1_attn_sq_w': _L1_attn_in['sq_w'], 'L1_attn_sq_b': _L1_attn_in['sq_b'], 'L1_attn_srw_w': _L1_attn_in['srw_w'], 'L1_attn_srw_b': _L1_attn_in['srw_b'], 'L1_attn_res_scale': _L1_attn_in['res_scale'], 'L1_attn_in_proj_w': _L1_attn_in['in_proj_w'], 'L1_attn_conv_w': _L1_attn_in['conv_w'], 'L1_attn_conv_b': _L1_attn_in['conv_b'], 'L1_attn_x_proj_w': _L1_attn_in['x_proj_w'], 'L1_attn_dt_w': _L1_attn_in['dt_w'], 'L1_attn_dt_b': _L1_attn_in['dt_b'], 'L1_attn_A_log': _L1_attn_in['A_log'], 'L1_attn_D': _L1_attn_in['D'], 'L1_attn_out_proj_w': _L1_attn_in['out_proj_w'], 'L1_ffn_router_w': _L1_ffn_in['router_w'], 'L1_ffn_up_w': _L1_ffn_in['up_w'], 'L1_ffn_gate_w': _L1_ffn_in['gate_w'], 'L1_ffn_down_w': _L1_ffn_in['down_w'], 'L1_ffn_shared_up_w': _L1_ffn_in['shared_up_w'], 'L1_ffn_shared_gate_w': _L1_ffn_in['shared_gate_w'], 'L1_ffn_shared_down_w': _L1_ffn_in['shared_down_w']}
    _x0 = _d['L0_attn_x']
    _d['L0_attn_x'] = jax.random.normal(jax.random.fold_in(jax.random.key(seed), 1), (8, 256, 128), dtype=_x0.dtype)
    del _x0
    return _d

def reference(L0_attn_x, L0_attn_Wq, L0_attn_bq, L0_attn_Wk, L0_attn_bk, L0_attn_Wv, L0_attn_bv, L0_attn_Wo, L0_attn_bo, L0_attn_J_attn, L0_attn_lambda_attn, L0_ffn_wg, L0_ffn_shared_w1, L0_ffn_shared_w2, L0_ffn_expert_w1, L0_ffn_expert_w2, L1_attn_ln_g, L1_attn_ln_b, L1_attn_sq_w, L1_attn_sq_b, L1_attn_srw_w, L1_attn_srw_b, L1_attn_res_scale, L1_attn_in_proj_w, L1_attn_conv_w, L1_attn_conv_b, L1_attn_x_proj_w, L1_attn_dt_w, L1_attn_dt_b, L1_attn_A_log, L1_attn_D, L1_attn_out_proj_w, L1_ffn_router_w, L1_ffn_up_w, L1_ffn_gate_w, L1_ffn_down_w, L1_ffn_shared_up_w, L1_ffn_shared_gate_w, L1_ffn_shared_down_w):

    def _L0_attn_ref(x, Wq, bq, Wk, bk, Wv, bv, Wo, bo, J_attn, lambda_attn):
        import jax, jax.numpy as jnp
        import numpy as np
        B, S, E = (2, 256, 128)
        H = 16
        D = E // H
        b, s, _ = x.shape
        scale = jnp.sqrt(jnp.float32(D))

        def split_heads(y):
            return y.reshape(b, s, H, D).transpose(0, 2, 1, 3)
        Q = split_heads(x @ Wq.T + bq)
        K = split_heads(x @ Wk.T + bk)
        V = split_heads(x @ Wv.T + bv)
        attn_scores = jnp.einsum('bhid,bhjd->bhij', Q, K) / scale
        Qn = jnp.tanh(Q)
        Kn = jnp.tanh(K)
        QJ = jnp.einsum('bhid,hde->bhie', Qn, J_attn)
        delta = jnp.einsum('bhie,bhje->bhij', QJ, Kn)
        attn_scores = attn_scores + lambda_attn * delta
        attn_probs = jax.nn.softmax(attn_scores, axis=-1)
        out = jnp.einsum('bhij,bhjd->bhid', attn_probs, V)
        out = out.transpose(0, 2, 1, 3).reshape(b, s, E)
        return out @ Wo.T + bo

    def _L0_ffn_ref(hidden_states, wg, shared_w1, shared_w2, expert_w1, expert_w2):
        import jax, jax.numpy as jnp
        import numpy as np
        TOPK = 8
        NUM_EXPERTS = 64
        FFN = 384
        CAPACITY = 160

        def _swiglu(x, w1, w2):
            h = x @ w1.T
            x1, x2 = jnp.split(h, 2, axis=-1)
            return x1 * jax.nn.silu(x2) @ w2.T
        B, S, H = hidden_states.shape
        T = B * S
        x = hidden_states.reshape(T, H)
        shared_out = _swiglu(x, shared_w1, shared_w2)
        logits = x.astype(jnp.float32) @ wg.T
        gates = jax.nn.softmax(logits, axis=-1)
        w_topk, idx_topk = jax.lax.top_k(gates, TOPK)
        denom = jnp.maximum(w_topk.sum(-1, keepdims=True), jnp.finfo(jnp.float32).eps)
        w_topk = w_topk / denom
        A = T * TOPK
        flat_e = idx_topk.reshape(A)
        flat_w = w_topk.reshape(A)
        flat_t = jnp.repeat(jnp.arange(T), TOPK)
        order = jnp.argsort(flat_e)
        se, st, sw = (flat_e[order], flat_t[order], flat_w[order])
        counts = jnp.zeros(NUM_EXPERTS, jnp.int32).at[flat_e].add(1)
        starts = jnp.cumsum(counts) - counts
        rank = jnp.arange(A) - starts[se]
        valid = rank < CAPACITY
        buf = jnp.zeros((NUM_EXPERTS, CAPACITY, H), x.dtype).at[se, rank].set(x[st], mode='drop')
        h = jnp.einsum('ech,efh->ecf', buf, expert_w1)
        x1, x2 = jnp.split(h, 2, axis=-1)
        out = jnp.einsum('ecf,ehf->ech', x1 * jax.nn.silu(x2), expert_w2)
        y = out[se, jnp.clip(rank, 0, CAPACITY - 1)]
        y = jnp.where(valid[:, None], y * sw[:, None].astype(y.dtype), 0.0)
        combined = jnp.zeros((T, H), x.dtype).at[st].add(y)
        return (shared_out + combined).reshape(B, S, H)

    def _L1_attn_ref(x, ln_g, ln_b, sq_w, sq_b, srw_w, srw_b, res_scale, in_proj_w, conv_w, conv_b, x_proj_w, dt_w, dt_b, A_log, D, out_proj_w):
        import jax, jax.numpy as jnp
        import numpy as np
        from jax import lax
        D_MODEL = 128
        D_STATE = 16
        D_CONV = 4
        EXPAND = 2
        D_INNER = EXPAND * D_MODEL
        DT_RANK = (D_MODEL + 15) // 16
        B, L = (2, 256)
        EPS = 1e-05

        def _layernorm(x, g, b):
            mu = jnp.mean(x, axis=-1, keepdims=True)
            var = jnp.mean(jnp.square(x - mu), axis=-1, keepdims=True)
            return (x - mu) * lax.rsqrt(var + EPS) * g + b

        def _causal_dwconv(u, w, b):
            din, dc = w.shape
            up = jnp.pad(u, ((0, 0), (dc - 1, 0), (0, 0)))
            k = w.T[:, None, :]
            out = lax.conv_general_dilated(up, k, (1,), 'VALID', dimension_numbers=('NWC', 'WIO', 'NWC'), feature_group_count=din)
            return out + b

        def _mamba(h, in_proj_w, conv_w, conv_b, x_proj_w, dt_w, dt_b, A_log, D, out_proj_w):
            xz = h @ in_proj_w
            u, z = jnp.split(xz, 2, axis=-1)
            u = jax.nn.silu(_causal_dwconv(u, conv_w, conv_b))
            x_dbl = u @ x_proj_w
            dt, Bm, Cm = jnp.split(x_dbl, [DT_RANK, DT_RANK + D_STATE], axis=-1)
            delta = jax.nn.softplus(dt @ dt_w + dt_b)
            A = -jnp.exp(A_log)
            dA = jnp.exp(jnp.einsum('bld,dn->bldn', delta, A))
            dBu = jnp.einsum('bld,bln,bld->bldn', delta, Bm, u)

            def step(hst, inp):
                dA_t, dBu_t, C_t = inp
                hst = dA_t * hst + dBu_t
                y = jnp.einsum('bdn,bn->bd', hst, C_t)
                return (hst, y)
            h0 = jnp.zeros((u.shape[0], D_INNER, D_STATE), u.dtype)
            _, ys = lax.scan(step, h0, (dA.transpose(1, 0, 2, 3), dBu.transpose(1, 0, 2, 3), Cm.transpose(1, 0, 2)))
            y = ys.transpose(1, 0, 2) + u * D
            y = y * jax.nn.silu(z)
            return y @ out_proj_w
        residual = x
        h = _layernorm(x, ln_g, ln_b)
        h = h + (h @ sq_w + sq_b)
        y = _mamba(h, in_proj_w, conv_w, conv_b, x_proj_w, dt_w, dt_b, A_log, D, out_proj_w)
        y = y * (y @ srw_w + srw_b)
        return residual + res_scale * y

    def _L1_ffn_ref(x, router_w, up_w, gate_w, down_w, shared_up_w, shared_gate_w, shared_down_w):
        import jax, jax.numpy as jnp
        import numpy as np
        ALPHA = 2.0
        TOP_K = 2
        logits = jnp.einsum('bsd,de->bse', x, router_w)
        probs = jax.nn.softmax(logits, axis=-1)
        topk_vals, topk_idx = jax.lax.top_k(probs, TOP_K)
        top1_val = topk_vals[..., 0]
        top1_idx = topk_idx[..., 0]
        hid = jnp.einsum('bsd,edh->ebsh', x, up_w) * jax.nn.silu(jnp.einsum('bsd,edh->ebsh', x, gate_w))
        Er = up_w.shape[0]
        mask = (top1_idx[None, :, :] == jnp.arange(Er)[:, None, None]).astype(x.dtype)
        routed = jnp.einsum('ebsh,ehd,ebs->bsd', hid, down_w, mask)
        shid = jnp.einsum('bsd,dh->bsh', x, shared_up_w) * jax.nn.silu(jnp.einsum('bsd,dh->bsh', x, shared_gate_w))
        shared = jnp.einsum('bsh,hd->bsd', shid, shared_down_w)
        return ALPHA * top1_val[..., None] * routed + shared
    x = L0_attn_x
    x = x + _layernorm(_L0_attn_ref(_layernorm(x, axis=-1), L0_attn_Wq, L0_attn_bq, L0_attn_Wk, L0_attn_bk, L0_attn_Wv, L0_attn_bv, L0_attn_Wo, L0_attn_bo, L0_attn_J_attn, L0_attn_lambda_attn), axis=-1)
    x = x + _layernorm(_L0_ffn_ref(_layernorm(x, axis=-1), L0_ffn_wg, L0_ffn_shared_w1, L0_ffn_shared_w2, L0_ffn_expert_w1, L0_ffn_expert_w2), axis=-1)
    x = x + _layernorm(_L1_attn_ref(_layernorm(x, axis=-1), L1_attn_ln_g, L1_attn_ln_b, L1_attn_sq_w, L1_attn_sq_b, L1_attn_srw_w, L1_attn_srw_b, L1_attn_res_scale, L1_attn_in_proj_w, L1_attn_conv_w, L1_attn_conv_b, L1_attn_x_proj_w, L1_attn_dt_w, L1_attn_dt_b, L1_attn_A_log, L1_attn_D, L1_attn_out_proj_w), axis=-1)
    x = x + _layernorm(_L1_ffn_ref(_layernorm(x, axis=-1), L1_ffn_router_w, L1_ffn_up_w, L1_ffn_gate_w, L1_ffn_down_w, L1_ffn_shared_up_w, L1_ffn_shared_gate_w, L1_ffn_shared_down_w), axis=-1)
    return x

_drawn_inputs = setup_inputs


def setup_inputs(seed=0):
    import zlib

    import numpy as np

    out = dict(_drawn_inputs(seed))
    spreads = {'L0_attn_bq': (0.0, 0.1),
     'L0_attn_bk': (0.0, 0.8),
     'L0_attn_bv': (0.0, 0.1),
     'L0_attn_bo': (0.0, 0.1),
     'L1_attn_ln_g': (1.0, 0.6),
     'L1_attn_ln_b': (0.0, 0.8),
     'L1_attn_sq_b': (0.0, 0.8),
     'L1_attn_srw_b': (0.0, 0.8),
     'L1_attn_conv_b': (0.0, 0.8),
     'L1_attn_dt_b': (-4.599999904632568, 0.6),
     'L1_attn_D': (1.0, 0.6)}
    factors = {'L0_attn_J_attn': 3.247,
     'L1_attn_sq_w': 8.0,
     'L1_attn_srw_w': 8.0,
     'L1_attn_in_proj_w': 8.0,
     'L1_attn_conv_w': 8.0,
     'L1_attn_x_proj_w': 8.0,
     'L1_attn_dt_w': 8.0,
     'L1_attn_A_log': 8.0,
     'L1_attn_out_proj_w': 8.0}
    for name, (base, spread) in spreads.items():
        noise = np.random.default_rng([zlib.crc32(name.encode()), seed]).standard_normal(out[name].shape)
        drawn = base * np.exp(spread * noise) if base else spread * noise
        out[name] = jnp.asarray(drawn.astype(out[name].dtype))
    for name, factor in factors.items():
        out[name] = (out[name] * factor).astype(out[name].dtype)
    return out
```

```python
from contextlib import ExitStack, contextmanager

import concourse.bass as bass
from concourse import mybir

F32 = mybir.dt.float32
BF16 = mybir.dt.bfloat16
I32 = mybir.dt.int32
ALU = mybir.AluOpType
ACT = mybir.ActivationFunctionType
AX = mybir.AxisListType

P = 128
NB, S, E = 8, 256, 128
TOK = NB * S
NT = TOK // P
TPB = S // P
CH = 512
NCH = TOK // CH
TPC = CH // P
EPS = 1e-5


@contextmanager
def semaphores(nc, prefix):
    taken = []

    def sem(name):
        taken.append(nc.alloc_semaphore(prefix + name))
        return taken[-1]

    yield sem
    nc.clear_and_free_semaphores(taken)
    nc.all_engine_barrier()


class Steps:

    def __init__(self, eng, sem, passes=None):
        self.eng, self.sem, self.n, self.passes = eng, sem, 0, passes

    def __call__(self, ins):
        ins.then_inc(self.sem, 1)
        self.n = self.n + 1
        return ins

    def wait(self):
        self.eng.wait_ge(self.sem, self.n)
        if self.passes is not None and not isinstance(self.n, int):
            self.eng.sem_inc(self.passes, 1)

    def then(self, ins):
        self(ins)
        self.wait()


def per_row(ap, n):
    return ap.unsqueeze(2).to_broadcast([ap.shape[0], ap.shape[1], n])


def layernorm_rows(dve, step, src, dst, xc, stat, rows_centered, var_ready, rstd_ready, n):
    v = dve
    step.wait()
    step.then(v.tensor_reduce(stat[:, 0, 0:n], src, AX.X, ALU.add))
    step.then(v.tensor_scalar(stat[:, 1, 0:n], stat[:, 0, 0:n], 1.0 / E, None, ALU.mult))
    step.then(v.tensor_tensor(xc, src, per_row(stat[:, 1, 0:n], E), ALU.subtract))
    step.then(v.tensor_tensor(dst, xc, xc, ALU.mult))
    v.tensor_reduce(stat[:, 2, 0:n], dst, AX.X, ALU.add).then_inc(var_ready, 1)
    v.wait_ge(rstd_ready[0], rstd_ready[1])
    step.then(v.tensor_tensor(dst, xc, per_row(stat[:, 3, 0:n], E), ALU.mult))


def pool_rstd(pool, step, stat, n, var_ready, count, rstd_ready, half):
    pool.wait_ge(var_ready, count)
    step.then(pool.tensor_scalar(stat[:, 4, 0:n], stat[:, 2, 0:n], 1.0 / E, EPS, ALU.mult, ALU.add))
    pool.tensor_tensor(stat[:, 3, 0:n], stat[:, 4, 0:n], half[:, 0:n], ALU.pow).then_inc(rstd_ready, 1)


H, D = 16, 8
PARTS = 3
BLOCKS = 6
FEAT = 2 * D
KROWS = BLOCKS * FEAT
KALL = KROWS + PARTS
RING = 8
AHEAD = (1, 1, 1, 1, 2, 1, 1, 1, 2, 1, 1, 1, 2, 0, 0, 0)


def attention(nc, io, X, ident):
    with ExitStack() as ctx:
        def sb(name, shape, dt=F32):
            return ctx.enter_context(nc.sbuf_tensor(name, shape, dt))

        def psum(name, shape, dt=F32):
            return ctx.enter_context(nc.psum_tensor(name, shape, dt))

        sem = ctx.enter_context(semaphores(nc, "a_"))

        w = sb("a_w", [P, 5, E])
        vec = sb("a_vec", [P, 4])
        rowb = sb("a_rowb", [P, 2, E])
        half = sb("a_half", [P, NT])
        stat = sb("a_stat", [P, 5, NT])
        Hn = sb("a_hn", [P, NT, E])
        Y = sb("a_y", [P, NT, E])
        hT = sb("a_hT", [P, TOK])
        TQ = sb("a_tq", [P, TOK])
        S4 = sb("a_s4", [P, 4, TOK])
        V = sb("a_v", [P, NT, H, D + 1])
        part = sb("a_part", [P, 2, PARTS, 4, S], BF16)
        rest = sb("a_rest", [P, 2, 4, S])
        QS = [sb(f"a_qs{i}", [KALL, H, S], BF16) for i in range(2)]
        KS = [sb(f"a_ks{i}", [KALL, H, S], BF16) for i in range(2)]
        mx = sb("a_mx", [P, TPB, H])
        mr = sb("a_mr", [2 * H, 2, P])
        mp = [sb(f"a_mp{i}", [2 * H, PARTS, P], BF16) for i in range(2)]
        PT = sb("a_pt", [P, RING, TPB, S])
        Vb = sb("a_vb", [P, 2, TPB, H, 32])
        OU = sb("a_ou", [P, 2, 2, S])
        rden = sb("a_rden", [P, 2, 2, TPB, 4])
        O = sb("a_o", [P, TPB, E])
        OT = sb("a_ot", [P, S])

        ps1 = [psum(f"a_s1_{i}", [P, TPB, S]) for i in range(2)]
        ps2 = [psum(f"a_s2_{i}", [P, TPB, S]) for i in range(2)]
        pso = [psum(f"a_po{i}", [P, 2, S]) for i in range(2)]
        pst = psum("a_pt_", [P, 2, TPB, P])
        psm = psum("a_pm", [P, CH])

        def flat(bank):
            return bank[:].rearrange("p a b -> p (a b)")

        wide = [flat(x) for x in (ps1[0], ps1[1], ps2[0], ps2[1])]
        qbank, kbank = [flat(x) for x in ps2], [flat(x) for x in pso]

        bounce = nc.dram_tensor("a_bounce", (2, PARTS * 4, P, S), BF16, kind="Internal").ap()
        bounced_rows = bounce.rearrange("s (c a) (d h) t -> s c (a d) (h t)", a=4, h=H)

        loaded, bounced = sem("loaded"), sem("bounced")
        var_ready, rstd_ready = sem("var_ready"), sem("rstd_ready")
        normed, hT_psum, hT_ready = sem("normed"), sem("hT_psum"), sem("hT_ready")
        qk_psum, qk_ready = sem("qk_psum"), sem("qk_ready")
        qj_psum, qj_ready = sem("qj_psum"), sem("qj_ready")
        v_psum, v_ready, v_ones = sem("v_psum"), sem("v_ready"), sem("v_ones")
        k_ones = sem("k_ones")
        split_ready, stack_ready = sem("split_ready"), [sem("stack0"), sem("stack1")]
        vb_ready = sem("vb_ready")
        rows_psum, rows_maxed = sem("rows_psum"), sem("rows_maxed")
        maxT_psum, maxT_ready, max_rows = sem("maxT_psum"), sem("maxT_ready"), [sem("maxr0"), sem("maxr1")]
        cols_psum, exp_ready, pv_done = sem("cols_psum"), sem("exp_ready"), sem("pv_done")
        ou_ready, ot_psum = sem("ou_ready"), sem("ot_psum")
        o_ready, oT_psum, oT_ready, y_psum, y_ready = (
            sem("o_ready"), sem("oT_psum"), sem("oT_ready"), sem("y_psum"), sem("y_ready"))
        den_ready = sem("den_ready")
        dve_step, act_step, pool_step = sem("dve_step"), sem("act_step"), sem("pool_step")
        pool_passes, sp_passes = sem("pool_passes"), sem("sp_passes")

        block = ctx.enter_context(nc.Block())

        @block.sync
        def _(sp):
            sp.dma_start(X[:], io["x"].rearrange("b (t p) e -> p (b t) e", p=P)).then_inc(loaded, 16)
            for n, name in enumerate(("WqT", "WkT", "WvT", "WoT", "Jd")):
                sp.dma_start(w[:, n, :], io[name]).then_inc(loaded, 16)
            for n, name in enumerate(("bq", "bk")):
                sp.dma_start(vec[:, n:n + 1], io[name].unsqueeze(1)).then_inc(loaded, 16)
            sp.dma_start(vec[:, 2:3], io["lam"].unsqueeze(1).to_broadcast([P, 1])).then_inc(loaded, 16)
            for n, name in enumerate(("bv", "bo")):
                sp.dma_start(rowb[:, n, :], io[name].unsqueeze(0).to_broadcast([P, E])).then_inc(loaded, 16)
            sp.dma_start(ident[:], io["ident"]).then_inc(loaded, 16)

            def bounce_out(b, s):
                sp.wait_ge(split_ready, b + 1)
                sp.dma_start(bounce[s].rearrange("c f t -> f c t"),
                             part[:, s].rearrange("p c a t -> p (c a) t")).then_inc(bounced, 16)

            def stack(b, s, first=False):
                if not first:
                    sp.wait_ge(cols_psum, (b - 1) * H)
                    sp.sem_inc(sp_passes, 1)
                sp.wait_ge(bounced, 16 * (b + 1))
                for row, n, qp, kp in ((0, 3, 0, 0), (3, 2, 1, 0), (5, 1, 2, 0)):
                    rows = slice(row * FEAT, (row + n) * FEAT)
                    q = bounced_rows[s, qp:qp + 1, 0:FEAT].to_broadcast([n, FEAT, H * S])
                    sp.dma_start(QS[s][rows].rearrange("r h t -> r (h t)"), q).then_inc(stack_ready[s], 16)
                    sp.dma_start(KS[s][rows].rearrange("r h t -> r (h t)"), bounced_rows[s, kp:kp + n, FEAT:2 * FEAT]
                                 ).then_inc(stack_ready[s], 16)

            def max_row(b, s):
                sp.wait_ge(maxT_ready, b + 1)
                for it in range(TPB):
                    for c in range(PARTS):
                        sp.dma_start(QS[s][KROWS + c:KROWS + c + 1, :, it * P:(it + 1) * P],
                                     mp[s][it * H:(it + 1) * H, c, :]
                                     ).then_inc(max_rows[s], 16)

            for b in range(2):
                bounce_out(b, b)
                stack(b, b, first=True)
            max_row(0, 0)

            def step(b, s):
                bounce_out(b + 2, s)
                max_row(b + 1, 1 - s)
                stack(b + 2, s)

            with sp.Fori(0, NB // 2 - 1) as i:
                for s in range(2):
                    step(2 * i + s, s)
            max_row(NB - 1, 1)

        @block.gpsimd
        def _(pool):
            step = Steps(pool, pool_step, passes=pool_passes)
            step.then(pool.memset(half[:], -0.5))
            pool.memset(V[:, :, :, D:D + 1], 1.0).then_inc(v_ones, 1)
            pool.wait_ge(v_ones, 1)
            for s in range(2):
                pool.memset(KS[s][KROWS:KALL], 1.0).then_inc(k_ones, 1)
                pool.wait_ge(k_ones, s + 1)
            pool_rstd(pool, step, stat, NT, var_ready, 1, rstd_ready, half)
            step.then(pool.memset(Vb[:], 0.0))
            pool.wait_ge(qj_ready, NCH)
            pool.wait_ge(v_ready, NCH)

            def split(b, s):
                src = S4[:, :, bass.ds(b * S, S)]
                step.then(pool.tensor_copy(part[:, s, 0], src))
                step.then(pool.tensor_tensor(rest[:, s], src, part[:, s, 0], ALU.subtract))
                step.then(pool.tensor_copy(part[:, s, 1], rest[:, s]))
                pool.tensor_tensor(part[:, s, 2], rest[:, s], part[:, s, 1], ALU.subtract).then_inc(split_ready, 1)

            def v_of(b, s):
                pool.tensor_copy(Vb[:, s, :, :, 0:D + 1], V[:, bass.ds(b * TPB, TPB)]).then_inc(vb_ready, 1)

            for b in range(2):
                split(b, b)
                v_of(b, b)
            first = step.n
            with pool.Fori(0, NB // 2 - 1) as i:
                for s in range(2):
                    step.n = first + i * 6 + 3 * s
                    pool.wait_ge(bounced, 16 * (2 * i + s + 1))
                    split(2 * i + s + 2, s)
                    pool.wait_ge(pv_done, 4 * (2 * i + s + 1))
                    v_of(2 * i + s + 2, s)
            step.n = first + (NB // 2 - 1) * 6
            pool_rstd(pool, step, stat, NT, var_ready, 2, rstd_ready, half)

        @block.scalar
        def _(act):
            for c in range(NCH):
                act.wait_ge(hT_psum, c + 1)
                act.activation(hT[:, c * CH:(c + 1) * CH], wide[c], ACT.Copy).then_inc(hT_ready, 1)
            act.wait_ge(loaded, 16 * 12)
            step = Steps(act, act_step)
            for c in range(NCH):
                at = slice(c * CH, (c + 1) * CH)
                for n in range(2):
                    act.wait_ge(qk_psum, 2 * c + n + 1)
                    src = (qbank, kbank)[n][c % 2]
                    if n == 0:
                        step.then(act.activation(S4[:, 0, at], src, ACT.Identity, bias=vec[:, 0:1]))
                        act.activation(TQ[:, at], S4[:, 0, at], ACT.Tanh).then_inc(qk_ready, 1)
                        act.wait_ge(qk_ready, 2 * c + 1)
                        step(act.activation(S4[:, 0, at], S4[:, 0, at], ACT.Copy, scale=float(D) ** -0.5))
                    else:
                        step(act.activation(S4[:, 2, at], src, ACT.Identity, bias=vec[:, 1:2]))
                        act.activation(S4[:, 3, at], src, ACT.Tanh, bias=vec[:, 1:2]).then_inc(qk_ready, 1)
                act.wait_ge(qj_psum, c + 1)
                act.activation(S4[:, 1, at], psm[:], ACT.Copy, scale=vec[:, 2:3]).then_inc(qj_ready, 1)

            def evacuate(b, q):
                act.wait_ge(pv_done, 4 * b + 2 * q + 2)
                act.activation(OU[:, q], pso[q][:], ACT.Copy).then_inc(ou_ready, 1)

            def one(b, first=False):
                for h in range(H):
                    act.wait_ge(cols_psum, b * H + h + 1)
                    if not (first and h < RING):
                        act.wait_ge(pv_done, 4 * b + (h - RING) // 4 + 1)
                    act.activation(PT[:, h % RING], ps2[h % 2][:], ACT.Exp).then_inc(exp_ready, 1)
                    if h == 0 and not first:
                        evacuate(b - 1, 1)
                    if h == 11:
                        evacuate(b, 0)

            step.wait()
            one(0, first=True)
            with act.Fori(1, NB) as b:
                one(b)
            evacuate(NB - 1, 1)

        @block.vector
        def _(dve):
            step = Steps(dve, dve_step)
            dve.wait_ge(loaded, 16 * 12)
            xc = Y[:]
            layernorm_rows(dve, step, X[:], Hn[:], xc, stat, None, var_ready, (rstd_ready, 1), NT)
            dve.nop().then_inc(normed, 1)
            dve.wait_ge(v_ones, 1)
            for c in range(NCH):
                dve.wait_ge(v_psum, c + 1)
                dve.tensor_tensor(V[:, c * TPC:(c + 1) * TPC, :, 0:D],
                                  ps1[c % 2][:].rearrange("p a (t h d) -> p (a t) h d", h=H, d=D),
                                  rowb[:, 0, :].rearrange("p (h d) -> p h d", d=D).unsqueeze(1)
                                  .to_broadcast([P, TPC, H, D]), ALU.add).then_inc(v_ready, 1)

            def maxima(b, h):
                dve.wait_ge(rows_psum, b * H + h + 1)
                dve.tensor_reduce(mx[:, :, h], ps1[h % 2][:], AX.X, ALU.max, negate=True).then_inc(rows_maxed, 1)

            def split_max(b, s):
                dve.wait_ge(maxT_psum, b + 1)
                src = psm[0:2 * H, 0:P]
                step.then(dve.tensor_copy(mp[s][:, 0], src))
                step.then(dve.tensor_tensor(mr[:, 0], src, mp[s][:, 0], ALU.subtract))
                step.then(dve.tensor_copy(mp[s][:, 1], mr[:, 0]))
                dve.tensor_tensor(mp[s][:, 2], mr[:, 0], mp[s][:, 1], ALU.subtract).then_inc(maxT_ready, 1)

            def normalise(b, q):
                dve.wait_ge(ot_psum, 2 * b + q + 1)
                src = pst[:].rearrange("p g t (h c) -> p g t h c", c=32)
                dve.reciprocal(rden[:, q], src[:, :, :, :, D]).then_inc(den_ready, 1)
                dve.wait_ge(den_ready, 2 * b + q + 1)
                for g in range(2):
                    m = dve.tensor_tensor(
                        O[:].rearrange("p t (g h d) -> p g t h d", g=4, d=D)[:, 2 * q + g],
                        src[:, g, :, :, 0:D], rden[:, q, g].unsqueeze(3).to_broadcast([P, TPB, 4, D]), ALU.mult)
                m.then_inc(o_ready, 1)

            def transposed(b):
                dve.wait_ge(oT_psum, b + 1)
                dve.tensor_copy(OT[:], psm[:, 0:S]).then_inc(oT_ready, 1)

            def project(b):
                dve.wait_ge(y_psum, b + 1)
                dve.tensor_tensor(Y[:, bass.ds(b * TPB, TPB)],
                                  psm[:, S:2 * S].rearrange("p (t e) -> p t e", e=E),
                                  rowb[:, 1:2, :].to_broadcast([P, TPB, E]), ALU.add).then_inc(y_ready, 1)

            for h in range(H):
                maxima(0, h)
            split_max(0, 0)
            first = step.n

            def one(b, s, previous=True, ahead=True):
                step.n = first + b * 3
                head = 0
                for h in range(H):
                    for _ in range(AHEAD[h] if ahead else 0):
                        maxima(b + 1, head)
                        head += 1
                    if previous and h == 1:
                        normalise(b - 1, 1)
                    if previous and h == 5:
                        transposed(b - 1)
                    if previous and h == 8:
                        project(b - 1)
                    if h == 13:
                        normalise(b, 0)
                    if h == 14 and ahead:
                        split_max(b + 1, 1 - s)

            one(0, 0, previous=False)
            one(1, 1)
            with dve.Fori(1, NB // 2 - 1) as i:
                for s in range(2):
                    one(2 * i + s, s)
            one(NB - 2, 0)
            one(NB - 1, 1, ahead=False)
            normalise(NB - 1, 1)
            transposed(NB - 1)
            project(NB - 1)
            step.n = first + (NB - 1) * 3
            dve.wait_ge(y_ready, NB)
            layernorm_rows(dve, step, Y[:], Hn[:], Y[:], stat, None, var_ready, (rstd_ready, 2), NT)
            step.then(dve.tensor_tensor(X[:], X[:], Hn[:], ALU.add))

        @block.tensor
        def _(pe):
            pe.wait_ge(loaded, 16 * 12)
            pe.wait_ge(normed, 1)
            for c in range(NCH):
                for j in range(TPC):
                    t = pe.transpose(wide[c][:, j * P:(j + 1) * P], Hn[:, c * TPC + j, :], ident[:])
                t.then_inc(hT_psum, 1)
            for c in range(NCH):
                at = slice(c * CH, (c + 1) * CH)
                pe.wait_ge(hT_ready, NCH if c == 0 else c + 1)
                if c >= 2:
                    pe.wait_ge(qk_ready, 2 * (c - 1))
                for n in range(2):
                    pe.matmul((qbank, kbank)[n][c % 2], w[:, n, :], hT[:, at],
                              start=True, stop=True).then_inc(qk_psum, 1)
                if c >= 2:
                    pe.wait_ge(v_ready, c - 1)
                for j in range(TPC):
                    v = pe.matmul(ps1[c % 2][:].rearrange("p a b -> p (a b)")[:, j * P:(j + 1) * P],
                                  hT[:, (c * TPC + j) * P:(c * TPC + j + 1) * P], w[:, 2, :], start=True, stop=True)
                v.then_inc(v_psum, 1)
                pe.wait_ge(qk_ready, 2 * c + 1)
                if c >= 1:
                    pe.wait_ge(qj_ready, c)
                pe.matmul(psm[:], w[:, 4, :], TQ[:, at], start=True, stop=True).then_inc(qj_psum, 1)

            def by_rows(b, s, h):
                if not (isinstance(b, int) and b == 0 and h < 2):
                    pe.wait_ge(rows_maxed, b * H + h - 1)
                for it in range(TPB):
                    m = pe.matmul(ps1[h % 2][:, it], QS[s][0:KROWS, h, it * P:(it + 1) * P],
                                  KS[s][0:KROWS, h, :], start=True, stop=True)
                m.then_inc(rows_psum, 1)

            def by_columns(b, s, h, first=False):
                if not (first and h < 2):
                    pe.wait_ge(exp_ready, b * H + h - 1)
                for jt in range(TPB):
                    m = pe.matmul(ps2[h % 2][:, jt], KS[s][:, h, jt * P:(jt + 1) * P], QS[s][:, h, :],
                                  start=True, stop=True)
                m.then_inc(cols_psum, 1)

            def pv(b, s, g, first=False):
                pe.wait_ge(exp_ready, b * H + 4 * g + 4)
                if g % 2 == 0 and not first:
                    pe.wait_ge(ou_ready, 2 * b + g // 2 - 1)
                for jt in range(TPB):
                    for k in range(4):
                        m = pe.matmul(pso[g // 2][32 * k:32 * k + 32, g % 2, :], Vb[:, s, jt, 4 * g + k, :],
                                      PT[:, (4 * g + k) % RING, jt, :], start=(jt == 0), stop=(jt == TPB - 1))
                m.then_inc(pv_done, 1)

            def max_transposed():
                pe.transpose(psm[0:2 * H, 0:P], mx[:].rearrange("p t h -> p (t h)"), ident[:]).then_inc(maxT_psum, 1)

            def to_rows(b, q, first=False):
                pe.wait_ge(ou_ready, 2 * b + q + 1)
                if not first:
                    pe.wait_ge(o_ready, 2 * b + q)
                for g in range(2):
                    for it in range(TPB):
                        m = pe.transpose(pst[:, g, it, :], OU[:, q, g, it * P:(it + 1) * P], ident[:])
                m.then_inc(ot_psum, 1)

            def o_transposed(b):
                pe.wait_ge(o_ready, 2 * b + 2)
                for it in range(TPB):
                    m = pe.transpose(psm[:, it * P:(it + 1) * P], O[:, it, :], ident[:])
                m.then_inc(oT_psum, 1)

            def project(b):
                pe.wait_ge(oT_ready, b + 1)
                for it in range(TPB):
                    m = pe.matmul(psm[:, S + it * P:S + (it + 1) * P], OT[:, it * P:(it + 1) * P], w[:, 3, :],
                                  start=True, stop=True)
                m.then_inc(y_psum, 1)

            pe.wait_ge(v_ready, NCH)
            pe.wait_ge(qj_ready, NCH)
            pe.wait_ge(qk_ready, 2 * NCH)
            pe.wait_ge(stack_ready[0], 16 * 6)
            for h in range(H):
                by_rows(0, 0, h)
            pe.wait_ge(rows_maxed, H)
            max_transposed()

            def one(b, s, k, previous=True, ahead=True):
                first = not previous
                pe.wait_ge(k_ones, 2)
                pe.wait_ge(max_rows[s], 16 * PARTS * TPB * (k + 1))
                pe.wait_ge(vb_ready, b + 1)
                if ahead:
                    pe.wait_ge(maxT_ready, b + 1)
                head = 0
                for h in range(H):
                    by_columns(b, s, h, first)
                    if ahead and AHEAD[h] and head == 0:
                        pe.wait_ge(stack_ready[1 - s], 16 * 6 * (k + 1 + s))
                    for _ in range(AHEAD[h] if ahead else 0):
                        by_rows(b + 1, 1 - s, head)
                        head += 1
                    if previous and h == 1:
                        to_rows(b - 1, 1)
                    if previous and h == 5:
                        o_transposed(b - 1)
                    if previous and h == 8:
                        project(b - 1)
                    if h in (5, 9, 13):
                        pv(b, s, (h - 5) // 4, first)
                    if h == 13:
                        to_rows(b, 0, first)
                    if h == 14 and ahead:
                        pe.wait_ge(rows_maxed, (b + 2) * H)
                        if previous:
                            pe.wait_ge(y_ready, b)
                        max_transposed()
                pv(b, s, 3, first)

            one(0, 0, 0, previous=False)
            one(1, 1, 0)
            with pe.Fori(1, NB // 2 - 1) as i:
                for s in range(2):
                    one(2 * i + s, s, i)
            one(NB - 2, 0, NB // 2 - 1)
            one(NB - 1, 1, NB // 2 - 1, ahead=False)
            to_rows(NB - 1, 1)
            o_transposed(NB - 1)
            project(NB - 1)


NE, TOPK, CAP, FF = 64, 8, 160, 384
FT = FF // P
GE = 4
NG = NE // GE
GC = GE * CAP // P
GR = GE * CAP
NSLOT = NE * CAP
ROWW = E + NE
NZ = TOK * TOPK
ROUNDS = CAP // 8
FEPS = 1.1920928955078125e-07


def route(nc, io, X, ident, rows, slots, tab, ST):
    with ExitStack() as ctx:
        def sb(name, shape, dt=F32):
            return ctx.enter_context(nc.sbuf_tensor("r_" + name, shape, dt))

        def psum(name, shape, dt=F32):
            return ctx.enter_context(nc.psum_tensor("r_" + name, shape, dt))

        sem = ctx.enter_context(semaphores(nc, "r_"))

        half, stat = sb("half", [P, NT]), sb("stat", [P, 5, NT])
        Hn, xc = sb("hn", [P, NT, E]), sb("xc", [P, NT, E])
        hT = sb("hT", [P, TOK])
        wg = sb("wg", [P, NE])
        w1, w2 = sb("w1", [P, 2 * FF]), sb("w2", [P, FT, E])
        G, R, M, C = (sb(n, [P, NT, NE]) for n in ("g", "r", "m", "c"))
        Wt = sb("wt", [P, NT, NE])
        top = sb("top", [P, NT, TOPK])
        small = sb("small", [P, 4, NT])
        basei, base = sb("basei", [P, NT], I32), sb("base", [P, NT])
        key = sb("key", [P, NT // 2, 2, NE])
        keyT = sb("keyT", [P, TOK // 2])
        m8 = sb("m8", [P, 8])
        lists = sb("lists", [P, CAP])
        both, final = sb("both", [NE, 2 * CAP]), sb("final", [NE, CAP])
        flat_slots = sb("flat", [NSLOT // P, P])
        dest = sb("dest", [P, NG, GC])
        sg = sb("sg", [P, FT, CH])
        act_in = sb("act_in", [P, 2, FT, CH])

        pl = psum("pl", [P, NT, NE])
        pt = [psum(f"pt{i}", [P, CH]) for i in range(2)]
        pu = [psum(f"pu{i}", [P, CH]) for i in range(3)]
        pd = psum("pd", [P, CH])

        loaded = sem("loaded")
        var_ready, rstd_ready, normed = sem("var_ready"), sem("rstd_ready"), sem("normed")
        hT_psum, hT_ready = sem("hT_psum"), sem("hT_ready")
        logits_psum, centred, exp_ready = sem("logits_psum"), sem("centred"), sem("exp_ready")
        base_ready = sem("base_ready")
        key_ready, keyT_psum = sem("key_ready"), sem("keyT_psum")
        half_lists, both_ready = sem("half_lists"), sem("both_ready")
        final_ready, slots_out, slots_in, slots_psum = (
            sem("final_ready"), sem("slots_out"), sem("slots_in"), sem("slots_psum"))
        weights_ready, rows_out = sem("weights_ready"), sem("rows_out")
        up_psum, up_read, gated, down_psum, down_read = (
            sem("up_psum"), sem("up_read"), sem("gated"), sem("down_psum"), sem("down_read"))
        dve_step, pool_step = sem("dve_step"), sem("pool_step")

        block = ctx.enter_context(nc.Block())

        @block.sync
        def _(sp):
            for dst, src in ((wg, "wgT"), (w1, "sw1T")):
                sp.dma_start(dst[:], io[src]).then_inc(loaded, 16)
            sp.dma_start(w2[:], io["sw2T"]).then_inc(loaded, 16)
            out = rows.rearrange("(t p) c -> p t c", p=P)
            sp.wait_ge(normed, 1)
            sp.dma_start(out[:, :, 0:E], Hn[:]).then_inc(rows_out, 16)
            sp.wait_ge(weights_ready, 1)
            sp.dma_start(out[:, :, E:ROWW], Wt[:]).then_inc(rows_out, 16)
            sp.wait_ge(half_lists, 1)
            for i in range(2):
                sp.dma_start(both[:, i * CAP:(i + 1) * CAP], lists[i * NE:(i + 1) * NE, :]).then_inc(both_ready, 16)
            sp.wait_ge(final_ready, 1)
            sp.dma_start(slots.rearrange("(e c) -> e c", c=CAP), final[:]).then_inc(slots_out, 16)
            sp.wait_ge(slots_out, 16)
            sp.dma_start(flat_slots[:], slots.rearrange("(n p) -> n p", p=P)).then_inc(slots_in, 16)
            sp.wait_ge(rows_out, 32)
            sp.wait_ge(slots_in, 16)

        @block.gpsimd
        def _(pool):
            step = Steps(pool, pool_step)
            step.then(pool.memset(half[:], -0.5))
            step.then(pool.iota(basei[:], pattern=[[8 - 8 * P, NT]], base=NZ + 1, channel_multiplier=-8))
            pool.tensor_copy(base[:], basei[:]).then_inc(base_ready, 1)
            pool_rstd(pool, step, stat, NT, var_ready, 1, rstd_ready, half)

        @block.scalar
        def _(act):
            for c in range(NCH):
                act.wait_ge(hT_psum, c + 1)
                act.activation(hT[:, c * CH:(c + 1) * CH], pt[c % 2][:], ACT.Copy).then_inc(hT_ready, 1)
            act.wait_ge(centred, 1)
            act.activation(R[:], G[:], ACT.Exp).then_inc(exp_ready, 1)
            for c in range(NCH):
                for j in range(FT):
                    n = c * FT + j
                    act.wait_ge(up_psum, 2 * n + 1)
                    if n:
                        act.wait_ge(gated, n)
                    act.activation(sg[:, 0, :], pu[2 * n % 3][:], ACT.Silu).then_inc(up_read, 1)
                act.wait_ge(down_psum, c + 1)
                act.activation(ST[:, c * CH:(c + 1) * CH], pd[:], ACT.Copy).then_inc(down_read, 1)

        @block.vector
        def _(dve):
            v = dve
            step = Steps(dve, dve_step)
            layernorm_rows(dve, step, X[:], Hn[:], xc[:], stat, None, var_ready, (rstd_ready, 1), NT)
            dve.nop().then_inc(normed, 1)
            dve.wait_ge(logits_psum, 1)
            step.then(v.tensor_reduce(small[:, 0], pl[:], AX.X, ALU.max))
            v.tensor_tensor(G[:], pl[:], per_row(small[:, 0], NE), ALU.subtract).then_inc(centred, 1)
            dve.wait_ge(exp_ready, 1)
            step.then(v.tensor_reduce(small[:, 1], R[:], AX.X, ALU.add))
            step.then(v.reciprocal(small[:, 2], small[:, 1]))
            step.then(v.tensor_tensor(G[:], R[:], per_row(small[:, 2], NE), ALU.mult))
            for t in range(NT):
                step(v.max(top[:, t, :], G[:, t, :]))
            step.wait()
            for t in range(NT):
                step(v.match_replace(R[:, t, :], top[:, t, :], G[:, t, :], -1.0))
            step(v.tensor_reduce(small[:, 0], top[:], AX.X, ALU.add))
            step.wait()
            step(v.tensor_scalar(M[:], R[:], 0.0, None, ALU.is_lt))
            step.then(v.tensor_scalar(small[:, 1], small[:, 0], FEPS, None, ALU.max))
            step(v.reciprocal(small[:, 2], small[:, 1]))
            step(v.tensor_tensor(Wt[:], G[:], M[:], ALU.mult))
            step.then(v.memset(R[:], 1.0))
            v.tensor_tensor(Wt[:], Wt[:], per_row(small[:, 2], NE), ALU.mult).then_inc(weights_ready, 1)
            flat = "p t e -> p (t e)"
            step.then(v.tensor_tensor_scan(C[:].rearrange(flat), R[:].rearrange(flat), M[:].rearrange(flat),
                                           0.0, ALU.mult, ALU.add))
            dve.wait_ge(base_ready, 1)
            step.then(v.tensor_tensor(C[:], per_row(base[:], NE), C[:], ALU.subtract))
            v.tensor_tensor(key[:].rearrange("p j h e -> p h j e"), C[:].rearrange("p (h j) e -> p h j e", h=2),
                            M[:].rearrange("p (h j) e -> p h j e", h=2), ALU.mult).then_inc(key_ready, 1)
            dve.wait_ge(keyT_psum, 1)
            step.then(v.tensor_copy(keyT[:], pl[:].rearrange(flat)))

            def largest(src, dst):
                first = step.n
                with dve.Fori(0, ROUNDS) as i:
                    step.n = first + 3 * i
                    step.then(v.max(m8[0:src.shape[0]], src))
                    step(v.tensor_copy(dst[:, bass.ds(8 * i, 8)], m8[0:src.shape[0]]))
                    step.then(v.match_replace(src, m8[0:src.shape[0]], src, 0.0))
                step.n = first + 3 * ROUNDS

            largest(keyT[:], lists)
            dve.nop().then_inc(half_lists, 1)
            for n in range(NCH * FT):
                dve.wait_ge(up_read, n + 1)
                v.tensor_tensor(act_in[:, (n // FT) % 2, n % FT, :], sg[:, 0, :], pu[(2 * n + 1) % 3][:],
                                ALU.mult).then_inc(gated, 1)
            dve.wait_ge(both_ready, 32)
            largest(both[:], final)
            dve.nop().then_inc(final_ready, 1)
            dve.wait_ge(slots_psum, 1)
            keys = pd[:, 0:NG * GC].rearrange("p (g c) -> p g c", c=GC)
            step.then(v.tensor_scalar(dest[:], keys, -1.0, float(NZ), ALU.mult, ALU.add))
            step(v.tensor_copy(tab[:, :, 1, :], dest[:]))
            step.wait()
            step.then(v.tensor_scalar(dest[:], dest[:], float(NZ - 1), None, ALU.min))
            step.then(v.tensor_copy(tab[:, :, 0, :], dest[:]))
            step.then(v.tensor_single_scalar(tab[:, :, 0, :], tab[:, :, 0, :], 3, ALU.logical_shift_right))

        @block.tensor
        def _(pe):
            pe.wait_ge(loaded, 16 * 3)
            pe.wait_ge(normed, 1)
            for c in range(NCH):
                if c >= 2:
                    pe.wait_ge(hT_ready, c - 1)
                for j in range(TPC):
                    t = pe.transpose(pt[c % 2][:, j * P:(j + 1) * P], Hn[:, c * TPC + j, :], ident[:])
                t.then_inc(hT_psum, 1)
            pe.wait_ge(hT_ready, NCH)
            for t in range(NT):
                m = pe.matmul(pl[:, t, :], hT[:, t * P:(t + 1) * P], wg[:], start=True, stop=True)
            m.then_inc(logits_psum, 1)
            pe.wait_ge(key_ready, 1)
            flat = pl[:].rearrange("p t e -> p (t e)")
            for j in range(NT // 2):
                m = pe.transpose(flat[:, j * P:(j + 1) * P], key[:, j].rearrange("p h e -> p (h e)"), ident[:])
            m.then_inc(keyT_psum, 1)
            for c in range(NCH):
                at = slice(c * CH, (c + 1) * CH)
                for j in range(FT):
                    n = c * FT + j
                    if n:
                        pe.wait_ge(gated, n)
                    pe.matmul(pu[2 * n % 3][:], w1[:, FF + j * P:FF + (j + 1) * P], hT[:, at],
                              start=True, stop=True)
                    pe.matmul(pu[(2 * n + 1) % 3][:], w1[:, j * P:(j + 1) * P], hT[:, at],
                              start=True, stop=True).then_inc(up_psum, 2)
                pe.wait_ge(gated, (c + 1) * FT)
                if c:
                    pe.wait_ge(down_read, c)
                for j in range(FT):
                    m = pe.matmul(pd[:], w2[:, j, :], act_in[:, c % 2, j, :], start=(j == 0), stop=(j == FT - 1))
                m.then_inc(down_psum, 1)
            pe.wait_ge(down_read, NCH)
            pe.wait_ge(slots_in, 16)
            pe.transpose(pd[:, 0:NSLOT // P], flat_slots[:], ident[0:NSLOT // P, 0:NSLOT // P]).then_inc(slots_psum, 1)


def experts(nc, io, ident, rows, results, tab):
    with ExitStack() as ctx:
        def sb(name, shape, dt=F32):
            return ctx.enter_context(nc.sbuf_tensor("e_" + name, shape, dt))

        def psum(name, shape, dt=F32):
            return ctx.enter_context(nc.psum_tensor("e_" + name, shape, dt))

        sem = ctx.enter_context(semaphores(nc, "e_"))

        W1 = [sb(f"w1_{i}", [P, GE, 2 * FF]) for i in range(2)]
        W2 = [sb(f"w2_{i}", [P, GE, FT, E]) for i in range(2)]
        idx = [sb(f"idx{i}", [P, 2, GC], I32) for i in range(2)]
        G = [sb(f"g{i}", [P, GC, ROWW]) for i in range(2)]
        GT = [sb(f"gt{i}", [P, GR]) for i in range(2)]
        own = sb("own", [P, GC, GE])
        wsel = sb("wsel", [P, GC, GE])
        wrow = [sb(f"wrow{i}", [P, GC]) for i in range(2)]
        silu = sb("silu", [P, 2, FT, CAP])
        A = sb("a", [P, 2, FT, CAP])
        D_ = sb("d", [P, GR])
        out = [sb(f"out{i}", [P, GC, E]) for i in range(2)]
        zero = sb("zero", [P, 4096])

        px1 = [psum(f"px1_{i}", [P, FT, CAP]) for i in range(2)]
        px2 = [psum(f"px2_{i}", [P, FT, CAP]) for i in range(2)]
        pd = [psum(f"pd{i}", [P, 2, CAP]) for i in range(2)]
        pt = psum("pt", [P, 8, P])

        loaded = [sem("loaded0"), sem("loaded1")]
        own_ready, zero_ready, zeroed = sem("own_ready"), sem("zero_ready"), sem("zeroed")
        idx_ready, gathered, weighed = sem("idx_ready"), [sem("gathered0"), sem("gathered1")], sem("weighed")
        in_psum, in_ready = sem("in_psum"), sem("in_ready")
        up_psum, silu_ready, gated, down_psum, down_ready = (
            sem("up_psum"), sem("silu_ready"), sem("gated"), sem("down_psum"), sem("down_ready"))
        out_psum, out_ready, scattered = sem("out_psum"), sem("out_ready"), [sem("scattered0"), sem("scattered1")]
        dve_step, pool_passes = sem("dve_step"), sem("pool_passes")

        block = ctx.enter_context(nc.Block())

        def groups(eng, one):
            one(0, 0, 0, True, False)
            with eng.Fori(0, NG // 2 - 1) as i:
                one(2 * i + 1, 1, i, False, False)
                one(2 * i + 2, 0, i + 1, False, False)
            one(NG - 1, 1, NG // 2 - 1, False, True)

        @block.sync
        def _(sp):
            sp.dma_start(own[:], io["own"]).then_inc(own_ready, 16)

            def load(g, slot):
                sp.dma_start(W1[slot][:], io["w1T"][bass.ds(g, 1)].rearrange("g h e f -> (g h) e f")
                             ).then_inc(loaded[slot], 16)
                sp.dma_start(W2[slot][:], io["w2T"][bass.ds(g, 1)].rearrange("g p e j h -> (g p) e j h")
                             ).then_inc(loaded[slot], 16)

            load(0, 0)
            load(1, 1)
            sp.wait_ge(zero_ready, 1)
            z = results.rearrange("(n p r) e -> n p (r e)", p=P, n=4)
            for n in range(4):
                sp.dma_start(z[n], zero[:]).then_inc(zeroed, 16)
            with sp.Fori(0, NG // 2 - 1) as i:
                for s in range(2):
                    sp.wait_ge(down_psum, GE * (2 * i + s + 1))
                    load(2 * i + s + 2, s)

        @block.gpsimd
        def _(pool):
            pool.memset(zero[:], 0.0).then_inc(zero_ready, 1)

            def gather(g, slot, first):
                if not first:
                    pool.wait_ge(in_psum, g - 1)
                    pool.wait_ge(weighed, g - 1)
                    pool.wait_ge(scattered[slot], 16 * GC * ((g - 2) // 2 + 1))
                pool.tensor_copy(idx[slot][:], tab[:, bass.ds(g, 1)].rearrange("p g a c -> p (g a) c")
                                 ).then_inc(idx_ready, 1)
                pool.wait_ge(idx_ready, g + 1)
                pool.sem_inc(pool_passes, 1)
                for c in range(GC):
                    pool.indirect_dma_start(G[slot][:, c, :], None, rows,
                                            bass.IndirectOffsetOnAxis(ap=idx[slot][:, 0, c:c + 1], axis=0)
                                            ).then_inc(gathered[slot], 16)

            def scatter(g, slot, first=False):
                pool.wait_ge(out_ready, g + 1)
                pool.sem_inc(pool_passes, 1)
                if first:
                    pool.wait_ge(zeroed, 64)
                for c in range(GC):
                    pool.indirect_dma_start(results, bass.IndirectOffsetOnAxis(ap=idx[slot][:, 1, c:c + 1], axis=0),
                                            out[slot][:, c, :], None, bounds_check=NZ - 1, oob_is_err=False
                                            ).then_inc(scattered[slot], 16)

            gather(0, 0, True)
            gather(1, 1, True)
            scatter(0, 0, True)
            with pool.Fori(0, NG // 2 - 1) as i:
                for s in range(2):
                    gather(2 * i + s + 2, s, False)
                    scatter(2 * i + s + 1, 1 - s)
            scatter(NG - 1, 1)
            for s in range(2):
                pool.wait_ge(scattered[s], 16 * GC * NG // 2)

        @block.scalar
        def _(act):
            def turned(g, slot):
                act.wait_ge(in_psum, g + 1)
                act.activation(GT[slot][:], pt[:, 0:GC].rearrange("p c r -> p (c r)"), ACT.Copy).then_inc(in_ready, 1)

            def silus(g, slot, e, first):
                n = GE * g + e
                act.wait_ge(up_psum, n + 1)
                if not (first and e < 2):
                    act.wait_ge(gated, n - 1)
                act.activation(silu[:, e % 2], px2[e % 2][:], ACT.Silu).then_inc(silu_ready, 1)

            def downs(g, j, first):
                act.wait_ge(down_psum, GE * g + 2 * j + 2)
                if not first:
                    act.wait_ge(out_psum, g)
                act.activation(D_[:, 2 * j * CAP:(2 * j + 2) * CAP], pd[j][:].rearrange("p e c -> p (e c)"),
                               ACT.Copy).then_inc(down_ready, 1)

            turned(0, 0)
            silus(0, 0, 0, True)

            def one(g, slot, pair, first, last):
                for e in range(GE):
                    if e == 2 and not last:
                        turned(g + 1, 1 - slot)
                    if not (last and e == 3):
                        silus(g if e < 3 else g + 1, slot, (e + 1) % GE, first and e < 3)
                    if e == 2:
                        downs(g, 0, first)
                downs(g, 1, first)

            groups(act, one)

        @block.vector
        def _(dve):
            v = dve
            dve.wait_ge(own_ready, 16)

            def gate(g, e, first):
                n = GE * g + e
                dve.wait_ge(silu_ready, n + 1)
                if not (first and e < 2):
                    dve.wait_ge(down_psum, n - 1)
                v.tensor_tensor(A[:, e % 2], px1[e % 2][:], silu[:, e % 2], ALU.mult).then_inc(gated, 1)

            def finish(g, slot, first=False):
                dve.wait_ge(out_psum, g + 1)
                if not first:
                    dve.wait_ge(scattered[slot], 16 * GC * ((g - 2) // 2 + 1))
                v.tensor_tensor(out[slot][:], pt[:, 0:GC], per_row(wrow[slot][:], E), ALU.mult).then_inc(out_ready, 1)

            def weigh(g, slot, pair):
                dve.wait_ge(gathered[slot], 16 * GC * (pair + 1))
                v.tensor_tensor(wsel[:], G[slot][:, :, bass.ds(E + GE * g, GE)], own[:], ALU.mult).then_inc(dve_step, 1)
                dve.wait_ge(dve_step, g + 1)
                v.tensor_reduce(wrow[slot][:], wsel[:], AX.X, ALU.add).then_inc(weighed, 1)

            weigh(0, 0, 0)
            gate(0, 0, True)

            def one(g, slot, pair, first, last):
                for e in range(GE):
                    if not (last and e == 3):
                        gate(g if e < 3 else g + 1, (e + 1) % GE, first and e < 3)
                    if e == 1 and not first:
                        finish(g - 1, 1 - slot, False if not isinstance(g, int) or g > 2 else True)
                    if e == 2 and not last:
                        weigh(g + 1, 1 - slot, pair + slot)

            one(0, 0, 0, True, False)
            one(1, 1, 0, False, False)
            one(2, 0, 1, False, False)
            with dve.Fori(1, NG // 2 - 1) as i:
                one(2 * i + 1, 1, i, False, False)
                one(2 * i + 2, 0, i + 1, False, False)
            one(NG - 1, 1, NG // 2 - 1, False, True)
            finish(NG - 1, 1)

        @block.tensor
        def _(pe):
            def turn(g, slot, pair):
                pe.wait_ge(gathered[slot], 16 * GC * (pair + 1))
                for c in range(GC):
                    m = pe.transpose(pt[:, c, :], G[slot][:, c, 0:E], ident[:])
                m.then_inc(in_psum, 1)

            def up(g, slot, e, pair, first):
                n = GE * g + e
                if e == 0:
                    pe.wait_ge(in_ready, g + 1)
                    pe.wait_ge(loaded[slot], 32 * (pair + 1))
                if not (first and e < 2):
                    pe.wait_ge(gated, n - 1)
                at = slice(e * CAP, (e + 1) * CAP)
                for j in range(FT):
                    pe.matmul(px2[e % 2][:, j, :], W1[slot][:, e, FF + j * P:FF + (j + 1) * P], GT[slot][:, at],
                              start=True, stop=True)
                for j in range(FT):
                    m = pe.matmul(px1[e % 2][:, j, :], W1[slot][:, e, j * P:(j + 1) * P], GT[slot][:, at],
                                  start=True, stop=True)
                m.then_inc(up_psum, 1)

            def down(g, slot, e, first):
                n = GE * g + e
                pe.wait_ge(gated, n + 1)
                if e % 2 == 0 and not first:
                    pe.wait_ge(down_ready, 2 * g - 1 + e // 2)
                for j in range(FT):
                    m = pe.matmul(pd[e // 2][:, e % 2, :], W2[slot][:, e, j, :], A[:, e % 2, j, :],
                                  start=(j == 0), stop=(j == FT - 1))
                m.then_inc(down_psum, 1)

            def turn_out(g):
                pe.wait_ge(down_ready, 2 * g + 2)
                for c in range(GC):
                    m = pe.transpose(pt[:, c, :], D_[:, c * P:(c + 1) * P], ident[:])
                m.then_inc(out_psum, 1)

            turn(0, 0, 0)
            up(0, 0, 0, 0, True)

            def one(g, slot, pair, first, last):
                for e in range(GE):
                    if e == 2 and not last:
                        if not first:
                            pe.wait_ge(out_ready, g)
                        turn(g + 1, 1 - slot, pair + slot)
                    if not (last and e == 3):
                        if e < 3:
                            up(g, slot, e + 1, pair, first)
                        else:
                            up(g + 1, 1 - slot, 0, pair + slot, False)
                    if e == 1 and not first:
                        pe.wait_ge(in_ready, g + 1)
                        turn_out(g - 1)
                    down(g, slot, e, first)

            groups(pe, one)
            turn_out(NG - 1)


def combine(nc, io, X, ident, results, ST):
    with ExitStack() as ctx:
        def sb(name, shape, dt=F32):
            return ctx.enter_context(nc.sbuf_tensor("c_" + name, shape, dt))

        sem = ctx.enter_context(semaphores(nc, "c_"))

        half, stat = sb("half", [P, NT]), sb("stat", [P, 5, NT])
        Z = sb("z", [P, 4, TOPK, E])
        Y, N_ = sb("y", [P, NT, E]), sb("n", [P, NT, E])
        ps = [ctx.enter_context(nc.psum_tensor(f"c_ps{i}", [P, TPC, E], F32)) for i in range(NCH)]
        loaded = [sem(f"loaded{i}") for i in range(4)]
        summed, shared_psum = sem("summed"), sem("shared_psum")
        var_ready, rstd_ready, dve_step, pool_step = (
            sem("var_ready"), sem("rstd_ready"), sem("dve_step"), sem("pool_step"))
        block = ctx.enter_context(nc.Block())

        @block.sync
        def _(sp):
            z = results.rearrange("(t p k) e -> t p k e", p=P, k=TOPK)
            for t in range(4):
                sp.dma_start(Z[:, t], z[t]).then_inc(loaded[t], 16)
            with sp.Fori(1, NT // 4) as i:
                for s in range(4):
                    sp.wait_ge(summed, 4 * i + s - 3)
                    sp.dma_start(Z[:, s], z[bass.ds(4 * i + s, 1)].rearrange("t p k e -> (t p) k e")
                                 ).then_inc(loaded[s], 16)

        @block.tensor
        def _(pe):
            for c in range(NCH):
                for j in range(TPC):
                    m = pe.transpose(ps[c][:, j, :], ST[:, (c * TPC + j) * P:(c * TPC + j + 1) * P], ident[:])
                m.then_inc(shared_psum, 1)

        @block.gpsimd
        def _(pool):
            step = Steps(pool, pool_step)
            step.then(pool.memset(half[:], -0.5))
            pool_rstd(pool, step, stat, NT, var_ready, 1, rstd_ready, half)

        @block.vector
        def _(dve):
            step = Steps(dve, dve_step)
            with dve.Fori(0, NT // 4) as i:
                for s in range(4):
                    dve.wait_ge(loaded[s], 16 * (i + 1))
                    dve.tensor_reduce(Y[:, bass.ds(4 * i + s, 1)], Z[:, s].rearrange("p k e -> p e k"),
                                      AX.X, ALU.add).then_inc(summed, 1)
            dve.wait_ge(summed, NT)
            for c in range(NCH):
                dve.wait_ge(shared_psum, c + 1)
                step(dve.tensor_tensor(Y[:, c * TPC:(c + 1) * TPC], Y[:, c * TPC:(c + 1) * TPC], ps[c][:], ALU.add))
            layernorm_rows(dve, step, Y[:], N_[:], Y[:], stat, None, var_ready, (rstd_ready, 1), NT)
            step.then(dve.tensor_tensor(X[:], X[:], N_[:], ALU.add))


DI, DS, DR, DC = 256, 16, 8, 4
DH = DI // P
PAD = DC - 1
TH = TOK // 2
HB = TH // S
HCH = TH // CH


def mamba(nc, io, X, ident):
    with ExitStack() as ctx:
        def sb(name, shape, dt=F32):
            return ctx.enter_context(nc.sbuf_tensor("m_" + name, shape, dt))

        def psum(name, shape, dt=F32):
            return ctx.enter_context(nc.psum_tensor("m_" + name, shape, dt))

        sem = ctx.enter_context(semaphores(nc, "m_"))

        half, stat = sb("half", [P, NT]), sb("stat", [P, 5, NT])
        N1, N2 = sb("n1", [P, NT, E]), sb("n2", [P, NT, E])
        sq, srw = sb("sq", [P, E]), sb("srw", [P, E])
        win = sb("win", [P, 2 * DI])
        wconv = sb("wconv", [P, DC, DI])
        wx = sb("wx", [P, DH, DR + 3 * 2 * DS])
        wdt = sb("wdt", [DR, DI])
        wout = sb("wout", [P, DH, E])
        vec = sb("vec", [P, 16])
        alog = sb("alog", [P, DH, DS])
        nA, negA = sb("na", [P, DH, DS]), sb("nega", [P, DH, DS])
        pick = sb("pick", [3 * 2 * DS, 2 * DS], BF16)
        pickf = sb("pickf", [3 * 2 * DS, 2 * DS])
        diagD = sb("diagd", [P, DH, P])
        gT = sb("gt", [P, CH])
        hP = sb("hp", [P, NB, PAD + S])
        U, SZ, delta, du = (sb(n, [P, DH, TOK]) for n in ("u", "sz", "delta", "du"))
        dtT = sb("dtT", [DR, TOK])
        BC = sb("bc", [3 * 2 * DS, TOK], BF16)
        rest = sb("rest", [3 * 2 * DS, CH])
        tmp = sb("tmp", [3 * 2 * DS, CH], BF16)
        Bn = [sb(f"bn{i}", [P, TH]) for i in range(2)]
        dA = [sb(f"da{i}", [P, HB, S]) for i in range(2)]
        dBu = [sb(f"dbu{i}", [P, TH]) for i in range(2)]
        hst = [sb(f"h{i}", [P, TH]) for i in range(2)]
        hC = [sb(f"hc{i}", [P, TH]) for i in range(2)]

        ps = [psum(f"ps{i}", [P, CH]) for i in range(4)]
        pB, pC = psum("pb", [P, TH]), psum("pc", [P, TH])
        vecs = {"g": 0, "b": 1, "sq_b": 2, "srw_b": 3, "scale": 4, "conv_b": 6, "dt_b": 8, "D": 10}

        def col(name, i=0):
            return vec[:, vecs[name] + i:vecs[name] + i + 1]

        loaded = sem("loaded")
        var_ready, rstd_ready, normed = sem("var_ready"), sem("rstd_ready"), sem("normed")
        hT_psum, gT_ready, sq_psum, hP_ready = sem("hT_psum"), sem("gT_ready"), sem("sq_psum"), sem("hP_ready")
        padded, taps_ready = sem("padded"), sem("taps_ready")
        uz_psum, uz_ready = sem("uz_psum"), sem("uz_ready")
        dbc_psum, dt_ready, bc_ready = sem("dbc_psum"), sem("dt_ready"), sem("bc_ready")
        dl_psum, e_ready, ln_ready, delta_ready = sem("dl_psum"), sem("e_ready"), sem("ln_ready"), sem("delta_ready")
        du_ready, diag_ready, nA_ready, dA_zero = sem("du_ready"), sem("diag_ready"), sem("nA_ready"), sem("dA_zero")
        negA_ready = sem("negA_ready")
        b_psum, c_psum, b_ready = sem("b_psum"), sem("c_psum"), sem("b_ready")
        dA_ready, dBu_ready, h_ready, hC_ready, hC_used = (
            sem("dA_ready"), sem("dBu_ready"), sem("h_ready"), sem("hC_ready"), sem("hC_used"))
        y_gated, out_psum, out_ready = sem("y_gated"), sem("out_psum"), sem("out_ready")
        srw_psum, g_ready, tok_psum, tok_read = sem("srw_psum"), sem("g_ready"), sem("tok_psum"), sem("tok_read")
        dve_step, pool_step, act_step = sem("dve_step"), sem("pool_step"), sem("act_step")

        block = ctx.enter_context(nc.Block())
        NLOAD = 20

        def over_states(eng, half_, one):
            one(0, 0, True, False)
            one(1, 1, False, False)
            with eng.Fori(1, DS // 2 - 1) as i:
                for s in range(2):
                    one(2 * i + s, s, False, False)
            one(DS - 2, 0, False, False)
            one(DS - 1, 1, False, True)

        @block.sync
        def _(sp):
            for dst, src in ((sq, "sq_w"), (srw, "srw_w"), (win, "in_proj_w"), (wdt, "dt_w"), (pickf, "pick")):
                sp.dma_start(dst[:], io[src]).then_inc(loaded, 16)
            sp.dma_start(wx[:], io["x_proj"].rearrange("(h p) c -> p h c", p=P)).then_inc(loaded, 16)
            sp.dma_start(wout[:], io["out_proj_w"].rearrange("(h p) c -> p h c", p=P)).then_inc(loaded, 16)
            sp.dma_start(alog[:], io["A_log"].rearrange("(h p) c -> p h c", p=P)).then_inc(loaded, 16)
            sp.dma_start(wconv[:], io["conv_wT"].unsqueeze(0).to_broadcast([P, DC, DI])).then_inc(loaded, 16)
            for n in ("g", "b", "sq_b", "srw_b"):
                sp.dma_start(col(n), io["m_" + n].unsqueeze(1)).then_inc(loaded, 16)
            sp.dma_start(col("scale"), io["res_scale"].unsqueeze(1).to_broadcast([P, 1])).then_inc(loaded, 16)
            for n in ("conv_b", "dt_b", "D"):
                for h in range(DH):
                    sp.dma_start(col(n, h), io["m_" + n][h * P:(h + 1) * P].unsqueeze(1)).then_inc(loaded, 16)
            sp.wait_ge(loaded, 16 * NLOAD)

        @block.gpsimd
        def _(pool):
            step = Steps(pool, pool_step)
            step.then(pool.memset(half[:], -0.5))
            pool.memset(hP[:, :, 0:PAD], 0.0).then_inc(padded, 1)
            pool.wait_ge(padded, 1)
            for s in range(2):
                pool.memset(dA[s][:, :, 0:1], 0.0).then_inc(dA_zero, 1)
            pool.wait_ge(dA_zero, 2)
            pool_rstd(pool, step, stat, NT, var_ready, 1, rstd_ready, half)
            pool_rstd(pool, step, stat, NT, var_ready, 2, rstd_ready, half)
            pool.wait_ge(loaded, 16 * NLOAD)
            for h in range(DH):
                pool.tensor_scalar(diagD[:, h], ident[:], col("D", h), 1.0, ALU.mult, ALU.mult).then_inc(diag_ready, 1)
            pool.wait_ge(nA_ready, 1)
            pool.tensor_scalar(negA[:], nA[:], -1.0, 1.0, ALU.mult, ALU.mult).then_inc(negA_ready, 1)
            for c in range(NCH):
                pool.wait_ge(delta_ready, c + 1)
                at = slice(c * CH, (c + 1) * CH)
                pool.tensor_tensor(du[:, :, at], delta[:, :, at], U[:, :, at], ALU.mult).then_inc(du_ready, 1)
            pool.wait_ge(du_ready, NCH)

            for hf in range(2):
                def one(n, s, first, last):
                    for h in range(DH):
                        k = (hf * DS + n) * DH + h
                        pool.wait_ge(b_ready, hf * DS + n + 1)
                        if not (hf == 0 and first):
                            pool.wait_ge(h_ready, k - 1)
                        pool.tensor_tensor(dBu[h][:], du[:, h, hf * TH:(hf + 1) * TH], Bn[s][:], ALU.mult
                                           ).then_inc(dBu_ready, 1)

                over_states(pool, hf, one)
            pool_rstd(pool, step, stat, NT, var_ready, 3, rstd_ready, half)

        @block.scalar
        def _(act):
            step = Steps(act, act_step)
            act.wait_ge(loaded, 16 * NLOAD)
            step.then(act.activation(pick[:], pickf[:], ACT.Copy))
            for c in range(NCH):
                act.wait_ge(hT_psum, c + 1)
                if c:
                    act.wait_ge(hP_ready, c)
                act.activation(gT[:], ps[0][:], ACT.Identity, bias=col("b"), scale=col("g")).then_inc(gT_ready, 1)
            for c in range(NCH):
                at = slice(c * CH, (c + 1) * CH)
                for j in range(4):
                    n = 4 * c + j
                    act.wait_ge(uz_psum, n + 1)
                    if j < DH:
                        act.activation(U[:, j, at], ps[j][:], ACT.Silu, bias=col("conv_b", j)).then_inc(uz_ready, 1)
                    else:
                        act.activation(SZ[:, j - DH, at], ps[j][:], ACT.Silu).then_inc(uz_ready, 1)
            act.activation(nA[:], alog[:], ACT.Exp).then_inc(nA_ready, 1)
            for c in range(NCH):
                at = slice(c * CH, (c + 1) * CH)
                act.wait_ge(dbc_psum, 2 * c + 1)
                act.activation(dtT[:, at], ps[2][0:DR, :], ACT.Copy).then_inc(dt_ready, 1)
            for c in range(NCH):
                at = slice(c * CH, (c + 1) * CH)
                act.wait_ge(dl_psum, c + 1)
                for h in range(DH):
                    step.then(act.activation(delta[:, h, at], ps[h][:], ACT.Identity, bias=col("dt_b", h)))
                    step.then(act.activation(du[:, h, at], delta[:, h, at], ACT.Abs))
                    step(act.activation(du[:, h, at], du[:, h, at], ACT.Exp, scale=-1.0))
                step.wait()
                act.drain().then_inc(e_ready, 1)
                for h in range(DH):
                    step(act.activation(hC[c % 2][:, h * CH:(h + 1) * CH], du[:, h, at], ACT.Ln, bias=1.0))
                step.wait()
                act.drain().then_inc(ln_ready, 1)
                act.wait_ge(delta_ready, c + 1)
            for hf in range(2):
                def one(n, s, first, last):
                    m = hf * DS + n
                    act.wait_ge(b_psum, m + 1)
                    if not (hf == 0 and isinstance(n, int) and n < 2):
                        act.wait_ge(dBu_ready, DH * (m - 1))
                    act.activation(Bn[s][:], pB[:], ACT.Copy).then_inc(b_ready, 1)
                    for h in range(DH):
                        k = m * DH + h
                        if not (hf == 0 and first):
                            act.wait_ge(h_ready, k - 1)
                        else:
                            act.wait_ge(dA_zero, 2)
                            act.wait_ge(negA_ready, 1)
                        act.activation(dA[h][:, :, 1:S],
                                       delta[:, h, hf * TH:(hf + 1) * TH].rearrange("p (b t) -> p b t", t=S)[:, :, 1:S],
                                       ACT.Exp, scale=negA[:, h, bass.ds(n, 1)]).then_inc(dA_ready, 1)

                over_states(act, hf, one)
                for c in range(HCH):
                    g = hf * HCH + c
                    act.wait_ge(out_psum, g + 1)
                    act.activation(gT[:], ps[2 * c][:], ACT.Copy).then_inc(out_ready, 1)
                    act.wait_ge(g_ready, g + 1)

        @block.vector
        def _(dve):
            v = dve
            step = Steps(dve, dve_step)
            layernorm_rows(dve, step, X[:], N1[:], N2[:], stat, None, var_ready, (rstd_ready, 1), NT)
            layernorm_rows(dve, step, N1[:], N2[:], U[:, 0].rearrange("p (t e) -> p t e", e=E), stat, None,
                           var_ready, (rstd_ready, 2), NT)
            dve.nop().then_inc(normed, 1)
            dve.wait_ge(loaded, 16 * NLOAD)
            v.tensor_tensor(wconv[:], wconv[:], win[:, 0:DI].unsqueeze(1).to_broadcast([P, DC, DI]), ALU.mult
                            ).then_inc(taps_ready, 1)
            for c in range(NCH):
                dve.wait_ge(sq_psum, c + 1)
                dve.wait_ge(padded, 1)
                v.scalar_tensor_tensor(hP[:, 2 * c:2 * c + 2, PAD:PAD + S], ps[1][:].rearrange("p (b t) -> p b t", t=S),
                                       col("sq_b"), gT[:].rearrange("p (b t) -> p b t", t=S), ALU.add, ALU.add
                                       ).then_inc(hP_ready, 1)
            for c in range(NCH):
                at = slice(c * CH, (c + 1) * CH)
                dve.wait_ge(dbc_psum, 2 * c + 2)
                step.then(v.tensor_copy(BC[:, at], ps[3][0:96, :]))
                step.then(v.tensor_tensor(rest[:], ps[3][0:96, :], BC[:, at], ALU.subtract))
                step(v.tensor_copy(BC[32:64, at], rest[32:64, :]))
                step.then(v.tensor_copy(tmp[64:96, :], rest[64:96, :]))
                v.tensor_tensor(BC[64:96, at], rest[64:96, :], tmp[64:96, :], ALU.subtract).then_inc(bc_ready, 1)
            for c in range(NCH):
                at = slice(c * CH, (c + 1) * CH)
                dve.wait_ge(e_ready, c + 1)
                lost = dBu[c % 2][:].rearrange("p (h t) -> p h t", h=DH)
                step.then(v.tensor_scalar(lost, du[:, :, at], 1.0, -1.0, ALU.add, ALU.add))
                step.then(v.tensor_tensor(lost, du[:, :, at], lost, ALU.subtract))
                dve.wait_ge(ln_ready, c + 1)
                step.then(v.tensor_tensor(lost, lost, hC[c % 2][:].rearrange("p (h t) -> p h t", h=DH), ALU.add))
                v.scalar_tensor_tensor(delta[:, :, at], delta[:, :, at], 0.0, lost, ALU.max, ALU.add
                                       ).then_inc(delta_ready, 1)
            for hf in range(2):
                def one(n, s, first, last):
                    for h in range(DH):
                        k = (hf * DS + n) * DH + h
                        dve.wait_ge(dA_ready, k + 1)
                        dve.wait_ge(dBu_ready, k + 1)
                        if not (hf == 0 and first):
                            dve.wait_ge(hC_ready, k - 1)
                        v.tensor_tensor_scan(hst[h][:], dA[h][:].rearrange("p b t -> p (b t)"), dBu[h][:], 0.0,
                                             ALU.mult, ALU.add).then_inc(h_ready, 1)
                        dve.wait_ge(h_ready, k + 1)
                        dve.wait_ge(c_psum, hf * DS + n + 1)
                        if not (hf == 0 and first):
                            dve.wait_ge(hC_used, k - 1)
                        v.tensor_tensor(hC[h][:], hst[h][:], pC[:], ALU.mult).then_inc(hC_ready, 1)

                over_states(dve, hf, one)
                dve.wait_ge(hC_used, DS * DH * (hf + 1))
                for h in range(DH):
                    for c in range(HCH):
                        at = slice(hf * TH + c * CH, hf * TH + (c + 1) * CH)
                        v.tensor_tensor(SZ[:, h, at], SZ[:, h, at], ps[2 * h + c][:], ALU.mult).then_inc(y_gated, 1)
                for c in range(HCH):
                    g = hf * HCH + c
                    dve.wait_ge(srw_psum, g + 1)
                    v.scalar_tensor_tensor(U[:, 0, g * CH:(g + 1) * CH], ps[2 * c + 1][:], col("srw_b"), gT[:],
                                           ALU.add, ALU.mult).then_inc(g_ready, 1)
                    dve.wait_ge(tok_psum, g + 1)
                    v.scalar_tensor_tensor(N2[:, g * TPC:(g + 1) * TPC], ps[2 * c][:].rearrange("p (t e) -> p t e", e=E),
                                           col("scale"), N1[:, g * TPC:(g + 1) * TPC], ALU.mult, ALU.add
                                           ).then_inc(tok_read, 1)
            dve.wait_ge(tok_read, NCH)
            layernorm_rows(dve, step, N2[:], N1[:], N2[:], stat, None, var_ready, (rstd_ready, 3), NT)
            step.then(v.tensor_tensor(X[:], X[:], N1[:], ALU.add))

        @block.tensor
        def _(pe):
            pe.wait_ge(loaded, 16 * NLOAD)
            pe.wait_ge(normed, 1)
            for c in range(NCH):
                if c:
                    pe.wait_ge(gT_ready, c)
                for j in range(TPC):
                    m = pe.transpose(ps[0][:, j * P:(j + 1) * P], N2[:, c * TPC + j, :], ident[:])
                m.then_inc(hT_psum, 1)
                pe.wait_ge(gT_ready, c + 1)
                if c:
                    pe.wait_ge(hP_ready, c)
                pe.matmul(ps[1][:], sq[:], gT[:], start=True, stop=True).then_inc(sq_psum, 1)
            pe.wait_ge(taps_ready, 1)
            pe.wait_ge(hP_ready, NCH)
            for c in range(NCH):
                for j in range(4):
                    if c:
                        pe.wait_ge(uz_ready, 4 * (c - 1) + j + 1)
                    out = ps[j][:].rearrange("p (b t) -> p b t", t=S)
                    if j < DH:
                        for k in range(DC):
                            m = pe.matmul(out, wconv[:, k, j * P:(j + 1) * P], hP[:, 2 * c:2 * c + 2, k:k + S],
                                          start=(k == 0), stop=(k == DC - 1))
                    else:
                        m = pe.matmul(out, win[:, j * P:(j + 1) * P], hP[:, 2 * c:2 * c + 2, PAD:PAD + S],
                                      start=True, stop=True)
                    m.then_inc(uz_psum, 1)
            pe.wait_ge(uz_ready, 4 * NCH)
            for c in range(NCH):
                at = slice(c * CH, (c + 1) * CH)
                if c:
                    pe.wait_ge(dt_ready, c)
                for h in range(DH):
                    m = pe.matmul(ps[2][0:DR, :], wx[:, h, 0:DR], U[:, h, at], start=(h == 0), stop=(h == DH - 1))
                m.then_inc(dbc_psum, 1)
                if c:
                    pe.wait_ge(bc_ready, c)
                for h in range(DH):
                    m = pe.matmul(ps[3][0:96, :], wx[:, h, DR:], U[:, h, at], start=(h == 0), stop=(h == DH - 1))
                m.then_inc(dbc_psum, 1)
            for c in range(NCH):
                at = slice(c * CH, (c + 1) * CH)
                pe.wait_ge(dt_ready, c + 1)
                if c:
                    pe.wait_ge(e_ready, c)
                for h in range(DH):
                    m = pe.matmul(ps[h][:], wdt[:, h * P:(h + 1) * P], dtT[:, at], start=True, stop=True)
                m.then_inc(dl_psum, 1)
            pe.wait_ge(bc_ready, NCH)
            pe.wait_ge(e_ready, NCH)
            pe.wait_ge(diag_ready, DH)
            for hf in range(2):
                if hf:
                    pe.wait_ge(tok_read, HCH)
                for h in range(DH):
                    for c in range(HCH):
                        pe.matmul(ps[2 * h + c][:], diagD[:, h], U[:, h, hf * TH + c * CH:hf * TH + (c + 1) * CH],
                                  start=True, stop=False)

                def one(n, s, first, last):
                    m = hf * DS + n
                    for p, row, free, done in ((pB, 0, (b_ready, m), b_psum), (pC, DS, (hC_ready, DH * m), c_psum)):
                        if not (hf == 0 and first):
                            pe.wait_ge(*free)
                        for c in range(HCH):
                            x = pe.matmul(p[:, c * CH:(c + 1) * CH],
                                          pick[:, bass.ds(n + row, 1)].to_broadcast([96, P]),
                                          BC[:, hf * TH + c * CH:hf * TH + (c + 1) * CH], start=True, stop=True)
                        x.then_inc(done, 1)
                    if not first:
                        add(n - 1, False)
                    if last:
                        add(n, True)

                def add(n, last):
                    for h in range(DH):
                        pe.wait_ge(hC_ready, (hf * DS + n) * DH + h + 1)
                        for c in range(HCH):
                            x = pe.matmul(ps[2 * h + c][:], ident[:], hC[h][:, c * CH:(c + 1) * CH],
                                          start=False, stop=last)
                        x.then_inc(hC_used, 1)

                over_states(pe, hf, one)
                for c in range(HCH):
                    g = hf * HCH + c
                    pe.wait_ge(y_gated, DH * HCH * (hf + 1))
                    for h in range(DH):
                        m = pe.matmul(ps[2 * c][:], wout[:, h, :], SZ[:, h, g * CH:(g + 1) * CH],
                                      start=(h == 0), stop=(h == DH - 1))
                    m.then_inc(out_psum, 1)
                    pe.wait_ge(out_ready, g + 1)
                    pe.matmul(ps[2 * c + 1][:], srw[:], gT[:], start=True, stop=True).then_inc(srw_psum, 1)
                    pe.wait_ge(g_ready, g + 1)
                    for j in range(TPC):
                        t = g * TPC + j
                        m = pe.transpose(ps[2 * c][:, j * P:(j + 1) * P], U[:, 0, t * P:(t + 1) * P], ident[:])
                    m.then_inc(tok_psum, 1)


RE, RH = 8, 512
NR = RE - 1
RT = RH // P
XW = E + 4
TILES = NT + NR
NROW = TILES * P
ALPHA = 2.0


def switch(nc, io, X, ident, xs, ys, out):
    with ExitStack() as ctx:
        def sb(name, shape, dt=F32):
            return ctx.enter_context(nc.sbuf_tensor("s_" + name, shape, dt))

        def psum(name, shape, dt=F32):
            return ctx.enter_context(nc.psum_tensor("s_" + name, shape, dt))

        sem = ctx.enter_context(semaphores(nc, "s_"))

        half, stat = sb("half", [P, NT]), sb("stat", [P, 5, NT])
        R4, Y = sb("r4", [P, NT, XW]), sb("y", [P, NT, E])
        Hn = R4[:, :, 0:E]
        hT, ST = sb("hT", [P, TOK]), sb("st", [P, TOK])
        rw = sb("rw", [P, RE])
        sug, sd = sb("sug", [P, 2, RH]), sb("sd", [P, RT, E])
        UG = sb("ug", [P, NR, 2, RH])
        DW = sb("dw", [P, NR, RT, E])
        zero = sb("zero", [P, TILES * XW])
        pr = [sb(f"pr{i}", [P, NT, RE]) for i in range(5)]
        small = sb("small", [P, 4, NT])
        rev = sb("rev", [P, RE])
        revi = sb("revi", [P, RE], I32)
        jrow, ji = sb("jrow", [P, TILES]), sb("ji", [P, TILES], I32)
        hot = sb("hot", [P, NT, RE], BF16)
        tri, ones = sb("tri", [P, P], BF16), sb("ones", [P, P], BF16)
        carry = sb("carry", [P, RE, NT])
        tot, inc, exc = (sb(n, [P, RE, NT]) for n in ("tot", "inc", "exc"))
        cnt = sb("cnt", [P, 6, RE])
        cnti = sb("cnti", [P, RE], I32)
        ge = sb("ge", [P, TILES, NR - 1])
        eidf, eid = sb("eidf", [P, TILES]), sb("eid", [P, TILES], I32)
        posf, pos = sb("posf", [P, NT]), sb("pos", [P, NT], I32)
        sgate = sb("sgate", [P, 2, CH])
        sact = sb("sact", [P, 2, RT, CH])
        xt = [sb(f"xt{i}", [P, XW]) for i in range(4)]
        xT = [sb(f"xT{i}", [P, P]) for i in range(2)]
        gl = [sb(f"gl{i}", [P, RH]) for i in range(2)]
        hid = [sb(f"hid{i}", [P, RH]) for i in range(2)]
        hidT = [sb(f"hidT{i}", [P, RT, P]) for i in range(2)]
        yt = [sb(f"yt{i}", [P, E]) for i in range(2)]
        back = sb("back", [P, NT, E])

        pu = [psum(f"pu{i}", [P, CH]) for i in range(2)]
        pg = [psum(f"pg{i}", [P, CH]) for i in range(2)]
        ph, px, py, pr_ = psum("ph", [P, RT, P]), psum("px", [P, P]), psum("py", [P, E]), psum("pr", [P, CH])

        loaded, cleared, zero_ready = sem("loaded"), sem("cleared"), sem("zero_ready")
        var_ready, rstd_ready, normed = sem("var_ready"), sem("rstd_ready"), sem("normed")
        hT_psum, hT_ready = sem("hT_psum"), sem("hT_ready")
        logits_psum, centred, exp_ready, const_ready = (
            sem("logits_psum"), sem("centred"), sem("exp_ready"), sem("const_ready"))
        hot_ready, counts_psum, pos_ready, eid_ready = (
            sem("hot_ready"), sem("counts_psum"), sem("pos_ready"), sem("eid_ready"))
        sorted_ = sem("sorted")
        sh_psum, sh_silu, sh_gated, sd_psum, sd_read = (
            sem("sh_psum"), sem("sh_silu"), sem("sh_gated"), sem("sd_psum"), sem("sd_read"))
        x_in = [sem(f"x_in{i}") for i in range(4)]
        xT_psum, xT_ready, ug_psum, silu_ready, hid_ready = (
            sem("xT_psum"), sem("xT_ready"), sem("ug_psum"), sem("silu_ready"), sem("hid_ready"))
        hT2_psum, hT2_ready, y_psum, y_ready, y_out = (
            sem("hT2_psum"), sem("hT2_ready"), sem("y_psum"), sem("y_ready"), [sem("y_out0"), sem("y_out1")])
        zrow_out, returned, shared_psum, final_ready, out_done = (
            sem("zrow_out"), sem("returned"), sem("shared_psum"), sem("final_ready"), sem("out_done"))
        dve_step, pool_step = sem("dve_step"), sem("pool_step")

        block = ctx.enter_context(nc.Block())
        NLOAD = 5

        @block.sync
        def _(sp):
            sp.dma_start(rw[:], io["router_w"]).then_inc(loaded, 16)
            sp.dma_start(sug[:], io["sug"]).then_inc(loaded, 16)
            sp.dma_start(sd[:], io["sdw"]).then_inc(loaded, 16)
            sp.dma_start(UG[:], io["ug"]).then_inc(loaded, 16)
            sp.dma_start(DW[:], io["dw"]).then_inc(loaded, 16)
            sp.wait_ge(zero_ready, 1)
            sp.dma_start(xs.rearrange("(p r) c -> p (r c)", p=P), zero[:]).then_inc(cleared, 16)
            sp.dma_start(ys[NROW:NROW + 1, :], zero[0:1, 0:E]).then_inc(zrow_out, 16)
            sp.wait_ge(sorted_, 16 * NT)
            src = xs.rearrange("(t p) c -> t p c", p=P)
            dst = ys[0:NROW].rearrange("(t p) c -> t p c", p=P)

            def load(j, s):
                sp.dma_start(xt[s][:], src[bass.ds(j, 1)].rearrange("t p c -> (t p) c")).then_inc(x_in[s], 16)

            def store(j, s):
                sp.wait_ge(y_ready, j + 1)
                sp.dma_start(dst[bass.ds(j, 1)].rearrange("t p c -> (t p) c"), yt[s][:]).then_inc(y_out[s], 16)

            for j in range(4):
                load(j, j)
            with sp.Fori(0, (TILES - 4) // 4) as i:
                for s in range(4):
                    sp.wait_ge(hid_ready, 4 * i + s + 1)
                    load(4 * i + s + 4, s)
                    store(4 * i + s, s % 2)
            done = (TILES - 4) // 4 * 4
            for j in range(done, TILES):
                if j + 4 < TILES:
                    sp.wait_ge(hid_ready, j + 1)
                    load(j + 4, j % 4)
                store(j, j % 2)
            sp.wait_ge(final_ready, 1)
            sp.dma_start(out.rearrange("b (t p) e -> p (b t) e", p=P), X[:]).then_inc(out_done, 16)
            sp.wait_ge(out_done, 16)

        @block.gpsimd
        def _(pool):
            step = Steps(pool, pool_step)
            pool.memset(zero[:], 0.0).then_inc(zero_ready, 1)
            step.then(pool.memset(half[:], -0.5))
            step.then(pool.iota(revi[:], pattern=[[-1, RE]], base=RE, channel_multiplier=0))
            step.then(pool.iota(ji[:], pattern=[[1, TILES]], base=0, channel_multiplier=0))
            step.then(pool.tensor_copy(rev[:], revi[:]))
            step.then(pool.tensor_copy(jrow[:], ji[:]))
            step.then(pool.memset(ones[:], 1.0))
            step.then(pool.affine_select(out=tri[:], in_=ones[:], compare_op=ALU.is_gt, fill=0.0, base=0,
                                         pattern=[[1, P]], channel_multiplier=-1))
            step.then(pool.memset(carry[:], 1.0))
            pool.memset(carry[:, :, 0:1], 0.0).then_inc(const_ready, 1)
            pool.wait_ge(const_ready, 1)
            pool_rstd(pool, step, stat, NT, var_ready, 1, rstd_ready, half)
            pool.wait_ge(pos_ready, 1)
            pool.wait_ge(cleared, 16)
            for t in range(NT):
                pool.indirect_dma_start(xs, bass.IndirectOffsetOnAxis(ap=pos[:, t:t + 1], axis=0), R4[:, t, :], None,
                                        bounds_check=NROW - 1, oob_is_err=False).then_inc(sorted_, 16)
            pool.wait_ge(y_out[0], 16 * ((TILES + 1) // 2))
            pool.wait_ge(y_out[1], 16 * (TILES // 2))
            pool.wait_ge(zrow_out, 16)
            for t in range(NT):
                pool.indirect_dma_start(back[:, t, :], None, ys, bass.IndirectOffsetOnAxis(ap=pos[:, t:t + 1], axis=0)
                                        ).then_inc(returned, 16)
            pool_rstd(pool, step, stat, NT, var_ready, 2, rstd_ready, half)

        def tile_loop(eng, one):
            one(0, 0)
            with eng.Fori(0, (TILES - 3) // 2) as i:
                one(2 * i + 1, 1)
                one(2 * i + 2, 0)
            one(TILES - 2, 1)
            one(TILES - 1, 0)

        @block.scalar
        def _(act):
            for c in range(NCH):
                act.wait_ge(hT_psum, c + 1)
                act.activation(hT[:, c * CH:(c + 1) * CH], pu[c % 2][:], ACT.Copy).then_inc(hT_ready, 1)
            act.wait_ge(centred, 1)
            act.activation(pr[1][:], pr[0][:], ACT.Exp).then_inc(exp_ready, 1)
            for c in range(NCH):
                for j in range(RT):
                    n = c * RT + j
                    act.wait_ge(sh_psum, n + 1)
                    if n >= 2:
                        act.wait_ge(sh_gated, n - 1)
                    act.activation(sgate[:, n % 2], pg[n % 2][:], ACT.Silu).then_inc(sh_silu, 1)
                act.wait_ge(sd_psum, c + 1)
                act.activation(ST[:, c * CH:(c + 1) * CH], pr_[:], ACT.Copy).then_inc(sd_read, 1)

            def turned(j, s):
                act.wait_ge(xT_psum, j + 1)
                if not (isinstance(j, int) and j < 2):
                    act.wait_ge(ug_psum, j - 1)
                act.activation(xT[s][:], px[:], ACT.Copy).then_inc(xT_ready, 1)

            def silu(j, s):
                act.wait_ge(ug_psum, j + 1)
                if not (isinstance(j, int) and j < 2):
                    act.wait_ge(hid_ready, j - 1)
                act.activation(gl[s][:], pg[s][:], ACT.Silu).then_inc(silu_ready, 1)

            def hidden_turned(j, s):
                act.wait_ge(hT2_psum, j + 1)
                if not (isinstance(j, int) and j < 2):
                    act.wait_ge(y_psum, j - 1)
                act.activation(hidT[s][:], ph[:], ACT.Copy).then_inc(hT2_ready, 1)

            turned(0, 0)
            turned(1, 1)
            silu(0, 0)

            def one(j, s):
                if not (isinstance(j, int) and j >= TILES - 2):
                    turned(j + 2, s)
                if not (isinstance(j, int) and j >= TILES - 1):
                    silu(j + 1, 1 - s)
                hidden_turned(j, s)

            tile_loop(act, one)

        @block.vector
        def _(dve):
            v = dve
            step = Steps(dve, dve_step)
            layernorm_rows(dve, step, X[:], Hn, Y[:], stat, None, var_ready, (rstd_ready, 1), NT)
            dve.nop().then_inc(normed, 1)
            dve.wait_ge(logits_psum, 1)
            lg = pr_[:, 0:NT * RE].rearrange("p (t e) -> p t e", e=RE)
            step.then(v.tensor_reduce(small[:, 0], lg, AX.X, ALU.max))
            v.tensor_tensor(pr[0][:], lg, per_row(small[:, 0], RE), ALU.subtract).then_inc(centred, 1)
            dve.wait_ge(exp_ready, 1)
            step.then(v.tensor_reduce(small[:, 1], pr[1][:], AX.X, ALU.add))
            step.then(v.reciprocal(small[:, 2], small[:, 1]))
            step.then(v.tensor_tensor(pr[0][:], pr[1][:], per_row(small[:, 2], RE), ALU.mult))
            step.then(v.tensor_reduce(small[:, 3], pr[0][:], AX.X, ALU.max))
            step.then(v.tensor_tensor(pr[1][:], pr[0][:], per_row(small[:, 3], RE), ALU.is_equal))
            dve.wait_ge(const_ready, 1)
            revb = rev[:].unsqueeze(1).to_broadcast([P, NT, RE])
            step.then(v.tensor_tensor(pr[2][:], pr[1][:], revb, ALU.mult))
            step.then(v.tensor_reduce(small[:, 0], pr[2][:], AX.X, ALU.max))
            step.then(v.tensor_tensor(pr[3][:], revb, per_row(small[:, 0], RE), ALU.is_equal))
            step(v.tensor_scalar(R4[:, :, E:XW], small[:, 3].unsqueeze(2).to_broadcast([P, NT, XW - E]), ALPHA, None,
                                 ALU.mult))
            v.tensor_copy(hot[:], pr[3][:]).then_inc(hot_ready, 1)
            dve.wait_ge(counts_psum, 1)
            before = pr_[:, 0:NT * RE].rearrange("p (t e) -> p t e", e=RE)
            totals = pr_[:, NT * RE:2 * NT * RE].rearrange("p (t e) -> p e t", e=RE)
            step.then(v.tensor_copy(tot[:], totals))
            flat = "p e t -> p (e t)"
            step.then(v.tensor_tensor_scan(inc[:].rearrange(flat), carry[:].rearrange(flat), tot[:].rearrange(flat),
                                           0.0, ALU.mult, ALU.add))
            step.then(v.tensor_tensor(exc[:], inc[:], tot[:], ALU.subtract))
            step.then(v.tensor_scalar(cnti[:], inc[:, :, NT - 1], float(P - 1), None, ALU.add))
            step.then(v.tensor_single_scalar(cnti[:], cnti[:], 7, ALU.logical_shift_right))
            step.then(v.tensor_copy(cnt[:, 0], cnti[:]))
            step.then(v.memset(cnt[:, 1], 1.0))
            step.then(v.tensor_tensor_scan(cnt[:, 2], cnt[:, 1], cnt[:, 0], 0.0, ALU.mult, ALU.add))
            step.then(v.tensor_tensor(cnt[:, 3], cnt[:, 2], cnt[:, 0], ALU.subtract))
            step.then(v.tensor_scalar(cnt[:, 4], cnt[:, 3], float(P), None, ALU.mult))
            step.then(v.tensor_tensor(pr[0][:], before, exc[:].rearrange("p e t -> p t e"), ALU.add))
            step.then(v.tensor_tensor(pr[1][:], pr[0][:], cnt[:, 4:5].to_broadcast([P, NT, RE]), ALU.add))
            step.then(v.memset(pr[1][:, :, NR:RE], float(NROW)))
            step.then(v.tensor_tensor(pr[2][:], pr[1][:], pr[3][:], ALU.mult))
            step.then(v.tensor_reduce(posf[:], pr[2][:], AX.X, ALU.add))
            v.tensor_copy(pos[:], posf[:]).then_inc(pos_ready, 1)
            step.then(v.tensor_tensor(ge[:], per_row(jrow[:], NR - 1),
                                      cnt[:, 2:3, 0:NR - 1].to_broadcast([P, TILES, NR - 1]), ALU.is_ge))
            step.then(v.tensor_reduce(eidf[:], ge[:], AX.X, ALU.add))
            v.tensor_copy(eid[:], eidf[:]).then_inc(eid_ready, 1)
            for c in range(NCH):
                for j in range(RT):
                    n = c * RT + j
                    dve.wait_ge(sh_silu, n + 1)
                    if c >= 2 and j == 0:
                        dve.wait_ge(sd_psum, c - 1)
                    v.tensor_tensor(sact[:, c % 2, j], sgate[:, n % 2], pu[n % 2][:], ALU.mult).then_inc(sh_gated, 1)

            def gate4(j, s4, k4):
                s = s4 % 2
                dve.wait_ge(silu_ready, j + 1)
                dve.wait_ge(x_in[s4], 16 * (k4 + 1))
                if not (isinstance(j, int) and j < 2):
                    dve.wait_ge(hT2_psum, j - 1)
                v.scalar_tensor_tensor(hid[s][:], pu[s][:], xt[s4][:, E:E + 1], gl[s][:], ALU.mult, ALU.mult
                                       ).then_inc(hid_ready, 1)

            def result(j, s, k, first=False):
                dve.wait_ge(y_psum, j + 1)
                if not first:
                    dve.wait_ge(y_out[s], 16 * k)
                v.tensor_copy(yt[s][:], py[:]).then_inc(y_ready, 1)

            gate4(0, 0, 0)
            gate4(1, 1, 0)
            gate4(2, 2, 0)
            result(0, 0, 0, True)
            gate4(3, 3, 0)
            result(1, 1, 0, True)
            with dve.Fori(1, TILES // 4) as i:
                for s4 in range(4):
                    gate4(4 * i + s4, s4, i)
                    result(4 * i + s4 - 2, s4 % 2, 2 * i + s4 // 2 - 1)
            for j in range(TILES // 4 * 4, TILES):
                gate4(j, j % 4, j // 4)
                result(j - 2, j % 2, j // 2 - 1)
            for j in (TILES - 2, TILES - 1):
                result(j, j % 2, j // 2)
            dve.wait_ge(returned, 16 * NT)
            banks = [pu[0], pu[1], pg[0], pg[1]]
            for c in range(NCH):
                dve.wait_ge(shared_psum, c + 1)
                step(v.tensor_tensor(Y[:, c * TPC:(c + 1) * TPC], back[:, c * TPC:(c + 1) * TPC],
                                     banks[c][:].rearrange("p (t e) -> p t e", e=E), ALU.add))
            layernorm_rows(dve, step, Y[:], back[:], Y[:], stat, None, var_ready, (rstd_ready, 2), NT)
            v.tensor_tensor(X[:], X[:], back[:], ALU.add).then_inc(final_ready, 1)

        @block.tensor
        def _(pe):
            pe.wait_ge(loaded, 16 * NLOAD)
            pe.wait_ge(normed, 1)
            for c in range(NCH):
                if c >= 2:
                    pe.wait_ge(hT_ready, c - 1)
                for j in range(TPC):
                    t = pe.transpose(pu[c % 2][:, j * P:(j + 1) * P], Hn[:, c * TPC + j, :], ident[:])
                t.then_inc(hT_psum, 1)
            pe.wait_ge(hT_ready, NCH)
            for t in range(NT):
                m = pe.matmul(pr_[:, t * RE:(t + 1) * RE], hT[:, t * P:(t + 1) * P], rw[:], start=True, stop=True)
            m.then_inc(logits_psum, 1)
            pe.wait_ge(hot_ready, 1)
            pe.wait_ge(const_ready, 1)
            hots = hot[:].rearrange("p t e -> p (t e)")
            pe.matmul(pr_[:, 0:NT * RE], tri[:], hots, start=True, stop=True)
            pe.matmul(pr_[:, NT * RE:2 * NT * RE], ones[:], hots, start=True, stop=True).then_inc(counts_psum, 1)
            for c in range(NCH):
                at = slice(c * CH, (c + 1) * CH)
                for j in range(RT):
                    n = c * RT + j
                    if n >= 2:
                        pe.wait_ge(sh_gated, n - 1)
                    pe.matmul(pg[n % 2][:], sug[:, 1, j * P:(j + 1) * P], hT[:, at], start=True, stop=True)
                    pe.matmul(pu[n % 2][:], sug[:, 0, j * P:(j + 1) * P], hT[:, at], start=True, stop=True
                              ).then_inc(sh_psum, 1)
                pe.wait_ge(sh_gated, (c + 1) * RT)
                if c:
                    pe.wait_ge(sd_read, c)
                else:
                    pe.wait_ge(pos_ready, 1)
                for j in range(RT):
                    m = pe.matmul(pr_[:], sd[:, j, :], sact[:, c % 2, j, :], start=(j == 0), stop=(j == RT - 1))
                m.then_inc(sd_psum, 1)

            def turn(j, s4, k4):
                pe.wait_ge(x_in[s4], 16 * (k4 + 1))
                if not (isinstance(j, int) and j == 0):
                    pe.wait_ge(xT_ready, j)
                pe.transpose(px[:], xt[s4][:, 0:E], ident[:]).then_inc(xT_psum, 1)

            def up(j, s):
                e = pe.value_load(eid[0:1, bass.ds(j, 1)], min_val=0, max_val=NR - 1)
                pe.wait_ge(xT_ready, j + 1)
                if not (isinstance(j, int) and j < 2):
                    pe.wait_ge(hid_ready, j - 1)
                pe.matmul(pg[s][:], xT[s][:], UG[:, bass.ds(e, 1), 1, :].rearrange("p a h -> p (a h)"),
                          start=True, stop=True)
                pe.matmul(pu[s][:], xT[s][:], UG[:, bass.ds(e, 1), 0, :].rearrange("p a h -> p (a h)"),
                          start=True, stop=True).then_inc(ug_psum, 1)

            def hidden(j, s):
                pe.wait_ge(hid_ready, j + 1)
                if not (isinstance(j, int) and j == 0):
                    pe.wait_ge(hT2_ready, j)
                for i in range(RT):
                    m = pe.transpose(ph[:, i, :], hid[s][:, i * P:(i + 1) * P], ident[:])
                m.then_inc(hT2_psum, 1)

            def down(j, s):
                e = pe.value_load(eid[0:1, bass.ds(j, 1)], min_val=0, max_val=NR - 1)
                pe.wait_ge(hT2_ready, j + 1)
                if not (isinstance(j, int) and j == 0):
                    pe.wait_ge(y_ready, j)
                for i in range(RT):
                    m = pe.matmul(py[:], hidT[s][:, i, :], DW[:, bass.ds(e, 1), i, :].rearrange("p a h -> p (a h)"),
                                  start=(i == 0), stop=(i == RT - 1))
                m.then_inc(y_psum, 1)

            pe.wait_ge(eid_ready, 1)
            pe.wait_ge(sh_gated, NCH * RT)

            def one(j, s4, k4):
                last = isinstance(j, int)
                if not (last and j >= TILES - 2):
                    turn(j + 2, (s4 + 2) % 4, k4 + (s4 + 2) // 4)
                if not (last and j >= TILES - 1):
                    up(j + 1, (s4 + 1) % 2)
                if not (last and j == 0):
                    down(j - 1, (s4 + 1) % 2)
                hidden(j, s4 % 2)

            turn(0, 0, 0)
            turn(1, 1, 0)
            up(0, 0)
            for j in range(4):
                one(j, j, 0)
            with pe.Fori(1, TILES // 4) as i:
                for s4 in range(4):
                    one(4 * i + s4, s4, i)
            for j in range(TILES // 4 * 4, TILES):
                one(j, j % 4, j // 4)
            down(TILES - 1, (TILES - 1) % 2)
            pe.wait_ge(hid_ready, TILES)
            pe.wait_ge(sd_read, NCH)
            banks = [pu[0], pu[1], pg[0], pg[1]]
            for c in range(NCH):
                for j in range(TPC):
                    m = pe.transpose(banks[c][:, j * P:(j + 1) * P], ST[:, (c * TPC + j) * P:(c * TPC + j + 1) * P],
                                     ident[:])
                m.then_inc(shared_psum, 1)


def sandwich(nc, io, out):
    rows = nc.dram_tensor("expert_rows", (TOK, ROWW), F32, kind="Internal").ap()
    results = nc.dram_tensor("pick_results", (NZ, E), F32, kind="Internal").ap()
    slots = nc.dram_tensor("expert_slots", (NSLOT,), F32, kind="Internal").ap()
    xs = nc.dram_tensor("sorted_rows", (NROW, XW), F32, kind="Internal").ap()
    ys = nc.dram_tensor("sorted_results", (NROW + 1, E), F32, kind="Internal").ap()
    with ExitStack() as ctx:
        X = ctx.enter_context(nc.sbuf_tensor("X", [P, NT, E], F32))
        ident = ctx.enter_context(nc.sbuf_tensor("identity", [P, P], F32))
        attention(nc, io, X, ident)
        with ExitStack() as ffn:
            ST = ffn.enter_context(nc.sbuf_tensor("shared_T", [P, TOK], F32))
            tab = ffn.enter_context(nc.sbuf_tensor("row_table", [P, NG, 2, GC], I32))
            route(nc, io, X, ident, rows, slots, tab, ST)
            experts(nc, io, ident, rows, results, tab)
            combine(nc, io, X, ident, results, ST)
        mamba(nc, io, X, ident)
        switch(nc, io, X, ident, xs, ys, out)


def kernel(**inputs):
    import numpy as np
    import concourse.bacc as bacc
    from concourse.bass_utils import run_bass_kernel_spmd

    a = {name: np.asarray(value) for name, value in inputs.items()}

    def attn(name):
        return a["L0_attn_" + name]

    def moe(name):
        return a["L0_ffn_" + name]

    def mix(name):
        return a["L1_attn_" + name]

    def sw(name):
        return a["L1_ffn_" + name]

    def by_feature(w):
        return w.reshape(w.shape[:-1] + (H, D)).swapaxes(-1, -2).reshape(w.shape)

    Jd = np.zeros((E, E), np.float32)
    for h in range(H):
        Jd[h::H, h::H] = attn("J_attn")[h]
    own = np.zeros((P, GC, GE), np.float32)
    for r in range(GR):
        own[r % P, r // P, r // CAP] = 1
    bc_rows = 2 * DS
    pick = np.zeros((3 * bc_rows, bc_rows), np.float32)
    for r in range(3 * bc_rows):
        pick[r, r % bc_rows] = 1
    xp = mix("x_proj_w")
    arrays = dict(
        x=attn("x"), ident=np.eye(P, dtype=np.float32),
        WqT=by_feature(attn("Wq").T), WkT=by_feature(attn("Wk").T), WvT=attn("Wv").T, WoT=attn("Wo").T, Jd=Jd,
        bq=by_feature(attn("bq")), bk=by_feature(attn("bk")), bv=attn("bv"), bo=attn("bo"),
        lam=attn("lambda_attn").reshape(1),
        wgT=moe("wg").T, sw1T=moe("shared_w1").T, sw2T=moe("shared_w2").T.reshape(FT, P, E).transpose(1, 0, 2),
        w1T=moe("expert_w1").reshape(NG, GE, 2 * FF, E).transpose(0, 3, 1, 2),
        w2T=moe("expert_w2").reshape(NG, GE, E, FT, P).transpose(0, 4, 1, 3, 2), own=own,
        sq_w=mix("sq_w"), srw_w=mix("srw_w"), in_proj_w=mix("in_proj_w"), dt_w=mix("dt_w"), pick=pick,
        x_proj=np.concatenate([xp[:, :DR]] + [xp[:, DR:]] * 3, 1), out_proj_w=mix("out_proj_w"),
        A_log=mix("A_log"), conv_wT=mix("conv_w").T, m_g=mix("ln_g"), m_b=mix("ln_b"), m_sq_b=mix("sq_b"),
        m_srw_b=mix("srw_b"), res_scale=mix("res_scale"), m_conv_b=mix("conv_b"), m_dt_b=mix("dt_b"), m_D=mix("D"),
        router_w=sw("router_w"), sug=np.stack([sw("shared_up_w"), sw("shared_gate_w")], 1),
        sdw=sw("shared_down_w").reshape(RT, P, E).transpose(1, 0, 2),
        ug=np.stack([sw("up_w"), sw("gate_w")], 1).transpose(2, 0, 1, 3),
        dw=sw("down_w").reshape(NR, RT, P, E).transpose(2, 0, 1, 3))

    nc = bacc.Bacc("TRN2", target_bir_lowering=False, num_devices=1)
    io, fed = {}, {}
    for name, array in arrays.items():
        fed[f"in_{name}_dram"] = np.ascontiguousarray(array)
        io[name] = nc.dram_tensor(f"in_{name}_dram", array.shape, mybir.dt.from_np(array.dtype),
                                  kind="ExternalInput").ap()
    out = nc.dram_tensor("out_dram", (NB, S, E), F32, kind="ExternalOutput").ap()
    sandwich(nc, io, out)
    r = run_bass_kernel_spmd(nc, [fed], core_ids=[0])
    return r.results[0]["out_dram"]
```

```python
from contextlib import ExitStack, contextmanager

import concourse.bass as bass
from concourse import mybir

F32 = mybir.dt.float32
BF16 = mybir.dt.bfloat16
I32 = mybir.dt.int32
ALU = mybir.AluOpType
ACT = mybir.ActivationFunctionType
AX = mybir.AxisListType

P = 128
NB, S, E = 8, 256, 128
TOK = NB * S
NT = TOK // P
TPB = S // P
CH = 512
NCH = TOK // CH
TPC = CH // P
EPS = 1e-5


@contextmanager
def semaphores(nc, prefix):
    taken = []

    def sem(name):
        taken.append(nc.alloc_semaphore(prefix + name))
        return taken[-1]

    yield sem
    nc.clear_and_free_semaphores(taken)
    nc.all_engine_barrier()


class Steps:

    def __init__(self, eng, sem, passes=None):
        self.eng, self.sem, self.n, self.passes = eng, sem, 0, passes

    def __call__(self, ins):
        ins.then_inc(self.sem, 1)
        self.n = self.n + 1
        return ins

    def wait(self):
        self.eng.wait_ge(self.sem, self.n)
        if self.passes is not None and not isinstance(self.n, int):
            self.eng.sem_inc(self.passes, 1)

    def then(self, ins):
        self(ins)
        self.wait()


def per_row(ap, n):
    return ap.unsqueeze(2).to_broadcast([ap.shape[0], ap.shape[1], n])


class Norms:

    def __init__(self, sb, sem, n):
        self.moments = sb("ln_moments", [P, n, NT, 6])
        self.mean_var = sb("ln_mean_var", [P, n, NT, 2])
        self.var_eps, self.rstd = sb("ln_var_eps", [P, n, NT]), sb("ln_rstd", [P, n, NT])
        self.half = sb("ln_half", [P, TPC])
        self.stats_ready, self.rstd_ready = sem("ln_stats_ready"), sem("ln_rstd_ready")
        self.half_ready = sem("ln_half_ready")

    def statistics(self, dve, step, k, c, src):
        tiles = range(c * TPC, (c + 1) * TPC)
        for t in tiles:
            step(dve.bn_stats(self.moments[:, k, t, :], src[:, t, :]))
        step.wait()
        for t in tiles:
            a = dve.bn_aggr(self.mean_var[:, k, t, :], self.moments[:, k, t, :])
        a.then_inc(self.stats_ready, 1)

    def apply(self, dve, k, c, src, dst):
        dve.wait_ge(self.rstd_ready, k * NCH + c + 1)
        for t in range(c * TPC, (c + 1) * TPC):
            a = dve.tensor_scalar(dst[:, t, :], src[:, t, :], self.mean_var[:, k, t, 0:1], self.rstd[:, k, t:t + 1],
                                  ALU.subtract, ALU.mult)
        return a

    def rows(self, dve, step, k, src, dst, done):
        for c in range(NCH):
            self.statistics(dve, step, k, c, src)
        for c in range(NCH):
            self.apply(dve, k, c, src, dst).then_inc(done, 1)

    def residual(self, dve, step, k, src, X, done):
        for c in range(NCH):
            step.then(self.apply(dve, k, c, src, src))
            at = slice(c * TPC, (c + 1) * TPC)
            dve.tensor_tensor(X[:, at], X[:, at], src[:, at], ALU.add).then_inc(done, 1)

    def prepare(self, pool):
        pool.memset(self.half[:], -0.5).then_inc(self.half_ready, 1)

    def roots(self, pool, step, k):
        pool.wait_ge(self.half_ready, 1)
        for c in range(NCH):
            at = slice(c * TPC, (c + 1) * TPC)
            pool.wait_ge(self.stats_ready, k * NCH + c + 1)
            step.then(pool.tensor_scalar(self.var_eps[:, k, at], self.mean_var[:, k, at, 1], 1.0, EPS,
                                         ALU.mult, ALU.add))
            pool.tensor_tensor(self.rstd[:, k, at], self.var_eps[:, k, at], self.half[:], ALU.pow
                               ).then_inc(self.rstd_ready, 1)


H, D = 16, 8
PARTS = 3
BLOCKS = 6
FEAT = 2 * D
KROWS = BLOCKS * FEAT
KALL = KROWS + PARTS
RING = 8
ZW = 1024
AHEAD = (1, 1, 1, 1, 2, 1, 1, 1, 2, 1, 1, 1, 2, 0, 0, 0)


def attention(nc, io, X, ident, results):
    with ExitStack() as ctx:
        def sb(name, shape, dt=F32):
            return ctx.enter_context(nc.sbuf_tensor(name, shape, dt))

        def psum(name, shape, dt=F32):
            return ctx.enter_context(nc.psum_tensor(name, shape, dt))

        sem = ctx.enter_context(semaphores(nc, "a_"))

        w = sb("a_w", [P, 5, E])
        vec = sb("a_vec", [P, 4])
        rowb = sb("a_rowb", [P, 2, E])
        Hn = sb("a_hn", [P, NT, E])
        Y = sb("a_y", [P, NT, E])
        hT = sb("a_hT", [P, TOK])
        TQ = sb("a_tq", [P, TOK])
        S4 = sb("a_s4", [P, 4, TOK])
        V = sb("a_v", [P, NT, H, D + 1])
        part = sb("a_part", [P, 2, PARTS, 4, S], BF16)
        rest = sb("a_rest", [P, 2, 4, S])
        QS = [sb(f"a_qs{i}", [KALL, H, S], BF16) for i in range(2)]
        KS = [sb(f"a_ks{i}", [KALL, H, S], BF16) for i in range(2)]
        mx = sb("a_mx", [P, TPB, H])
        mr = sb("a_mr", [2 * H, 2, P])
        mp = [sb(f"a_mp{i}", [2 * H, PARTS, P], BF16) for i in range(2)]
        PT = sb("a_pt", [P, RING, TPB, S])
        Vb = sb("a_vb", [P, 2, TPB, H, 32])
        OU = sb("a_ou", [P, 2, 2, S])
        rden = sb("a_rden", [P, 2, 2, TPB, 4])
        O = sb("a_o", [P, TPB, E])
        OT = sb("a_ot", [P, S])
        zero = sb("a_zero", [P, ZW])

        ps1 = [psum(f"a_s1_{i}", [P, TPB, S]) for i in range(2)]
        ps2 = [psum(f"a_s2_{i}", [P, TPB, S]) for i in range(2)]
        pso = [psum(f"a_po{i}", [P, 2, S]) for i in range(2)]
        pst = psum("a_pt_", [P, 2, TPB, P])
        psm = psum("a_pm", [P, CH])

        def flat(bank):
            return bank[:].rearrange("p a b -> p (a b)")

        wide = [flat(x) for x in (ps1[0], ps1[1], ps2[0], ps2[1])]
        qbank, kbank = [flat(x) for x in ps2], [flat(x) for x in pso]

        bounce = nc.dram_tensor("a_bounce", (2, PARTS * 4, P, S), BF16, kind="Internal").ap()
        bounced_rows = bounce.rearrange("s (c a) (d h) t -> s c (a d) (h t)", a=4, h=H)

        loaded, bounced = sem("loaded"), sem("bounced")
        norms = Norms(lambda name, shape: sb("a_" + name, shape), sem, 2)
        zero_ready, cleared = sem("zero_ready"), sem("cleared")
        x_ready, x_done = sem("x_ready"), sem("x_done")
        normed, hT_psum, hT_ready = sem("normed"), sem("hT_psum"), sem("hT_ready")
        qk_psum, qk_ready = sem("qk_psum"), sem("qk_ready")
        qj_psum, qj_ready = sem("qj_psum"), sem("qj_ready")
        v_psum, v_ready, v_ones = sem("v_psum"), sem("v_ready"), sem("v_ones")
        k_ones = sem("k_ones")
        split_ready, stack_ready = sem("split_ready"), [sem("stack0"), sem("stack1")]
        vb_ready = sem("vb_ready")
        rows_psum, rows_maxed = sem("rows_psum"), sem("rows_maxed")
        maxT_psum, maxT_ready, max_rows = sem("maxT_psum"), sem("maxT_ready"), [sem("maxr0"), sem("maxr1")]
        cols_psum, exp_ready, pv_done = sem("cols_psum"), sem("exp_ready"), sem("pv_done")
        ou_ready, ot_psum = sem("ou_ready"), sem("ot_psum")
        o_ready, oT_psum, oT_ready, y_psum, y_ready = (
            sem("o_ready"), sem("oT_psum"), sem("oT_ready"), sem("y_psum"), sem("y_ready"))
        den_ready = sem("den_ready")
        dve_step, act_step, pool_step = sem("dve_step"), sem("act_step"), sem("pool_step")
        pool_passes, sp_passes = sem("pool_passes"), sem("sp_passes")

        NLOAD = 11

        block = ctx.enter_context(nc.Block())

        @block.sync
        def _(sp):
            sp.dma_start(X[:], io["x"].rearrange("b (t p) e -> p (b t) e", p=P)).then_inc(x_ready, 16)
            for n, name in enumerate(("WqT", "WkT", "WvT", "WoT", "Jd")):
                sp.dma_start(w[:, n, :], io[name]).then_inc(loaded, 16)
            for n, name in enumerate(("bq", "bk")):
                sp.dma_start(vec[:, n:n + 1], io[name].unsqueeze(1)).then_inc(loaded, 16)
            sp.dma_start(vec[:, 2:3], io["lam"].unsqueeze(1).to_broadcast([P, 1])).then_inc(loaded, 16)
            for n, name in enumerate(("bv", "bo")):
                sp.dma_start(rowb[:, n, :], io[name].unsqueeze(0).to_broadcast([P, E])).then_inc(loaded, 16)
            sp.dma_start(ident[:], io["ident"]).then_inc(loaded, 16)
            sp.wait_ge(zero_ready, 1)
            cleared_rows = results.rearrange("(n p r) e -> n p (r e)", p=P, r=ZW // E)
            for n in range(cleared_rows.shape[0]):
                sp.dma_start(cleared_rows[n], zero[:]).then_inc(cleared, 16)

            def bounce_out(b, s):
                sp.wait_ge(split_ready, b + 1)
                sp.dma_start(bounce[s].rearrange("c f t -> f c t"),
                             part[:, s].rearrange("p c a t -> p (c a) t")).then_inc(bounced, 16)

            def stack(b, s, first=False):
                if not first:
                    sp.wait_ge(cols_psum, (b - 1) * H)
                    sp.sem_inc(sp_passes, 1)
                sp.wait_ge(bounced, 16 * (b + 1))
                for row, n, qp, kp in ((0, 3, 0, 0), (3, 2, 1, 0), (5, 1, 2, 0)):
                    rows = slice(row * FEAT, (row + n) * FEAT)
                    q = bounced_rows[s, qp:qp + 1, 0:FEAT].to_broadcast([n, FEAT, H * S])
                    sp.dma_start(QS[s][rows].rearrange("r h t -> r (h t)"), q).then_inc(stack_ready[s], 16)
                    sp.dma_start(KS[s][rows].rearrange("r h t -> r (h t)"), bounced_rows[s, kp:kp + n, FEAT:2 * FEAT]
                                 ).then_inc(stack_ready[s], 16)

            def max_row(b, s):
                sp.wait_ge(maxT_ready, b + 1)
                for it in range(TPB):
                    for c in range(PARTS):
                        sp.dma_start(QS[s][KROWS + c:KROWS + c + 1, :, it * P:(it + 1) * P],
                                     mp[s][it * H:(it + 1) * H, c, :]
                                     ).then_inc(max_rows[s], 16)

            for b in range(2):
                bounce_out(b, b)
                stack(b, b, first=True)
            max_row(0, 0)

            def step(b, s):
                bounce_out(b + 2, s)
                max_row(b + 1, 1 - s)
                stack(b + 2, s)

            with sp.Fori(0, NB // 2 - 1) as i:
                for s in range(2):
                    step(2 * i + s, s)
            max_row(NB - 1, 1)
            sp.wait_ge(cleared, 16 * cleared_rows.shape[0])

        @block.gpsimd
        def _(pool):
            step = Steps(pool, pool_step, passes=pool_passes)
            pool.memset(zero[:], 0.0).then_inc(zero_ready, 1)
            norms.prepare(pool)
            pool.memset(V[:, :, :, D:D + 1], 1.0).then_inc(v_ones, 1)
            pool.wait_ge(v_ones, 1)
            for s in range(2):
                pool.memset(KS[s][KROWS:KALL], 1.0).then_inc(k_ones, 1)
                pool.wait_ge(k_ones, s + 1)
            norms.roots(pool, step, 0)
            step.then(pool.memset(Vb[:], 0.0))
            pool.wait_ge(qj_ready, NCH)
            pool.wait_ge(v_ready, NCH)

            def split(b, s):
                src = S4[:, :, bass.ds(b * S, S)]
                step.then(pool.tensor_copy(part[:, s, 0], src))
                step.then(pool.tensor_tensor(rest[:, s], src, part[:, s, 0], ALU.subtract))
                step.then(pool.tensor_copy(part[:, s, 1], rest[:, s]))
                pool.tensor_tensor(part[:, s, 2], rest[:, s], part[:, s, 1], ALU.subtract).then_inc(split_ready, 1)

            def v_of(b, s):
                pool.tensor_copy(Vb[:, s, :, :, 0:D + 1], V[:, bass.ds(b * TPB, TPB)]).then_inc(vb_ready, 1)

            for b in range(2):
                split(b, b)
                v_of(b, b)
            first = step.n
            with pool.Fori(0, NB // 2 - 1) as i:
                for s in range(2):
                    step.n = first + i * 6 + 3 * s
                    pool.wait_ge(bounced, 16 * (2 * i + s + 1))
                    split(2 * i + s + 2, s)
                    pool.wait_ge(pv_done, 4 * (2 * i + s + 1))
                    v_of(2 * i + s + 2, s)
            step.n = first + (NB // 2 - 1) * 6
            norms.roots(pool, step, 1)

        @block.scalar
        def _(act):
            for c in range(NCH):
                act.wait_ge(hT_psum, c + 1)
                act.activation(hT[:, c * CH:(c + 1) * CH], wide[c], ACT.Copy).then_inc(hT_ready, 1)
            act.wait_ge(loaded, 16 * NLOAD)
            step = Steps(act, act_step)
            for c in range(NCH):
                at = slice(c * CH, (c + 1) * CH)
                for n in range(2):
                    act.wait_ge(qk_psum, 2 * c + n + 1)
                    src = (qbank, kbank)[n][c % 2]
                    if n == 0:
                        step.then(act.activation(S4[:, 0, at], src, ACT.Identity, bias=vec[:, 0:1]))
                        act.activation(TQ[:, at], S4[:, 0, at], ACT.Tanh).then_inc(qk_ready, 1)
                        act.wait_ge(qk_ready, 2 * c + 1)
                        step(act.activation(S4[:, 0, at], S4[:, 0, at], ACT.Copy, scale=float(D) ** -0.5))
                    else:
                        step(act.activation(S4[:, 2, at], src, ACT.Identity, bias=vec[:, 1:2]))
                        act.activation(S4[:, 3, at], src, ACT.Tanh, bias=vec[:, 1:2]).then_inc(qk_ready, 1)
                act.wait_ge(qj_psum, c + 1)
                act.activation(S4[:, 1, at], psm[:], ACT.Copy, scale=vec[:, 2:3]).then_inc(qj_ready, 1)

            def evacuate(b, q):
                act.wait_ge(pv_done, 4 * b + 2 * q + 2)
                act.activation(OU[:, q], pso[q][:], ACT.Copy).then_inc(ou_ready, 1)

            def one(b, first=False):
                for h in range(H):
                    act.wait_ge(cols_psum, b * H + h + 1)
                    if not (first and h < RING):
                        act.wait_ge(pv_done, 4 * b + (h - RING) // 4 + 1)
                    act.activation(PT[:, h % RING], ps2[h % 2][:], ACT.Exp).then_inc(exp_ready, 1)
                    if h == 0 and not first:
                        evacuate(b - 1, 1)
                    if h == 11:
                        evacuate(b, 0)

            step.wait()
            one(0, first=True)
            with act.Fori(1, NB) as b:
                one(b)
            evacuate(NB - 1, 1)

        @block.vector
        def _(dve):
            step = Steps(dve, dve_step)
            dve.wait_ge(x_ready, 16)
            norms.rows(dve, step, 0, X, Hn, normed)
            dve.wait_ge(loaded, 16 * NLOAD)
            dve.wait_ge(v_ones, 1)
            for c in range(NCH):
                dve.wait_ge(v_psum, c + 1)
                dve.tensor_tensor(V[:, c * TPC:(c + 1) * TPC, :, 0:D],
                                  ps1[c % 2][:].rearrange("p a (t h d) -> p (a t) h d", h=H, d=D),
                                  rowb[:, 0, :].rearrange("p (h d) -> p h d", d=D).unsqueeze(1)
                                  .to_broadcast([P, TPC, H, D]), ALU.add).then_inc(v_ready, 1)

            def maxima(b, h):
                dve.wait_ge(rows_psum, b * H + h + 1)
                dve.tensor_reduce(mx[:, :, h], ps1[h % 2][:], AX.X, ALU.max, negate=True).then_inc(rows_maxed, 1)

            def split_max(b, s):
                dve.wait_ge(maxT_psum, b + 1)
                src = psm[0:2 * H, 0:P]
                step.then(dve.tensor_copy(mp[s][:, 0], src))
                step.then(dve.tensor_tensor(mr[:, 0], src, mp[s][:, 0], ALU.subtract))
                step.then(dve.tensor_copy(mp[s][:, 1], mr[:, 0]))
                dve.tensor_tensor(mp[s][:, 2], mr[:, 0], mp[s][:, 1], ALU.subtract).then_inc(maxT_ready, 1)

            def normalise(b, q):
                dve.wait_ge(ot_psum, 2 * b + q + 1)
                src = pst[:].rearrange("p g t (h c) -> p g t h c", c=32)
                dve.reciprocal(rden[:, q], src[:, :, :, :, D]).then_inc(den_ready, 1)
                dve.wait_ge(den_ready, 2 * b + q + 1)
                for g in range(2):
                    m = dve.tensor_tensor(
                        O[:].rearrange("p t (g h d) -> p g t h d", g=4, d=D)[:, 2 * q + g],
                        src[:, g, :, :, 0:D], rden[:, q, g].unsqueeze(3).to_broadcast([P, TPB, 4, D]), ALU.mult)
                m.then_inc(o_ready, 1)

            def transposed(b):
                dve.wait_ge(oT_psum, b + 1)
                dve.tensor_copy(OT[:], psm[:, 0:S]).then_inc(oT_ready, 1)

            def project(b):
                dve.wait_ge(y_psum, b + 1)
                dve.tensor_tensor(Y[:, bass.ds(b * TPB, TPB)],
                                  psm[:, S:2 * S].rearrange("p (t e) -> p t e", e=E),
                                  rowb[:, 1:2, :].to_broadcast([P, TPB, E]), ALU.add).then_inc(y_ready, 1)

            for h in range(H):
                maxima(0, h)
            split_max(0, 0)
            first = step.n

            def one(b, s, previous=True, ahead=True):
                step.n = first + b * 3
                head = 0
                for h in range(H):
                    for _ in range(AHEAD[h] if ahead else 0):
                        maxima(b + 1, head)
                        head += 1
                    if previous and h == 1:
                        normalise(b - 1, 1)
                    if previous and h == 5:
                        transposed(b - 1)
                    if previous and h == 8:
                        project(b - 1)
                    if h == 13:
                        normalise(b, 0)
                    if h == 14 and ahead:
                        split_max(b + 1, 1 - s)

            one(0, 0, previous=False)
            one(1, 1)
            with dve.Fori(1, NB // 2 - 1) as i:
                for s in range(2):
                    one(2 * i + s, s)
            one(NB - 2, 0)
            one(NB - 1, 1, ahead=False)
            normalise(NB - 1, 1)
            transposed(NB - 1)
            project(NB - 1)
            step.n = first + (NB - 1) * 3
            dve.wait_ge(y_ready, NB)
            for c in range(NCH):
                norms.statistics(dve, step, 1, c, Y)
            norms.residual(dve, step, 1, Y, X, x_done)

        @block.tensor
        def _(pe):
            pe.wait_ge(loaded, 16 * NLOAD)
            for c in range(NCH):
                pe.wait_ge(normed, c + 1)
                for j in range(TPC):
                    t = pe.transpose(wide[c][:, j * P:(j + 1) * P], Hn[:, c * TPC + j, :], ident[:])
                t.then_inc(hT_psum, 1)
            for c in range(NCH):
                at = slice(c * CH, (c + 1) * CH)
                pe.wait_ge(hT_ready, NCH if c == 0 else c + 1)
                if c >= 2:
                    pe.wait_ge(qk_ready, 2 * (c - 1))
                for n in range(2):
                    pe.matmul((qbank, kbank)[n][c % 2], w[:, n, :], hT[:, at],
                              start=True, stop=True).then_inc(qk_psum, 1)
                if c >= 2:
                    pe.wait_ge(v_ready, c - 1)
                for j in range(TPC):
                    v = pe.matmul(ps1[c % 2][:].rearrange("p a b -> p (a b)")[:, j * P:(j + 1) * P],
                                  hT[:, (c * TPC + j) * P:(c * TPC + j + 1) * P], w[:, 2, :], start=True, stop=True)
                v.then_inc(v_psum, 1)
                pe.wait_ge(qk_ready, 2 * c + 1)
                if c >= 1:
                    pe.wait_ge(qj_ready, c)
                pe.matmul(psm[:], w[:, 4, :], TQ[:, at], start=True, stop=True).then_inc(qj_psum, 1)

            def by_rows(b, s, h):
                if not (isinstance(b, int) and b == 0 and h < 2):
                    pe.wait_ge(rows_maxed, b * H + h - 1)
                for it in range(TPB):
                    m = pe.matmul(ps1[h % 2][:, it], QS[s][0:KROWS, h, it * P:(it + 1) * P],
                                  KS[s][0:KROWS, h, :], start=True, stop=True)
                m.then_inc(rows_psum, 1)

            def by_columns(b, s, h, first=False):
                if not (first and h < 2):
                    pe.wait_ge(exp_ready, b * H + h - 1)
                for jt in range(TPB):
                    m = pe.matmul(ps2[h % 2][:, jt], KS[s][:, h, jt * P:(jt + 1) * P], QS[s][:, h, :],
                                  start=True, stop=True)
                m.then_inc(cols_psum, 1)

            def pv(b, s, g, first=False):
                pe.wait_ge(exp_ready, b * H + 4 * g + 4)
                if g % 2 == 0 and not first:
                    pe.wait_ge(ou_ready, 2 * b + g // 2 - 1)
                for jt in range(TPB):
                    for k in range(4):
                        m = pe.matmul(pso[g // 2][32 * k:32 * k + 32, g % 2, :], Vb[:, s, jt, 4 * g + k, :],
                                      PT[:, (4 * g + k) % RING, jt, :], start=(jt == 0), stop=(jt == TPB - 1))
                m.then_inc(pv_done, 1)

            def max_transposed():
                pe.transpose(psm[0:2 * H, 0:P], mx[:].rearrange("p t h -> p (t h)"), ident[:]).then_inc(maxT_psum, 1)

            def to_rows(b, q, first=False):
                pe.wait_ge(ou_ready, 2 * b + q + 1)
                if not first:
                    pe.wait_ge(o_ready, 2 * b + q)
                for g in range(2):
                    for it in range(TPB):
                        m = pe.transpose(pst[:, g, it, :], OU[:, q, g, it * P:(it + 1) * P], ident[:])
                m.then_inc(ot_psum, 1)

            def o_transposed(b):
                pe.wait_ge(o_ready, 2 * b + 2)
                for it in range(TPB):
                    m = pe.transpose(psm[:, it * P:(it + 1) * P], O[:, it, :], ident[:])
                m.then_inc(oT_psum, 1)

            def project(b):
                pe.wait_ge(oT_ready, b + 1)
                for it in range(TPB):
                    m = pe.matmul(psm[:, S + it * P:S + (it + 1) * P], OT[:, it * P:(it + 1) * P], w[:, 3, :],
                                  start=True, stop=True)
                m.then_inc(y_psum, 1)

            pe.wait_ge(v_ready, NCH)
            pe.wait_ge(qj_ready, NCH)
            pe.wait_ge(qk_ready, 2 * NCH)
            pe.wait_ge(stack_ready[0], 16 * 6)
            for h in range(H):
                by_rows(0, 0, h)
            pe.wait_ge(rows_maxed, H)
            max_transposed()

            def one(b, s, k, previous=True, ahead=True):
                first = not previous
                pe.wait_ge(k_ones, 2)
                pe.wait_ge(max_rows[s], 16 * PARTS * TPB * (k + 1))
                pe.wait_ge(vb_ready, b + 1)
                if ahead:
                    pe.wait_ge(maxT_ready, b + 1)
                head = 0
                for h in range(H):
                    by_columns(b, s, h, first)
                    if ahead and AHEAD[h] and head == 0:
                        pe.wait_ge(stack_ready[1 - s], 16 * 6 * (k + 1 + s))
                    for _ in range(AHEAD[h] if ahead else 0):
                        by_rows(b + 1, 1 - s, head)
                        head += 1
                    if previous and h == 1:
                        to_rows(b - 1, 1)
                    if previous and h == 5:
                        o_transposed(b - 1)
                    if previous and h == 8:
                        project(b - 1)
                    if h in (5, 9, 13):
                        pv(b, s, (h - 5) // 4, first)
                    if h == 13:
                        to_rows(b, 0, first)
                    if h == 14 and ahead:
                        pe.wait_ge(rows_maxed, (b + 2) * H)
                        if previous:
                            pe.wait_ge(y_ready, b)
                        max_transposed()
                pv(b, s, 3, first)

            one(0, 0, 0, previous=False)
            one(1, 1, 0)
            with pe.Fori(1, NB // 2 - 1) as i:
                for s in range(2):
                    one(2 * i + s, s, i)
            one(NB - 2, 0, NB // 2 - 1)
            one(NB - 1, 1, NB // 2 - 1, ahead=False)
            to_rows(NB - 1, 1)
            o_transposed(NB - 1)
            project(NB - 1)


NE, TOPK, CAP, FF = 64, 8, 160, 384
FT = FF // P
GE = 4
NG = NE // GE
AHEAD_G = 4
GC = GE * CAP // P
GR = GE * CAP
NSLOT = NE * CAP
ROWW = E + NE
NZ = TOK * TOPK
ROUNDS = CAP // 8
FEPS = 1.1920928955078125e-07


def load_group(eng, io, g, W1, W2, loaded):
    eng.dma_start(W1[:], io["w1T"][bass.ds(g, 1)].rearrange("g h e f -> (g h) e f")).then_inc(loaded, 16)
    eng.dma_start(W2[:], io["w2T"][bass.ds(g, 1)].rearrange("g p e j h -> (g p) e j h")).then_inc(loaded, 16)


def route(nc, io, X, ident, rows, slots, tab, ST, W1, W2):
    with ExitStack() as ctx:
        def sb(name, shape, dt=F32):
            return ctx.enter_context(nc.sbuf_tensor("r_" + name, shape, dt))

        def psum(name, shape, dt=F32):
            return ctx.enter_context(nc.psum_tensor("r_" + name, shape, dt))

        sem = ctx.enter_context(semaphores(nc, "r_"))

        Hn = sb("hn", [P, NT, E])
        hT = sb("hT", [P, TOK])
        wg = sb("wg", [P, NE])
        w1, w2 = sb("w1", [P, 2 * FF]), sb("w2", [P, FT, E])
        G, R, M, C = (sb(n, [P, NT, NE]) for n in ("g", "r", "m", "c"))
        Wt = sb("wt", [P, NT, NE])
        top = sb("top", [P, NT, TOPK])
        small = sb("small", [P, 4, NT])
        basei, base = sb("basei", [P, NT], I32), sb("base", [P, NT])
        key = sb("key", [P, NT // 2, 2, NE])
        keyT = sb("keyT", [P, TOK // 2])
        m8 = sb("m8", [P, 8])
        lists = sb("lists", [P, CAP])
        both, final = sb("both", [NE, 2 * CAP]), sb("final", [NE, CAP])
        flat_slots = sb("flat", [NSLOT // P, P])
        dest = sb("dest", [P, NG, GC])
        sg = sb("sg", [P, FT, CH])
        act_in = sb("act_in", [P, 2, FT, CH])

        pl = psum("pl", [P, NT, NE])
        pt = [psum(f"pt{i}", [P, CH]) for i in range(2)]
        pu = [psum(f"pu{i}", [P, CH]) for i in range(3)]
        pd = psum("pd", [P, CH])

        loaded, prefetched = sem("loaded"), sem("prefetched")
        norms, normed = Norms(sb, sem, 1), sem("normed")
        hT_psum, hT_ready = sem("hT_psum"), sem("hT_ready")
        logits_psum, centred, exp_ready = sem("logits_psum"), sem("centred"), sem("exp_ready")
        base_ready = sem("base_ready")
        key_ready, keyT_psum = sem("key_ready"), sem("keyT_psum")
        half_lists, both_ready = sem("half_lists"), sem("both_ready")
        final_ready, slots_out, slots_in, slots_psum = (
            sem("final_ready"), sem("slots_out"), sem("slots_in"), sem("slots_psum"))
        weights_ready, rows_out = sem("weights_ready"), sem("rows_out")
        up_psum, up_read, gated, down_psum, down_read = (
            sem("up_psum"), sem("up_read"), sem("gated"), sem("down_psum"), sem("down_read"))
        dve_step, pool_step = sem("dve_step"), sem("pool_step")

        block = ctx.enter_context(nc.Block())

        @block.sync
        def _(sp):
            for dst, src in ((wg, "wgT"), (w1, "sw1T")):
                sp.dma_start(dst[:], io[src]).then_inc(loaded, 16)
            sp.dma_start(w2[:], io["sw2T"]).then_inc(loaded, 16)
            for g in range(2):
                load_group(sp, io, g, W1[g], W2[g], prefetched)
            out = rows.rearrange("(t p) c -> p t c", p=P)
            sp.wait_ge(normed, NCH)
            sp.dma_start(out[:, :, 0:E], Hn[:]).then_inc(rows_out, 16)
            sp.wait_ge(weights_ready, 1)
            sp.dma_start(out[:, :, E:ROWW], Wt[:]).then_inc(rows_out, 16)
            sp.wait_ge(half_lists, 1)
            for i in range(2):
                sp.dma_start(both[:, i * CAP:(i + 1) * CAP], lists[i * NE:(i + 1) * NE, :]).then_inc(both_ready, 16)
            sp.wait_ge(final_ready, 1)
            sp.dma_start(slots.rearrange("(e c) -> e c", c=CAP), final[:]).then_inc(slots_out, 16)
            sp.wait_ge(slots_out, 16)
            sp.dma_start(flat_slots[:], slots.rearrange("(n p) -> n p", p=P)).then_inc(slots_in, 16)
            sp.wait_ge(rows_out, 32)
            sp.wait_ge(slots_in, 16)
            sp.wait_ge(prefetched, 64)

        @block.gpsimd
        def _(pool):
            step = Steps(pool, pool_step)
            norms.prepare(pool)
            step.then(pool.iota(basei[:], pattern=[[8 - 8 * P, NT]], base=NZ + 1, channel_multiplier=-8))
            pool.tensor_copy(base[:], basei[:]).then_inc(base_ready, 1)
            norms.roots(pool, step, 0)

        @block.scalar
        def _(act):
            for c in range(NCH):
                act.wait_ge(hT_psum, c + 1)
                act.activation(hT[:, c * CH:(c + 1) * CH], pt[c % 2][:], ACT.Copy).then_inc(hT_ready, 1)
            act.wait_ge(centred, 1)
            act.activation(R[:], G[:], ACT.Exp).then_inc(exp_ready, 1)
            for c in range(NCH):
                for j in range(FT):
                    n = c * FT + j
                    act.wait_ge(up_psum, 2 * n + 1)
                    if n:
                        act.wait_ge(gated, n)
                    act.activation(sg[:, 0, :], pu[2 * n % 3][:], ACT.Silu).then_inc(up_read, 1)
                act.wait_ge(down_psum, c + 1)
                act.activation(ST[:, c * CH:(c + 1) * CH], pd[:], ACT.Copy).then_inc(down_read, 1)

        @block.vector
        def _(dve):
            v = dve
            step = Steps(dve, dve_step)
            norms.rows(dve, step, 0, X, Hn, normed)
            dve.wait_ge(logits_psum, 1)
            step.then(v.tensor_reduce(small[:, 0], pl[:], AX.X, ALU.max))
            v.tensor_tensor(G[:], pl[:], per_row(small[:, 0], NE), ALU.subtract).then_inc(centred, 1)
            dve.wait_ge(exp_ready, 1)
            step.then(v.tensor_reduce(small[:, 1], R[:], AX.X, ALU.add))
            step.then(v.reciprocal(small[:, 2], small[:, 1]))
            step.then(v.tensor_tensor(G[:], R[:], per_row(small[:, 2], NE), ALU.mult))
            for t in range(NT):
                step(v.max(top[:, t, :], G[:, t, :]))
            step.wait()
            for t in range(NT):
                step(v.match_replace(R[:, t, :], top[:, t, :], G[:, t, :], -1.0))
            step(v.tensor_reduce(small[:, 0], top[:], AX.X, ALU.add))
            step.wait()
            step(v.tensor_scalar(M[:], R[:], 0.0, None, ALU.is_lt))
            step.then(v.tensor_scalar(small[:, 1], small[:, 0], FEPS, None, ALU.max))
            step(v.reciprocal(small[:, 2], small[:, 1]))
            step(v.tensor_tensor(Wt[:], G[:], M[:], ALU.mult))
            step.then(v.memset(R[:], 1.0))
            v.tensor_tensor(Wt[:], Wt[:], per_row(small[:, 2], NE), ALU.mult).then_inc(weights_ready, 1)
            flat = "p t e -> p (t e)"
            step.then(v.tensor_tensor_scan(C[:].rearrange(flat), R[:].rearrange(flat), M[:].rearrange(flat),
                                           0.0, ALU.mult, ALU.add))
            dve.wait_ge(base_ready, 1)
            step.then(v.tensor_tensor(C[:], per_row(base[:], NE), C[:], ALU.subtract))
            v.tensor_tensor(key[:].rearrange("p j h e -> p h j e"), C[:].rearrange("p (h j) e -> p h j e", h=2),
                            M[:].rearrange("p (h j) e -> p h j e", h=2), ALU.mult).then_inc(key_ready, 1)
            dve.wait_ge(keyT_psum, 1)
            step.then(v.tensor_copy(keyT[:], pl[:].rearrange(flat)))

            def largest(src, dst):
                first = step.n
                with dve.Fori(0, ROUNDS) as i:
                    step.n = first + 3 * i
                    step.then(v.max(m8[0:src.shape[0]], src))
                    step(v.tensor_copy(dst[:, bass.ds(8 * i, 8)], m8[0:src.shape[0]]))
                    step.then(v.match_replace(src, m8[0:src.shape[0]], src, 0.0))
                step.n = first + 3 * ROUNDS

            largest(keyT[:], lists)
            dve.nop().then_inc(half_lists, 1)
            for n in range(NCH * FT):
                dve.wait_ge(up_read, n + 1)
                v.tensor_tensor(act_in[:, (n // FT) % 2, n % FT, :], sg[:, 0, :], pu[(2 * n + 1) % 3][:],
                                ALU.mult).then_inc(gated, 1)
            dve.wait_ge(both_ready, 32)
            largest(both[:], final)
            dve.nop().then_inc(final_ready, 1)
            dve.wait_ge(slots_psum, 1)
            keys = pd[:, 0:NG * GC].rearrange("p (g c) -> p g c", c=GC)
            step.then(v.tensor_scalar(dest[:], keys, -1.0, float(NZ), ALU.mult, ALU.add))
            step(v.tensor_copy(tab[:, :, 1, :], dest[:]))
            step.wait()
            step.then(v.tensor_scalar(dest[:], dest[:], float(NZ - 1), None, ALU.min))
            step.then(v.tensor_copy(tab[:, :, 0, :], dest[:]))
            step.then(v.tensor_single_scalar(tab[:, :, 0, :], tab[:, :, 0, :], 3, ALU.logical_shift_right))

        @block.tensor
        def _(pe):
            pe.wait_ge(loaded, 16 * 3)
            for c in range(NCH):
                pe.wait_ge(normed, c + 1)
                if c >= 2:
                    pe.wait_ge(hT_ready, c - 1)
                for j in range(TPC):
                    t = pe.transpose(pt[c % 2][:, j * P:(j + 1) * P], Hn[:, c * TPC + j, :], ident[:])
                t.then_inc(hT_psum, 1)
            pe.wait_ge(hT_ready, NCH)
            for t in range(NT):
                m = pe.matmul(pl[:, t, :], hT[:, t * P:(t + 1) * P], wg[:], start=True, stop=True)
            m.then_inc(logits_psum, 1)
            pe.wait_ge(key_ready, 1)
            flat = pl[:].rearrange("p t e -> p (t e)")
            for j in range(NT // 2):
                m = pe.transpose(flat[:, j * P:(j + 1) * P], key[:, j].rearrange("p h e -> p (h e)"), ident[:])
            m.then_inc(keyT_psum, 1)
            for c in range(NCH):
                at = slice(c * CH, (c + 1) * CH)
                for j in range(FT):
                    n = c * FT + j
                    if n:
                        pe.wait_ge(gated, n)
                    pe.matmul(pu[2 * n % 3][:], w1[:, FF + j * P:FF + (j + 1) * P], hT[:, at],
                              start=True, stop=True)
                    pe.matmul(pu[(2 * n + 1) % 3][:], w1[:, j * P:(j + 1) * P], hT[:, at],
                              start=True, stop=True).then_inc(up_psum, 2)
                pe.wait_ge(gated, (c + 1) * FT)
                if c:
                    pe.wait_ge(down_read, c)
                for j in range(FT):
                    m = pe.matmul(pd[:], w2[:, j, :], act_in[:, c % 2, j, :], start=(j == 0), stop=(j == FT - 1))
                m.then_inc(down_psum, 1)
            pe.wait_ge(down_read, NCH)
            pe.wait_ge(slots_in, 16)
            pe.transpose(pd[:, 0:NSLOT // P], flat_slots[:], ident[0:NSLOT // P, 0:NSLOT // P]).then_inc(slots_psum, 1)


def experts(nc, io, ident, rows, results, tab, W1, W2):
    with ExitStack() as ctx:
        def sb(name, shape, dt=F32):
            return ctx.enter_context(nc.sbuf_tensor("e_" + name, shape, dt))

        def psum(name, shape, dt=F32):
            return ctx.enter_context(nc.psum_tensor("e_" + name, shape, dt))

        sem = ctx.enter_context(semaphores(nc, "e_"))

        idx = [sb(f"idx{i}", [P, 2, GC], I32) for i in range(AHEAD_G)]
        G = [sb(f"g{i}", [P, GC, ROWW]) for i in range(AHEAD_G)]
        GT = [sb(f"gt{i}", [P, GR]) for i in range(2)]
        own = sb("own", [P, GC, GE])
        wsel = sb("wsel", [P, GC, GE])
        wrow = [sb(f"wrow{i}", [P, GC]) for i in range(2)]
        silu = sb("silu", [P, 2, FT, CAP])
        A = sb("a", [P, 2, FT, CAP])
        D_ = sb("d", [P, GR])
        out = [sb(f"out{i}", [P, GC, E]) for i in range(2)]

        px1 = [psum(f"px1_{i}", [P, FT, CAP]) for i in range(2)]
        px2 = [psum(f"px2_{i}", [P, FT, CAP]) for i in range(2)]
        pd = [psum(f"pd{i}", [P, 2, CAP]) for i in range(2)]
        pt = psum("pt", [P, 8, P])

        loaded = [sem("loaded0"), sem("loaded1")]
        own_ready = sem("own_ready")
        idx_ready, weighed = sem("idx_ready"), sem("weighed")
        gathered = [sem(f"gathered{i}") for i in range(AHEAD_G)]
        in_psum, in_ready = sem("in_psum"), sem("in_ready")
        up_psum, silu_ready, gated, down_psum, down_ready = (
            sem("up_psum"), sem("silu_ready"), sem("gated"), sem("down_psum"), sem("down_ready"))
        out_psum, out_ready, scattered = sem("out_psum"), sem("out_ready"), [sem("scattered0"), sem("scattered1")]
        dve_step, pool_passes = sem("dve_step"), sem("pool_passes")

        block = ctx.enter_context(nc.Block())

        def groups(eng, one):
            for g in range(AHEAD_G):
                one(g, g, 0)
            with eng.Fori(1, NG // AHEAD_G - 1) as i:
                for s in range(AHEAD_G):
                    one(AHEAD_G * i + s, s, i)
            for g in range(NG - AHEAD_G, NG):
                one(g, g % AHEAD_G, g // AHEAD_G)

        @block.sync
        def _(sp):
            sp.dma_start(own[:], io["own"]).then_inc(own_ready, 16)
            with sp.Fori(0, NG // 2 - 1) as i:
                for s in range(2):
                    sp.wait_ge(down_psum, GE * (2 * i + s + 1))
                    load_group(sp, io, 2 * i + s + 2, W1[s], W2[s], loaded[s])

        @block.gpsimd
        def _(pool):
            def gather(g, s, k):
                if not isinstance(g, int) or g >= AHEAD_G:
                    pool.wait_ge(in_psum, g - AHEAD_G + 1)
                    pool.wait_ge(weighed, g - AHEAD_G + 1)
                    pool.wait_ge(scattered[s % 2], 16 * GC * (2 * k + s // 2 - 1))
                pool.tensor_copy(idx[s][:], tab[:, bass.ds(g, 1)].rearrange("p g a c -> p (g a) c")
                                 ).then_inc(idx_ready, 1)
                pool.wait_ge(idx_ready, g + 1)
                pool.sem_inc(pool_passes, 1)
                for c in range(GC):
                    pool.indirect_dma_start(G[s][:, c, :], None, rows,
                                            bass.IndirectOffsetOnAxis(ap=idx[s][:, 0, c:c + 1], axis=0)
                                            ).then_inc(gathered[s], 16)

            def scatter(g, s):
                pool.wait_ge(out_ready, g + 1)
                pool.sem_inc(pool_passes, 1)
                for c in range(GC):
                    pool.indirect_dma_start(results, bass.IndirectOffsetOnAxis(ap=idx[s][:, 1, c:c + 1], axis=0),
                                            out[s % 2][:, c, :], None, bounds_check=NZ - 1, oob_is_err=False
                                            ).then_inc(scattered[s % 2], 16)

            for g in range(AHEAD_G - 1):
                gather(g, g, 0)

            def one(g, s, k):
                if not isinstance(g, int) or g + AHEAD_G - 1 < NG:
                    gather(g + AHEAD_G - 1, (s + AHEAD_G - 1) % AHEAD_G, k + (s + AHEAD_G - 1) // AHEAD_G)
                scatter(g, s)

            groups(pool, one)
            for s in range(2):
                pool.wait_ge(scattered[s], 16 * GC * NG // 2)

        @block.scalar
        def _(act):
            def turned(g, s):
                act.wait_ge(in_psum, g + 1)
                act.activation(GT[s % 2][:], pt[:, 0:GC].rearrange("p c r -> p (c r)"), ACT.Copy).then_inc(in_ready, 1)

            def silus(g, e, first):
                n = GE * g + e
                act.wait_ge(up_psum, n + 1)
                if not (first and e < 2):
                    act.wait_ge(gated, n - 1)
                act.activation(silu[:, e % 2], px2[e % 2][:], ACT.Silu).then_inc(silu_ready, 1)

            def downs(g, j, first):
                act.wait_ge(down_psum, GE * g + 2 * j + 2)
                if not first:
                    act.wait_ge(out_psum, g)
                act.activation(D_[:, 2 * j * CAP:(2 * j + 2) * CAP], pd[j][:].rearrange("p e c -> p (e c)"),
                               ACT.Copy).then_inc(down_ready, 1)

            turned(0, 0)
            silus(0, 0, True)

            def one(g, s, k):
                first, last = isinstance(g, int) and g == 0, isinstance(g, int) and g == NG - 1
                for e in range(GE):
                    if e == 2 and not last:
                        turned(g + 1, s + 1)
                    if not (last and e == 3):
                        silus(g if e < 3 else g + 1, (e + 1) % GE, first and e < 3)
                    if e == 2:
                        downs(g, 0, first)
                downs(g, 1, first)

            groups(act, one)

        @block.vector
        def _(dve):
            v = dve
            dve.wait_ge(own_ready, 16)

            def gate(g, e, first):
                n = GE * g + e
                dve.wait_ge(silu_ready, n + 1)
                if not (first and e < 2):
                    dve.wait_ge(down_psum, n - 1)
                v.tensor_tensor(A[:, e % 2], px1[e % 2][:], silu[:, e % 2], ALU.mult).then_inc(gated, 1)

            def finish(g, s, k):
                dve.wait_ge(out_psum, g + 1)
                if not (isinstance(g, int) and g < 2):
                    dve.wait_ge(scattered[s % 2], 16 * GC * (2 * k + s // 2))
                v.tensor_tensor(out[s % 2][:], pt[:, 0:GC], per_row(wrow[s % 2][:], E), ALU.mult
                                ).then_inc(out_ready, 1)

            def weigh(g, s, k):
                dve.wait_ge(gathered[s], 16 * GC * (k + 1))
                v.tensor_tensor(wsel[:], G[s][:, :, bass.ds(E + GE * g, GE)], own[:], ALU.mult).then_inc(dve_step, 1)
                dve.wait_ge(dve_step, g + 1)
                v.tensor_reduce(wrow[s % 2][:], wsel[:], AX.X, ALU.add).then_inc(weighed, 1)

            weigh(0, 0, 0)
            gate(0, 0, True)

            def one(g, s, k):
                first, last = isinstance(g, int) and g == 0, isinstance(g, int) and g == NG - 1
                for e in range(GE):
                    if not (last and e == 3):
                        gate(g if e < 3 else g + 1, (e + 1) % GE, first and e < 3)
                    if e == 1 and not first:
                        finish(g - 1, (s - 1) % AHEAD_G, k if s else k - 1)
                    if e == 2 and not last:
                        weigh(g + 1, (s + 1) % AHEAD_G, k + (s + 1) // AHEAD_G)

            groups(dve, one)
            finish(NG - 1, AHEAD_G - 1, NG // AHEAD_G - 1)

        @block.tensor
        def _(pe):
            def turn(g, s, k):
                pe.wait_ge(gathered[s], 16 * GC * (k + 1))
                for c in range(GC):
                    m = pe.transpose(pt[:, c, :], G[s][:, c, 0:E], ident[:])
                m.then_inc(in_psum, 1)

            def up(g, s, k, e, first):
                n, slot = GE * g + e, s % 2
                if e == 0:
                    pe.wait_ge(in_ready, g + 1)
                    if not (isinstance(g, int) and g < 2):
                        pe.wait_ge(loaded[slot], 32 * (2 * k + s // 2))
                if not (first and e < 2):
                    pe.wait_ge(gated, n - 1)
                at = slice(e * CAP, (e + 1) * CAP)
                for j in range(FT):
                    pe.matmul(px2[e % 2][:, j, :], W1[slot][:, e, FF + j * P:FF + (j + 1) * P], GT[slot][:, at],
                              start=True, stop=True)
                for j in range(FT):
                    m = pe.matmul(px1[e % 2][:, j, :], W1[slot][:, e, j * P:(j + 1) * P], GT[slot][:, at],
                                  start=True, stop=True)
                m.then_inc(up_psum, 1)

            def down(g, slot, e, first):
                n = GE * g + e
                pe.wait_ge(gated, n + 1)
                if e % 2 == 0 and not first:
                    pe.wait_ge(down_ready, 2 * g - 1 + e // 2)
                for j in range(FT):
                    m = pe.matmul(pd[e // 2][:, e % 2, :], W2[slot][:, e, j, :], A[:, e % 2, j, :],
                                  start=(j == 0), stop=(j == FT - 1))
                m.then_inc(down_psum, 1)

            def turn_out(g):
                pe.wait_ge(down_ready, 2 * g + 2)
                for c in range(GC):
                    m = pe.transpose(pt[:, c, :], D_[:, c * P:(c + 1) * P], ident[:])
                m.then_inc(out_psum, 1)

            turn(0, 0, 0)
            up(0, 0, 0, 0, True)

            def one(g, s, k):
                first, last = isinstance(g, int) and g == 0, isinstance(g, int) and g == NG - 1
                after = (s + 1) % AHEAD_G, k + (s + 1) // AHEAD_G
                for e in range(GE):
                    if e == 2 and not last:
                        if not first:
                            pe.wait_ge(out_ready, g)
                        turn(g + 1, *after)
                    if not (last and e == 3):
                        if e < 3:
                            up(g, s, k, e + 1, first)
                        else:
                            up(g + 1, *after, 0, False)
                    if e == 1 and not first:
                        pe.wait_ge(in_ready, g + 1)
                        turn_out(g - 1)
                    down(g, s % 2, e, first)

            groups(pe, one)
            turn_out(NG - 1)


def combine(nc, io, X, ident, results, ST):
    with ExitStack() as ctx:
        def sb(name, shape, dt=F32):
            return ctx.enter_context(nc.sbuf_tensor("c_" + name, shape, dt))

        sem = ctx.enter_context(semaphores(nc, "c_"))
        norms = Norms(sb, sem, 1)

        Z = sb("z", [P, 4, TOPK, E])
        Y = sb("y", [P, NT, E])
        ps = [ctx.enter_context(nc.psum_tensor(f"c_ps{i}", [P, TPC, E], F32)) for i in range(NCH)]
        loaded = [sem(f"loaded{i}") for i in range(4)]
        summed, shared_psum = sem("summed"), sem("shared_psum")
        x_done, dve_step, pool_step = sem("x_done"), sem("dve_step"), sem("pool_step")
        block = ctx.enter_context(nc.Block())

        @block.sync
        def _(sp):
            z = results.rearrange("(t p k) e -> t p k e", p=P, k=TOPK)
            for t in range(4):
                sp.dma_start(Z[:, t], z[t]).then_inc(loaded[t], 16)
            with sp.Fori(1, NT // 4) as i:
                for s in range(4):
                    sp.wait_ge(summed, 4 * i + s - 3)
                    sp.dma_start(Z[:, s], z[bass.ds(4 * i + s, 1)].rearrange("t p k e -> (t p) k e")
                                 ).then_inc(loaded[s], 16)

        @block.tensor
        def _(pe):
            for c in range(NCH):
                for j in range(TPC):
                    m = pe.transpose(ps[c][:, j, :], ST[:, (c * TPC + j) * P:(c * TPC + j + 1) * P], ident[:])
                m.then_inc(shared_psum, 1)

        @block.gpsimd
        def _(pool):
            step = Steps(pool, pool_step)
            norms.prepare(pool)
            norms.roots(pool, step, 0)

        @block.vector
        def _(dve):
            step = Steps(dve, dve_step)
            with dve.Fori(0, NT // 4) as i:
                for s in range(4):
                    dve.wait_ge(loaded[s], 16 * (i + 1))
                    dve.tensor_reduce(Y[:, bass.ds(4 * i + s, 1)], Z[:, s].rearrange("p k e -> p e k"),
                                      AX.X, ALU.add).then_inc(summed, 1)
            dve.wait_ge(summed, NT)
            for c in range(NCH):
                dve.wait_ge(shared_psum, c + 1)
                step.then(dve.tensor_tensor(Y[:, c * TPC:(c + 1) * TPC], Y[:, c * TPC:(c + 1) * TPC], ps[c][:], ALU.add))
                norms.statistics(dve, step, 0, c, Y)
            norms.residual(dve, step, 0, Y, X, x_done)


DI, DS, DR, DC = 256, 16, 8, 4
DH = DI // P
PAD = DC - 1
TH = TOK // 2
HB = TH // S
HCH = TH // CH
BCR = 3 * 2 * DS


def mamba(nc, io, X, ident):
    with ExitStack() as ctx:
        def sb(name, shape, dt=F32):
            return ctx.enter_context(nc.sbuf_tensor("m_" + name, shape, dt))

        def psum(name, shape, dt=F32):
            return ctx.enter_context(nc.psum_tensor("m_" + name, shape, dt))

        sem = ctx.enter_context(semaphores(nc, "m_"))

        N1, N2 = sb("n1", [P, NT, E]), sb("n2", [P, NT, E])
        sq, srw = sb("sq", [P, E]), sb("srw", [P, E])
        win = sb("win", [P, 2 * DI])
        wconv = sb("wconv", [P, DC, DI])
        wx = sb("wx", [P, DH, BCR + DR])
        wdt = sb("wdt", [DR, DI])
        wout = sb("wout", [P, DH, E])
        vec = sb("vec", [P, 16])
        alog = sb("alog", [P, DH, DS])
        expA, negA = sb("expa", [P, DH, DS]), sb("nega", [P, DH, DS])
        pick = sb("pick", [BCR, 2 * DS], BF16)
        pickf = sb("pickf", [BCR, 2 * DS])
        diagD = sb("diagd", [P, DH, P])
        gT = sb("gt", [P, NCH, CH])
        hP = sb("hp", [P, NB, PAD + S])
        U, SZ, delta, du = (sb(n, [P, DH, TOK]) for n in ("u", "sz", "delta", "du"))
        dtT = sb("dtT", [DR, TOK])
        BC = sb("bc", [BCR, TOK], BF16)
        rest = sb("rest", [BCR, CH])
        tmp = sb("tmp", [BCR, CH], BF16)
        Bn, Cn = ([sb(f"{n}{i}", [P, TH]) for i in range(2)] for n in ("bn", "cn"))
        dA = [[sb(f"da{i}{h}", [P, HB, S]) for h in range(DH)] for i in range(2)]
        dBu = [[sb(f"dbu{i}{h}", [P, TH]) for h in range(DH)] for i in range(2)]
        hst = [sb(f"h{h}", [P, TH]) for h in range(DH)]
        hC = [[sb(f"hc{i}{h}", [P, TH]) for h in range(DH)] for i in range(2)]

        acc = [psum(f"acc{i}", [P, CH]) for i in range(4)]
        pB, pC = psum("pb", [P, TH]), psum("pc", [P, TH])
        bank = [x[:] for x in acc] + [x[:, c * CH:(c + 1) * CH] for x in (pB, pC) for c in range(HCH)]
        vecs = {"g": 0, "b": 1, "sq_b": 2, "srw_b": 3, "scale": 4, "conv_b": 6, "dt_b": 8, "D": 10}

        def col(name, i=0):
            return vec[:, vecs[name] + i:vecs[name] + i + 1]

        def halves(x):
            return x.rearrange("p (h t) -> p h t", h=DH)

        loaded = sem("loaded")
        norms, n1_ready, n2_ready, x_done = Norms(sb, sem, 3), sem("n1_ready"), sem("n2_ready"), sem("x_done")
        hT_psum, gT_ready, sq_psum, hP_ready = sem("hT_psum"), sem("gT_ready"), sem("sq_psum"), sem("hP_ready")
        padded, taps_ready = sem("padded"), sem("taps_ready")
        u_psum, u_ready, z_psum, z_ready = sem("u_psum"), sem("u_ready"), sem("z_psum"), sem("z_ready")
        dbc_psum, dt_ready, bc_read, bc_ready = sem("dbc_psum"), sem("dt_ready"), sem("bc_read"), sem("bc_ready")
        dl_psum, dl_read, e_ready, ln_ready, delta_ready = (
            sem("dl_psum"), sem("dl_read"), sem("e_ready"), sem("ln_ready"), sem("delta_ready"))
        du_ready, diag_ready, expA_ready, dA_zero = sem("du_ready"), sem("diag_ready"), sem("expA_ready"), sem("dA_zero")
        negA_ready = sem("negA_ready")
        b_psum, c_psum, b_ready, c_ready = sem("b_psum"), sem("c_psum"), sem("b_ready"), sem("c_ready")
        dA_ready, dBu_ready, h_ready, hC_ready, hC_used = (
            sem("dA_ready"), sem("dBu_ready"), sem("h_ready"), sem("hC_ready"), sem("hC_used"))
        y_gated, out_psum, out_ready = sem("y_gated"), sem("out_psum"), sem("out_ready")
        srw_psum, g_ready, tok_psum, tok_read = sem("srw_psum"), sem("g_ready"), sem("tok_psum"), sem("tok_read")
        dve_step, pool_step, act_step = sem("dve_step"), sem("pool_step"), sem("act_step")

        block = ctx.enter_context(nc.Block())
        NLOAD = 20

        def over_states(eng, one):
            one(0, 0)
            one(1, 1)
            with eng.Fori(1, DS // 2 - 1) as i:
                for s in range(2):
                    one(2 * i + s, s)
            one(DS - 2, 0)
            one(DS - 1, 1)

        def over_chunks(u, dbc, dl):
            for c in range(NCH + 2):
                if c < NCH:
                    u(c)
                if 0 < c <= NCH:
                    dbc(c - 1)
                if c > 1:
                    dl(c - 2)

        @block.sync
        def _(sp):
            for dst, src in ((sq, "sq_w"), (srw, "srw_w"), (win, "in_proj_w"), (wdt, "dt_w"), (pickf, "pick")):
                sp.dma_start(dst[:], io[src]).then_inc(loaded, 16)
            sp.dma_start(wx[:], io["x_proj"].rearrange("(h p) c -> p h c", p=P)).then_inc(loaded, 16)
            sp.dma_start(wout[:], io["out_proj_w"].rearrange("(h p) c -> p h c", p=P)).then_inc(loaded, 16)
            sp.dma_start(alog[:], io["A_log"].rearrange("(h p) c -> p h c", p=P)).then_inc(loaded, 16)
            sp.dma_start(wconv[:], io["conv_wT"].unsqueeze(0).to_broadcast([P, DC, DI])).then_inc(loaded, 16)
            for n in ("g", "b", "sq_b", "srw_b"):
                sp.dma_start(col(n), io["m_" + n].unsqueeze(1)).then_inc(loaded, 16)
            sp.dma_start(col("scale"), io["res_scale"].unsqueeze(1).to_broadcast([P, 1])).then_inc(loaded, 16)
            for n in ("conv_b", "dt_b", "D"):
                for h in range(DH):
                    sp.dma_start(col(n, h), io["m_" + n][h * P:(h + 1) * P].unsqueeze(1)).then_inc(loaded, 16)
            sp.wait_ge(loaded, 16 * NLOAD)

        @block.gpsimd
        def _(pool):
            step = Steps(pool, pool_step)
            norms.prepare(pool)
            pool.memset(hP[:, :, 0:PAD], 0.0).then_inc(padded, 1)
            for i in range(2):
                for h in range(DH):
                    pool.memset(dA[i][h][:, :, 0:1], 0.0).then_inc(dA_zero, 1)
            norms.roots(pool, step, 0)
            norms.roots(pool, step, 1)
            pool.wait_ge(loaded, 16 * NLOAD)
            for h in range(DH):
                pool.tensor_scalar(diagD[:, h], ident[:], col("D", h), 1.0, ALU.mult, ALU.mult).then_inc(diag_ready, 1)
            pool.wait_ge(expA_ready, 1)
            pool.tensor_scalar(negA[:], expA[:], -1.0, 1.0, ALU.mult, ALU.mult).then_inc(negA_ready, 1)

            def delta_u(c):
                pool.wait_ge(delta_ready, c + 1)
                at = slice(c * CH, (c + 1) * CH)
                pool.tensor_tensor(du[:, :, at], delta[:, :, at], U[:, :, at], ALU.mult).then_inc(du_ready, 1)

            for c in range(HCH):
                delta_u(c)
            pool.wait_ge(du_ready, HCH)
            for hf in range(2):
                def one(n, s):
                    m = hf * DS + n
                    for h in range(DH):
                        k = m * DH + h
                        pool.wait_ge(b_ready, m + 1)
                        if not (isinstance(m, int) and m < 2):
                            pool.wait_ge(h_ready, k - 2 * DH + 1)
                        pool.tensor_tensor(dBu[s][h][:], du[:, h, hf * TH:(hf + 1) * TH], Bn[s][:], ALU.mult
                                           ).then_inc(dBu_ready, 1)
                    if hf == 0 and isinstance(n, int) and n == 0:
                        for c in range(HCH, NCH):
                            delta_u(c)
                        pool.wait_ge(du_ready, NCH)

                over_states(pool, one)
            norms.roots(pool, step, 2)

        @block.scalar
        def _(act):
            step = Steps(act, act_step)
            act.wait_ge(loaded, 16 * NLOAD)
            step.then(act.activation(pick[:], pickf[:], ACT.Copy))
            for c in range(NCH):
                act.wait_ge(hT_psum, c + 1)
                act.activation(gT[:, c], bank[c % 2], ACT.Identity, bias=col("b"), scale=col("g")
                               ).then_inc(gT_ready, 1)

            def u(c):
                for j in range(DH):
                    act.wait_ge(u_psum, DH * c + j + 1)
                    act.activation(U[:, j, c * CH:(c + 1) * CH], bank[4 + 2 * (c % 2) + j], ACT.Silu,
                                   bias=col("conv_b", j)).then_inc(u_ready, 1)

            def dt(c):
                act.wait_ge(dbc_psum, c + 1)
                act.activation(dtT[:, c * CH:(c + 1) * CH], bank[c % 2][BCR:BCR + DR, :], ACT.Copy
                               ).then_inc(dt_ready, 1)

            def dl(c):
                at = slice(c * CH, (c + 1) * CH)
                for h in range(DH):
                    act.wait_ge(dl_psum, DH * c + h + 1)
                    act.activation(delta[:, h, at], bank[2 + h], ACT.Identity, bias=col("dt_b", h)).then_inc(act_step, 1)
                    act.activation(du[:, h, at], bank[2 + h], ACT.Abs, bias=col("dt_b", h)).then_inc(dl_read, 1)

            over_chunks(u, dt, dl)
            act.wait_ge(dl_read, DH * NCH)
            for c in range(NCH):
                at = slice(c * CH, (c + 1) * CH)
                act.activation(du[:, :, at], du[:, :, at], ACT.Exp, scale=-1.0).then_inc(e_ready, 1)
            act.activation(expA[:], alog[:], ACT.Exp).then_inc(expA_ready, 1)
            for c in range(NCH):
                act.wait_ge(e_ready, c + 1)
                act.activation(halves(hC[c // 2][c % 2][:]), du[:, :, c * CH:(c + 1) * CH], ACT.Ln, bias=1.0
                               ).then_inc(ln_ready, 1)
            for i in range(DH * NCH):
                c, h = i // DH, i % DH
                act.wait_ge(z_psum, i + 1)
                act.activation(SZ[:, h, c * CH:(c + 1) * CH], bank[4 + i % 4], ACT.Silu).then_inc(z_ready, 1)
            act.wait_ge(dA_zero, 2 * DH)
            act.wait_ge(negA_ready, 1)
            for hf in range(2):
                act.wait_ge(delta_ready, HCH * (hf + 1))

                def one(n, s):
                    m = hf * DS + n
                    early = isinstance(m, int) and m < 2
                    act.wait_ge(b_psum, m + 1)
                    if not early:
                        act.wait_ge(dBu_ready, DH * (m - 1))
                    act.activation(Bn[s][:], pB[:], ACT.Copy).then_inc(b_ready, 1)
                    for h in range(DH):
                        k = m * DH + h
                        if not early:
                            act.wait_ge(h_ready, k - 2 * DH + 1)
                        act.activation(dA[s][h][:, :, 1:S],
                                       delta[:, h, hf * TH:(hf + 1) * TH].rearrange("p (b t) -> p b t", t=S)[:, :, 1:S],
                                       ACT.Exp, scale=negA[:, h, bass.ds(n, 1)]).then_inc(dA_ready, 1)
                    act.wait_ge(c_psum, m + 1)
                    if not early:
                        act.wait_ge(hC_ready, DH * (m - 1))
                    act.activation(Cn[s][:], pC[:], ACT.Copy).then_inc(c_ready, 1)

                over_states(act, one)
            for c in range(NCH):
                act.wait_ge(out_psum, c + 1)
                act.activation(gT[:, c], bank[c], ACT.Copy).then_inc(out_ready, 1)

        @block.vector
        def _(dve):
            v = dve
            step = Steps(dve, dve_step)
            norms.rows(dve, step, 0, X, N1, n1_ready)
            for c in range(NCH):
                dve.wait_ge(n1_ready, c + 1)
                norms.statistics(dve, step, 1, c, N1)
            for c in range(NCH):
                norms.apply(dve, 1, c, N1, N2).then_inc(n2_ready, 1)
            dve.wait_ge(loaded, 16 * NLOAD)
            v.tensor_tensor(wconv[:], wconv[:], win[:, 0:DI].unsqueeze(1).to_broadcast([P, DC, DI]), ALU.mult
                            ).then_inc(taps_ready, 1)
            for c in range(NCH):
                dve.wait_ge(sq_psum, c + 1)
                dve.wait_ge(padded, 1)
                v.scalar_tensor_tensor(hP[:, 2 * c:2 * c + 2, PAD:PAD + S],
                                       bank[2 + c % 2].rearrange("p (b t) -> p b t", t=S), col("sq_b"),
                                       gT[:, c].rearrange("p (b t) -> p b t", t=S), ALU.add, ALU.add
                                       ).then_inc(hP_ready, 1)
            for c in range(NCH):
                at = slice(c * CH, (c + 1) * CH)
                dve.wait_ge(dbc_psum, c + 1)
                dve.wait_ge(dt_ready, c + 1)
                step.then(v.tensor_copy(BC[:, at], bank[c % 2][0:BCR, :]))
                v.tensor_tensor(rest[:], bank[c % 2][0:BCR, :], BC[:, at], ALU.subtract).then_inc(bc_read, 1)
                dve.wait_ge(bc_read, c + 1)
                step(v.tensor_copy(BC[32:64, at], rest[32:64, :]))
                step.then(v.tensor_copy(tmp[64:96, :], rest[64:96, :]))
                v.tensor_tensor(BC[64:96, at], rest[64:96, :], tmp[64:96, :], ALU.subtract).then_inc(bc_ready, 1)
                dve.wait_ge(bc_ready, c + 1)
            for c in range(NCH):
                at = slice(c * CH, (c + 1) * CH)
                dve.wait_ge(e_ready, c + 1)
                lost = halves(hst[c % 2][:])
                step.then(v.tensor_scalar(lost, du[:, :, at], 1.0, -1.0, ALU.add, ALU.add))
                step.then(v.tensor_tensor(lost, du[:, :, at], lost, ALU.subtract))
                dve.wait_ge(ln_ready, c + 1)
                step.then(v.tensor_tensor(lost, lost, halves(hC[c // 2][c % 2][:]), ALU.add))
                v.scalar_tensor_tensor(delta[:, :, at], delta[:, :, at], 0.0, lost, ALU.max, ALU.add
                                       ).then_inc(delta_ready, 1)
                dve.wait_ge(delta_ready, c + 1)
            for hf in range(2):
                def one(n, s):
                    m = hf * DS + n
                    early = isinstance(m, int) and m < 2
                    for h in range(DH):
                        k = m * DH + h
                        dve.wait_ge(dA_ready, k + 1)
                        dve.wait_ge(dBu_ready, k + 1)
                        if not (isinstance(m, int) and m < 1):
                            dve.wait_ge(hC_ready, k - DH + 1)
                        v.tensor_tensor_scan(hst[h][:], dA[s][h][:].rearrange("p b t -> p (b t)"), dBu[s][h][:], 0.0,
                                             ALU.mult, ALU.add).then_inc(h_ready, 1)
                    for h in range(DH):
                        k = m * DH + h
                        dve.wait_ge(h_ready, k + 1)
                        dve.wait_ge(c_ready, m + 1)
                        if not early:
                            dve.wait_ge(hC_used, k - 2 * DH + 1)
                        v.tensor_tensor(hC[s][h][:], hst[h][:], Cn[s][:], ALU.mult).then_inc(hC_ready, 1)

                over_states(dve, one)
                dve.wait_ge(hC_used, DS * DH * (hf + 1))
                dve.wait_ge(z_ready, DH * NCH)
                for h in range(DH):
                    for c in range(HCH):
                        at = slice(hf * TH + c * CH, hf * TH + (c + 1) * CH)
                        v.tensor_tensor(SZ[:, h, at], SZ[:, h, at], acc[2 * h + c][:], ALU.mult).then_inc(y_gated, 1)

            def gate(c):
                dve.wait_ge(srw_psum, c + 1)
                v.scalar_tensor_tensor(U[:, 0, c * CH:(c + 1) * CH], bank[4 + c], col("srw_b"), gT[:, c],
                                       ALU.add, ALU.mult).then_inc(g_ready, 1)

            gate(0)
            for c in range(NCH):
                if c + 1 < NCH:
                    gate(c + 1)
                at = slice(c * TPC, (c + 1) * TPC)
                dve.wait_ge(tok_psum, c + 1)
                v.scalar_tensor_tensor(N2[:, at], bank[c].rearrange("p (t e) -> p t e", e=E), col("scale"), N1[:, at],
                                       ALU.mult, ALU.add).then_inc(tok_read, 1)
                dve.wait_ge(tok_read, c + 1)
                norms.statistics(dve, step, 2, c, N2)
            norms.residual(dve, step, 2, N2, X, x_done)

        @block.tensor
        def _(pe):
            pe.wait_ge(loaded, 16 * NLOAD)

            def turn(c):
                pe.wait_ge(n2_ready, c + 1)
                if c > 1:
                    pe.wait_ge(gT_ready, c - 1)
                for j in range(TPC):
                    m = pe.transpose(bank[c % 2][:, j * P:(j + 1) * P], N2[:, c * TPC + j, :], ident[:])
                m.then_inc(hT_psum, 1)

            turn(0)
            for c in range(NCH):
                if c + 1 < NCH:
                    turn(c + 1)
                pe.wait_ge(gT_ready, c + 1)
                if c > 1:
                    pe.wait_ge(hP_ready, c - 1)
                pe.matmul(bank[2 + c % 2], sq[:], gT[:, c], start=True, stop=True).then_inc(sq_psum, 1)
            pe.wait_ge(taps_ready, 1)

            def u(c):
                pe.wait_ge(hP_ready, c + 1)
                for j in range(DH):
                    if c > 1:
                        pe.wait_ge(u_ready, DH * (c - 2) + j + 1)
                    for k in range(DC):
                        m = pe.matmul(bank[4 + 2 * (c % 2) + j].rearrange("p (b t) -> p b t", t=S),
                                      wconv[:, k, j * P:(j + 1) * P], hP[:, 2 * c:2 * c + 2, k:k + S],
                                      start=(k == 0), stop=(k == DC - 1))
                    m.then_inc(u_psum, 1)

            def dbc(c):
                pe.wait_ge(u_ready, DH * (c + 1))
                pe.wait_ge(gT_ready, NCH)
                if c > 1:
                    pe.wait_ge(bc_read, c - 1)
                for h in range(DH):
                    m = pe.matmul(bank[c % 2][0:BCR + DR, :], wx[:, h, :], U[:, h, c * CH:(c + 1) * CH],
                                  start=(h == 0), stop=(h == DH - 1))
                m.then_inc(dbc_psum, 1)

            def dl(c):
                pe.wait_ge(dt_ready, c + 1)
                pe.wait_ge(hP_ready, NCH)
                for h in range(DH):
                    if c:
                        pe.wait_ge(dl_read, DH * (c - 1) + h + 1)
                    pe.matmul(bank[2 + h], wdt[:, h * P:(h + 1) * P], dtT[:, c * CH:(c + 1) * CH],
                              start=True, stop=True).then_inc(dl_psum, 1)

            over_chunks(u, dbc, dl)
            pe.wait_ge(u_ready, DH * NCH)
            for i in range(DH * NCH):
                c, h = i // DH, i % DH
                if i > 3:
                    pe.wait_ge(z_ready, i - 3)
                pe.matmul(bank[4 + i % 4].rearrange("p (b t) -> p b t", t=S), win[:, DI + h * P:DI + (h + 1) * P],
                          hP[:, 2 * c:2 * c + 2, PAD:PAD + S], start=True, stop=True).then_inc(z_psum, 1)
            pe.wait_ge(bc_ready, NCH)
            pe.wait_ge(dl_read, DH * NCH)
            pe.wait_ge(diag_ready, DH)
            pe.wait_ge(z_ready, DH * NCH)
            for hf in range(2):
                def spread(n, hf=hf):
                    m = hf * DS + n
                    for p, row, read, done in ((pB, 0, b_ready, b_psum), (pC, DS, c_ready, c_psum)):
                        if not (isinstance(m, int) and m == 0):
                            pe.wait_ge(read, m)
                        for c in range(HCH):
                            x = pe.matmul(p[:, c * CH:(c + 1) * CH],
                                          pick[:, bass.ds(n + row, 1)].to_broadcast([BCR, P]),
                                          BC[:, hf * TH + c * CH:hf * TH + (c + 1) * CH], start=True, stop=True)
                        x.then_inc(done, 1)

                def add(n, s, last=False):
                    for h in range(DH):
                        pe.wait_ge(hC_ready, (hf * DS + n) * DH + h + 1)
                        for c in range(HCH):
                            x = pe.matmul(acc[2 * h + c][:], ident[:], hC[s][h][:, c * CH:(c + 1) * CH],
                                          start=False, stop=last)
                        x.then_inc(hC_used, 1)

                def one(n, s):
                    first, last = isinstance(n, int) and n == 0, isinstance(n, int) and n == DS - 1
                    if first and hf == 0:
                        spread(0)
                    if not last:
                        spread(n + 1)
                    elif hf == 0:
                        spread(0, hf=1)
                    if first:
                        if hf:
                            pe.wait_ge(y_gated, DH * HCH)
                        for h in range(DH):
                            for c in range(HCH):
                                pe.matmul(acc[2 * h + c][:], diagD[:, h],
                                          U[:, h, hf * TH + c * CH:hf * TH + (c + 1) * CH], start=True, stop=False)
                    else:
                        add(n - 1, 1 - s)

                over_states(pe, one)
                add(DS - 1, 1, last=True)
            pe.wait_ge(y_gated, 2 * DH * HCH)
            pe.wait_ge(b_ready, 2 * DS)
            pe.wait_ge(c_ready, 2 * DS)

            def project(c):
                for h in range(DH):
                    m = pe.matmul(bank[c], wout[:, h, :], SZ[:, h, c * CH:(c + 1) * CH],
                                  start=(h == 0), stop=(h == DH - 1))
                m.then_inc(out_psum, 1)

            def turn_back(c):
                pe.wait_ge(g_ready, c + 1)
                for j in range(TPC):
                    t = c * TPC + j
                    m = pe.transpose(bank[c][:, j * P:(j + 1) * P], U[:, 0, t * P:(t + 1) * P], ident[:])
                m.then_inc(tok_psum, 1)

            project(0)
            for c in range(NCH):
                if c + 1 < NCH:
                    project(c + 1)
                pe.wait_ge(out_ready, c + 1)
                pe.matmul(bank[4 + c], srw[:], gT[:, c], start=True, stop=True).then_inc(srw_psum, 1)
                if c:
                    turn_back(c - 1)
            turn_back(NCH - 1)


RE, RH = 8, 512
NR = RE - 1
RT = RH // P
XW = E + 4
TILES = NT + NR
NROW = TILES * P
ALPHA = 2.0


def switch(nc, io, X, ident, xs, ys, out):
    with ExitStack() as ctx:
        def sb(name, shape, dt=F32):
            return ctx.enter_context(nc.sbuf_tensor("s_" + name, shape, dt))

        def psum(name, shape, dt=F32):
            return ctx.enter_context(nc.psum_tensor("s_" + name, shape, dt))

        sem = ctx.enter_context(semaphores(nc, "s_"))

        R4, Y = sb("r4", [P, NT, XW]), sb("y", [P, NT, E])
        Hn = R4[:, :, 0:E]
        hT, ST = sb("hT", [P, TOK]), sb("st", [P, TOK])
        rw = sb("rw", [P, RE])
        sug, sd = sb("sug", [P, 2, RH]), sb("sd", [P, RT, E])
        UG = sb("ug", [P, NR, 2, RH])
        DW = sb("dw", [P, NR, RT, E])
        zero = sb("zero", [P, TILES * XW])
        pr = [sb(f"pr{i}", [P, NT, RE]) for i in range(5)]
        small = sb("small", [P, 4, NT])
        rev = sb("rev", [P, RE])
        revi = sb("revi", [P, RE], I32)
        jrow, ji = sb("jrow", [P, TILES]), sb("ji", [P, TILES], I32)
        hot = sb("hot", [P, NT, RE], BF16)
        tri, ones = sb("tri", [P, P], BF16), sb("ones", [P, P], BF16)
        carry = sb("carry", [P, RE, NT])
        tot, inc, exc = (sb(n, [P, RE, NT]) for n in ("tot", "inc", "exc"))
        cnt = sb("cnt", [P, 6, RE])
        cnti = sb("cnti", [P, RE], I32)
        ge = sb("ge", [P, TILES, NR - 1])
        eidf, eid = sb("eidf", [P, TILES]), sb("eid", [P, TILES], I32)
        posf, pos = sb("posf", [P, NT]), sb("pos", [P, NT], I32)
        sgate = sb("sgate", [P, 2, CH])
        sact = sb("sact", [P, 2, RT, CH])
        xt = [sb(f"xt{i}", [P, XW]) for i in range(4)]
        xT = [sb(f"xT{i}", [P, P]) for i in range(2)]
        gl = [sb(f"gl{i}", [P, RH]) for i in range(2)]
        hid = [sb(f"hid{i}", [P, RH]) for i in range(2)]
        hidT = [sb(f"hidT{i}", [P, RT, P]) for i in range(2)]
        yt = [sb(f"yt{i}", [P, E]) for i in range(2)]
        back = sb("back", [P, NT, E])

        pu = [psum(f"pu{i}", [P, CH]) for i in range(2)]
        pg = [psum(f"pg{i}", [P, CH]) for i in range(2)]
        ph, px, py, pr_ = psum("ph", [P, RT, P]), psum("px", [P, P]), psum("py", [P, E]), psum("pr", [P, CH])

        routed_loaded = sem("routed_loaded")
        loaded, cleared, zero_ready = sem("loaded"), sem("cleared"), sem("zero_ready")
        norms, normed = Norms(sb, sem, 2), sem("normed")
        hT_psum, hT_ready = sem("hT_psum"), sem("hT_ready")
        logits_psum, centred, exp_ready, const_ready = (
            sem("logits_psum"), sem("centred"), sem("exp_ready"), sem("const_ready"))
        hot_ready, counts_psum, pos_ready, eid_ready = (
            sem("hot_ready"), sem("counts_psum"), sem("pos_ready"), sem("eid_ready"))
        sorted_ = sem("sorted")
        sh_psum, sh_silu, sh_gated, sd_psum, sd_read = (
            sem("sh_psum"), sem("sh_silu"), sem("sh_gated"), sem("sd_psum"), sem("sd_read"))
        x_in = [sem(f"x_in{i}") for i in range(4)]
        xT_psum, xT_ready, ug_psum, silu_ready, hid_ready = (
            sem("xT_psum"), sem("xT_ready"), sem("ug_psum"), sem("silu_ready"), sem("hid_ready"))
        hT2_psum, hT2_ready, y_psum, y_ready, y_out = (
            sem("hT2_psum"), sem("hT2_ready"), sem("y_psum"), sem("y_ready"), [sem("y_out0"), sem("y_out1")])
        zrow_out, returned, shared_psum, final_ready, out_done = (
            sem("zrow_out"), sem("returned"), sem("shared_psum"), sem("final_ready"), sem("out_done"))
        dve_step, pool_step = sem("dve_step"), sem("pool_step")

        block = ctx.enter_context(nc.Block())

        @block.sync
        def _(sp):
            sp.dma_start(rw[:], io["router_w"]).then_inc(loaded, 16)
            sp.dma_start(sug[:], io["sug"]).then_inc(loaded, 16)
            sp.dma_start(sd[:], io["sdw"]).then_inc(loaded, 16)
            sp.dma_start(UG[:], io["ug"]).then_inc(routed_loaded, 16)
            sp.dma_start(DW[:], io["dw"]).then_inc(routed_loaded, 16)
            sp.wait_ge(zero_ready, 1)
            sp.dma_start(xs.rearrange("(p r) c -> p (r c)", p=P), zero[:]).then_inc(cleared, 16)
            sp.dma_start(ys[NROW:NROW + 1, :], zero[0:1, 0:E]).then_inc(zrow_out, 16)
            sp.wait_ge(sorted_, 16 * NT)
            src = xs.rearrange("(t p) c -> t p c", p=P)
            dst = ys[0:NROW].rearrange("(t p) c -> t p c", p=P)

            def load(j, s):
                sp.dma_start(xt[s][:], src[bass.ds(j, 1)].rearrange("t p c -> (t p) c")).then_inc(x_in[s], 16)

            def store(j, s):
                sp.wait_ge(y_ready, j + 1)
                sp.dma_start(dst[bass.ds(j, 1)].rearrange("t p c -> (t p) c"), yt[s][:]).then_inc(y_out[s], 16)

            for j in range(4):
                load(j, j)
            with sp.Fori(0, (TILES - 4) // 4) as i:
                for s in range(4):
                    sp.wait_ge(hid_ready, 4 * i + s + 1)
                    load(4 * i + s + 4, s)
                    store(4 * i + s, s % 2)
            done = (TILES - 4) // 4 * 4
            for j in range(done, TILES):
                if j + 4 < TILES:
                    sp.wait_ge(hid_ready, j + 1)
                    load(j + 4, j % 4)
                store(j, j % 2)
            by_tile = out.rearrange("b (t p) e -> p (b t) e", p=P)
            for c in range(NCH):
                sp.wait_ge(final_ready, c + 1)
                sp.dma_start(by_tile[:, c * TPC:(c + 1) * TPC], X[:, c * TPC:(c + 1) * TPC]).then_inc(out_done, 16)
            sp.wait_ge(out_done, 16 * NCH)

        @block.gpsimd
        def _(pool):
            step = Steps(pool, pool_step)
            pool.memset(zero[:], 0.0).then_inc(zero_ready, 1)
            norms.prepare(pool)
            step.then(pool.iota(revi[:], pattern=[[-1, RE]], base=RE, channel_multiplier=0))
            step.then(pool.iota(ji[:], pattern=[[1, TILES]], base=0, channel_multiplier=0))
            step.then(pool.tensor_copy(rev[:], revi[:]))
            step.then(pool.tensor_copy(jrow[:], ji[:]))
            step.then(pool.memset(ones[:], 1.0))
            step.then(pool.affine_select(out=tri[:], in_=ones[:], compare_op=ALU.is_gt, fill=0.0, base=0,
                                         pattern=[[1, P]], channel_multiplier=-1))
            step.then(pool.memset(carry[:], 1.0))
            pool.memset(carry[:, :, 0:1], 0.0).then_inc(const_ready, 1)
            pool.wait_ge(const_ready, 1)
            norms.roots(pool, step, 0)
            pool.wait_ge(pos_ready, 1)
            pool.wait_ge(cleared, 16)
            for t in range(NT):
                pool.indirect_dma_start(xs, bass.IndirectOffsetOnAxis(ap=pos[:, t:t + 1], axis=0), R4[:, t, :], None,
                                        bounds_check=NROW - 1, oob_is_err=False).then_inc(sorted_, 16)
            pool.wait_ge(y_out[0], 16 * ((TILES + 1) // 2))
            pool.wait_ge(y_out[1], 16 * (TILES // 2))
            pool.wait_ge(zrow_out, 16)
            for t in range(NT):
                pool.indirect_dma_start(back[:, t, :], None, ys, bass.IndirectOffsetOnAxis(ap=pos[:, t:t + 1], axis=0)
                                        ).then_inc(returned, 16)
            norms.roots(pool, step, 1)

        def tile_loop(eng, one):
            one(0, 0)
            with eng.Fori(0, (TILES - 3) // 2) as i:
                one(2 * i + 1, 1)
                one(2 * i + 2, 0)
            one(TILES - 2, 1)
            one(TILES - 1, 0)

        @block.scalar
        def _(act):
            for c in range(NCH):
                act.wait_ge(hT_psum, c + 1)
                act.activation(hT[:, c * CH:(c + 1) * CH], pu[c % 2][:], ACT.Copy).then_inc(hT_ready, 1)
            act.wait_ge(centred, 1)
            act.activation(pr[1][:], pr[0][:], ACT.Exp).then_inc(exp_ready, 1)
            for c in range(NCH):
                for j in range(RT):
                    n = c * RT + j
                    act.wait_ge(sh_psum, n + 1)
                    if n >= 2:
                        act.wait_ge(sh_gated, n - 1)
                    act.activation(sgate[:, n % 2], pg[n % 2][:], ACT.Silu).then_inc(sh_silu, 1)
                act.wait_ge(sd_psum, c + 1)
                act.activation(ST[:, c * CH:(c + 1) * CH], pr_[:], ACT.Copy).then_inc(sd_read, 1)

            def turned(j, s):
                act.wait_ge(xT_psum, j + 1)
                if not (isinstance(j, int) and j < 2):
                    act.wait_ge(ug_psum, j - 1)
                act.activation(xT[s][:], px[:], ACT.Copy).then_inc(xT_ready, 1)

            def silu(j, s):
                act.wait_ge(ug_psum, j + 1)
                if not (isinstance(j, int) and j < 2):
                    act.wait_ge(hid_ready, j - 1)
                act.activation(gl[s][:], pg[s][:], ACT.Silu).then_inc(silu_ready, 1)

            def hidden_turned(j, s):
                act.wait_ge(hT2_psum, j + 1)
                if not (isinstance(j, int) and j < 2):
                    act.wait_ge(y_psum, j - 1)
                act.activation(hidT[s][:], ph[:], ACT.Copy).then_inc(hT2_ready, 1)

            turned(0, 0)
            turned(1, 1)
            silu(0, 0)

            def one(j, s):
                if not (isinstance(j, int) and j >= TILES - 2):
                    turned(j + 2, s)
                if not (isinstance(j, int) and j >= TILES - 1):
                    silu(j + 1, 1 - s)
                hidden_turned(j, s)

            tile_loop(act, one)

        @block.vector
        def _(dve):
            v = dve
            step = Steps(dve, dve_step)
            norms.rows(dve, step, 0, X, Hn, normed)
            dve.wait_ge(logits_psum, 1)
            lg = pr_[:, 0:NT * RE].rearrange("p (t e) -> p t e", e=RE)
            step.then(v.tensor_reduce(small[:, 0], lg, AX.X, ALU.max))
            v.tensor_tensor(pr[0][:], lg, per_row(small[:, 0], RE), ALU.subtract).then_inc(centred, 1)
            dve.wait_ge(exp_ready, 1)
            step.then(v.tensor_reduce(small[:, 1], pr[1][:], AX.X, ALU.add))
            step.then(v.reciprocal(small[:, 2], small[:, 1]))
            step.then(v.tensor_tensor(pr[0][:], pr[1][:], per_row(small[:, 2], RE), ALU.mult))
            step.then(v.tensor_reduce(small[:, 3], pr[0][:], AX.X, ALU.max))
            step.then(v.tensor_tensor(pr[1][:], pr[0][:], per_row(small[:, 3], RE), ALU.is_equal))
            dve.wait_ge(const_ready, 1)
            revb = rev[:].unsqueeze(1).to_broadcast([P, NT, RE])
            step.then(v.tensor_tensor(pr[2][:], pr[1][:], revb, ALU.mult))
            step.then(v.tensor_reduce(small[:, 0], pr[2][:], AX.X, ALU.max))
            step.then(v.tensor_tensor(pr[3][:], revb, per_row(small[:, 0], RE), ALU.is_equal))
            step(v.tensor_scalar(R4[:, :, E:XW], small[:, 3].unsqueeze(2).to_broadcast([P, NT, XW - E]), ALPHA, None,
                                 ALU.mult))
            v.tensor_copy(hot[:], pr[3][:]).then_inc(hot_ready, 1)
            dve.wait_ge(counts_psum, 1)
            before = pr_[:, 0:NT * RE].rearrange("p (t e) -> p t e", e=RE)
            totals = pr_[:, NT * RE:2 * NT * RE].rearrange("p (t e) -> p e t", e=RE)
            step.then(v.tensor_copy(tot[:], totals))
            flat = "p e t -> p (e t)"
            step.then(v.tensor_tensor_scan(inc[:].rearrange(flat), carry[:].rearrange(flat), tot[:].rearrange(flat),
                                           0.0, ALU.mult, ALU.add))
            step.then(v.tensor_tensor(exc[:], inc[:], tot[:], ALU.subtract))
            step.then(v.tensor_scalar(cnti[:], inc[:, :, NT - 1], float(P - 1), None, ALU.add))
            step.then(v.tensor_single_scalar(cnti[:], cnti[:], 7, ALU.logical_shift_right))
            step.then(v.tensor_copy(cnt[:, 0], cnti[:]))
            step.then(v.memset(cnt[:, 1], 1.0))
            step.then(v.tensor_tensor_scan(cnt[:, 2], cnt[:, 1], cnt[:, 0], 0.0, ALU.mult, ALU.add))
            step.then(v.tensor_tensor(cnt[:, 3], cnt[:, 2], cnt[:, 0], ALU.subtract))
            step.then(v.tensor_scalar(cnt[:, 4], cnt[:, 3], float(P), None, ALU.mult))
            step.then(v.tensor_tensor(pr[0][:], before, exc[:].rearrange("p e t -> p t e"), ALU.add))
            step.then(v.tensor_tensor(pr[1][:], pr[0][:], cnt[:, 4:5].to_broadcast([P, NT, RE]), ALU.add))
            step.then(v.memset(pr[1][:, :, NR:RE], float(NROW)))
            step.then(v.tensor_tensor(pr[2][:], pr[1][:], pr[3][:], ALU.mult))
            step.then(v.tensor_reduce(posf[:], pr[2][:], AX.X, ALU.add))
            v.tensor_copy(pos[:], posf[:]).then_inc(pos_ready, 1)
            step.then(v.tensor_tensor(ge[:], per_row(jrow[:], NR - 1),
                                      cnt[:, 2:3, 0:NR - 1].to_broadcast([P, TILES, NR - 1]), ALU.is_ge))
            step.then(v.tensor_reduce(eidf[:], ge[:], AX.X, ALU.add))
            v.tensor_copy(eid[:], eidf[:]).then_inc(eid_ready, 1)
            for c in range(NCH):
                for j in range(RT):
                    n = c * RT + j
                    dve.wait_ge(sh_silu, n + 1)
                    if c >= 2 and j == 0:
                        dve.wait_ge(sd_psum, c - 1)
                    v.tensor_tensor(sact[:, c % 2, j], sgate[:, n % 2], pu[n % 2][:], ALU.mult).then_inc(sh_gated, 1)

            def gate4(j, s4, k4):
                s = s4 % 2
                dve.wait_ge(silu_ready, j + 1)
                dve.wait_ge(x_in[s4], 16 * (k4 + 1))
                if not (isinstance(j, int) and j < 2):
                    dve.wait_ge(hT2_psum, j - 1)
                v.scalar_tensor_tensor(hid[s][:], pu[s][:], xt[s4][:, E:E + 1], gl[s][:], ALU.mult, ALU.mult
                                       ).then_inc(hid_ready, 1)

            def result(j, s, k, first=False):
                dve.wait_ge(y_psum, j + 1)
                if not first:
                    dve.wait_ge(y_out[s], 16 * k)
                v.tensor_copy(yt[s][:], py[:]).then_inc(y_ready, 1)

            gate4(0, 0, 0)
            gate4(1, 1, 0)
            gate4(2, 2, 0)
            result(0, 0, 0, True)
            gate4(3, 3, 0)
            result(1, 1, 0, True)
            with dve.Fori(1, TILES // 4) as i:
                for s4 in range(4):
                    gate4(4 * i + s4, s4, i)
                    result(4 * i + s4 - 2, s4 % 2, 2 * i + s4 // 2 - 1)
            for j in range(TILES // 4 * 4, TILES):
                gate4(j, j % 4, j // 4)
                result(j - 2, j % 2, j // 2 - 1)
            for j in (TILES - 2, TILES - 1):
                result(j, j % 2, j // 2)
            dve.wait_ge(returned, 16 * NT)
            banks = [pu[0], pu[1], pg[0], pg[1]]
            for c in range(NCH):
                dve.wait_ge(shared_psum, c + 1)
                step.then(v.tensor_tensor(Y[:, c * TPC:(c + 1) * TPC], back[:, c * TPC:(c + 1) * TPC],
                                          banks[c][:].rearrange("p (t e) -> p t e", e=E), ALU.add))
                norms.statistics(dve, step, 1, c, Y)
            norms.residual(dve, step, 1, Y, X, final_ready)

        @block.tensor
        def _(pe):
            pe.wait_ge(loaded, 16 * 3)
            for c in range(NCH):
                pe.wait_ge(normed, c + 1)
                if c >= 2:
                    pe.wait_ge(hT_ready, c - 1)
                for j in range(TPC):
                    t = pe.transpose(pu[c % 2][:, j * P:(j + 1) * P], Hn[:, c * TPC + j, :], ident[:])
                t.then_inc(hT_psum, 1)
            pe.wait_ge(hT_ready, NCH)
            for t in range(NT):
                m = pe.matmul(pr_[:, t * RE:(t + 1) * RE], hT[:, t * P:(t + 1) * P], rw[:], start=True, stop=True)
            m.then_inc(logits_psum, 1)
            pe.wait_ge(hot_ready, 1)
            pe.wait_ge(const_ready, 1)
            hots = hot[:].rearrange("p t e -> p (t e)")
            pe.matmul(pr_[:, 0:NT * RE], tri[:], hots, start=True, stop=True)
            pe.matmul(pr_[:, NT * RE:2 * NT * RE], ones[:], hots, start=True, stop=True).then_inc(counts_psum, 1)
            for c in range(NCH):
                at = slice(c * CH, (c + 1) * CH)
                for j in range(RT):
                    n = c * RT + j
                    if n >= 2:
                        pe.wait_ge(sh_gated, n - 1)
                    pe.matmul(pg[n % 2][:], sug[:, 1, j * P:(j + 1) * P], hT[:, at], start=True, stop=True)
                    pe.matmul(pu[n % 2][:], sug[:, 0, j * P:(j + 1) * P], hT[:, at], start=True, stop=True
                              ).then_inc(sh_psum, 1)
                pe.wait_ge(sh_gated, (c + 1) * RT)
                if c:
                    pe.wait_ge(sd_read, c)
                else:
                    pe.wait_ge(pos_ready, 1)
                for j in range(RT):
                    m = pe.matmul(pr_[:], sd[:, j, :], sact[:, c % 2, j, :], start=(j == 0), stop=(j == RT - 1))
                m.then_inc(sd_psum, 1)

            def turn(j, s4, k4):
                pe.wait_ge(x_in[s4], 16 * (k4 + 1))
                if not (isinstance(j, int) and j == 0):
                    pe.wait_ge(xT_ready, j)
                pe.transpose(px[:], xt[s4][:, 0:E], ident[:]).then_inc(xT_psum, 1)

            def up(j, s):
                e = pe.value_load(eid[0:1, bass.ds(j, 1)], min_val=0, max_val=NR - 1)
                pe.wait_ge(xT_ready, j + 1)
                if not (isinstance(j, int) and j < 2):
                    pe.wait_ge(hid_ready, j - 1)
                pe.matmul(pg[s][:], xT[s][:], UG[:, bass.ds(e, 1), 1, :].rearrange("p a h -> p (a h)"),
                          start=True, stop=True)
                pe.matmul(pu[s][:], xT[s][:], UG[:, bass.ds(e, 1), 0, :].rearrange("p a h -> p (a h)"),
                          start=True, stop=True).then_inc(ug_psum, 1)

            def hidden(j, s):
                pe.wait_ge(hid_ready, j + 1)
                if not (isinstance(j, int) and j == 0):
                    pe.wait_ge(hT2_ready, j)
                for i in range(RT):
                    m = pe.transpose(ph[:, i, :], hid[s][:, i * P:(i + 1) * P], ident[:])
                m.then_inc(hT2_psum, 1)

            def down(j, s):
                e = pe.value_load(eid[0:1, bass.ds(j, 1)], min_val=0, max_val=NR - 1)
                pe.wait_ge(hT2_ready, j + 1)
                if not (isinstance(j, int) and j == 0):
                    pe.wait_ge(y_ready, j)
                for i in range(RT):
                    m = pe.matmul(py[:], hidT[s][:, i, :], DW[:, bass.ds(e, 1), i, :].rearrange("p a h -> p (a h)"),
                                  start=(i == 0), stop=(i == RT - 1))
                m.then_inc(y_psum, 1)

            pe.wait_ge(routed_loaded, 32)
            pe.wait_ge(eid_ready, 1)
            pe.wait_ge(sh_gated, NCH * RT)

            def one(j, s4, k4):
                last = isinstance(j, int)
                if not (last and j >= TILES - 2):
                    turn(j + 2, (s4 + 2) % 4, k4 + (s4 + 2) // 4)
                if not (last and j >= TILES - 1):
                    up(j + 1, (s4 + 1) % 2)
                if not (last and j == 0):
                    down(j - 1, (s4 + 1) % 2)
                hidden(j, s4 % 2)

            turn(0, 0, 0)
            turn(1, 1, 0)
            up(0, 0)
            for j in range(4):
                one(j, j, 0)
            with pe.Fori(1, TILES // 4) as i:
                for s4 in range(4):
                    one(4 * i + s4, s4, i)
            for j in range(TILES // 4 * 4, TILES):
                one(j, j % 4, j // 4)
            down(TILES - 1, (TILES - 1) % 2)
            pe.wait_ge(hid_ready, TILES)
            pe.wait_ge(sd_read, NCH)
            banks = [pu[0], pu[1], pg[0], pg[1]]
            for c in range(NCH):
                for j in range(TPC):
                    m = pe.transpose(banks[c][:, j * P:(j + 1) * P], ST[:, (c * TPC + j) * P:(c * TPC + j + 1) * P],
                                     ident[:])
                m.then_inc(shared_psum, 1)


def sandwich(nc, io, out):
    rows = nc.dram_tensor("expert_rows", (TOK, ROWW), F32, kind="Internal").ap()
    results = nc.dram_tensor("pick_results", (NZ, E), F32, kind="Internal").ap()
    slots = nc.dram_tensor("expert_slots", (NSLOT,), F32, kind="Internal").ap()
    xs = nc.dram_tensor("sorted_rows", (NROW, XW), F32, kind="Internal").ap()
    ys = nc.dram_tensor("sorted_results", (NROW + 1, E), F32, kind="Internal").ap()
    with ExitStack() as ctx:
        X = ctx.enter_context(nc.sbuf_tensor("X", [P, NT, E], F32))
        ident = ctx.enter_context(nc.sbuf_tensor("identity", [P, P], F32))
        attention(nc, io, X, ident, results)
        with ExitStack() as ffn:
            ST = ffn.enter_context(nc.sbuf_tensor("shared_T", [P, TOK], F32))
            tab = ffn.enter_context(nc.sbuf_tensor("row_table", [P, NG, 2, GC], I32))
            W1 = [ffn.enter_context(nc.sbuf_tensor(f"w1_{i}", [P, GE, 2 * FF], F32)) for i in range(2)]
            W2 = [ffn.enter_context(nc.sbuf_tensor(f"w2_{i}", [P, GE, FT, E], F32)) for i in range(2)]
            route(nc, io, X, ident, rows, slots, tab, ST, W1, W2)
            experts(nc, io, ident, rows, results, tab, W1, W2)
            combine(nc, io, X, ident, results, ST)
        mamba(nc, io, X, ident)
        switch(nc, io, X, ident, xs, ys, out)


def kernel(**inputs):
    import numpy as np
    import concourse.bacc as bacc
    from concourse.bass_utils import run_bass_kernel_spmd

    a = {name: np.asarray(value) for name, value in inputs.items()}

    def attn(name):
        return a["L0_attn_" + name]

    def moe(name):
        return a["L0_ffn_" + name]

    def mix(name):
        return a["L1_attn_" + name]

    def sw(name):
        return a["L1_ffn_" + name]

    def by_feature(w):
        return w.reshape(w.shape[:-1] + (H, D)).swapaxes(-1, -2).reshape(w.shape)

    Jd = np.zeros((E, E), np.float32)
    for h in range(H):
        Jd[h::H, h::H] = attn("J_attn")[h]
    own = np.zeros((P, GC, GE), np.float32)
    for r in range(GR):
        own[r % P, r // P, r // CAP] = 1
    bc_rows = 2 * DS
    pick = np.zeros((3 * bc_rows, bc_rows), np.float32)
    for r in range(3 * bc_rows):
        pick[r, r % bc_rows] = 1
    xp = mix("x_proj_w")
    arrays = dict(
        x=attn("x"), ident=np.eye(P, dtype=np.float32),
        WqT=by_feature(attn("Wq").T), WkT=by_feature(attn("Wk").T), WvT=attn("Wv").T, WoT=attn("Wo").T, Jd=Jd,
        bq=by_feature(attn("bq")), bk=by_feature(attn("bk")), bv=attn("bv"), bo=attn("bo"),
        lam=attn("lambda_attn").reshape(1),
        wgT=moe("wg").T, sw1T=moe("shared_w1").T, sw2T=moe("shared_w2").T.reshape(FT, P, E).transpose(1, 0, 2),
        w1T=moe("expert_w1").reshape(NG, GE, 2 * FF, E).transpose(0, 3, 1, 2),
        w2T=moe("expert_w2").reshape(NG, GE, E, FT, P).transpose(0, 4, 1, 3, 2), own=own,
        sq_w=mix("sq_w"), srw_w=mix("srw_w"), in_proj_w=mix("in_proj_w"), dt_w=mix("dt_w"), pick=pick,
        x_proj=np.concatenate([xp[:, DR:]] * 3 + [xp[:, :DR]], 1), out_proj_w=mix("out_proj_w"),
        A_log=mix("A_log"), conv_wT=mix("conv_w").T, m_g=mix("ln_g"), m_b=mix("ln_b"), m_sq_b=mix("sq_b"),
        m_srw_b=mix("srw_b"), res_scale=mix("res_scale"), m_conv_b=mix("conv_b"), m_dt_b=mix("dt_b"), m_D=mix("D"),
        router_w=sw("router_w"), sug=np.stack([sw("shared_up_w"), sw("shared_gate_w")], 1),
        sdw=sw("shared_down_w").reshape(RT, P, E).transpose(1, 0, 2),
        ug=np.stack([sw("up_w"), sw("gate_w")], 1).transpose(2, 0, 1, 3),
        dw=sw("down_w").reshape(NR, RT, P, E).transpose(2, 0, 1, 3))

    nc = bacc.Bacc("TRN2", target_bir_lowering=False, num_devices=1)
    io, fed = {}, {}
    for name, array in arrays.items():
        fed[f"in_{name}_dram"] = np.ascontiguousarray(array)
        io[name] = nc.dram_tensor(f"in_{name}_dram", array.shape, mybir.dt.from_np(array.dtype),
                                  kind="ExternalInput").ap()
    out = nc.dram_tensor("out_dram", (NB, S, E), F32, kind="ExternalOutput").ap()
    sandwich(nc, io, out)
    r = run_bass_kernel_spmd(nc, [fed], core_ids=[0])
    return r.results[0]["out_dram"]
```

```python
from contextlib import ExitStack, contextmanager

import concourse.bass as bass
from concourse import mybir

F32 = mybir.dt.float32
BF16 = mybir.dt.bfloat16
I32 = mybir.dt.int32
ALU = mybir.AluOpType
ACT = mybir.ActivationFunctionType
AX = mybir.AxisListType

P = 128
NB, S, E = 8, 256, 128
TOK = NB * S
NT = TOK // P
TPB = S // P
CH = 512
NCH = TOK // CH
TPC = CH // P
EPS = 1e-5


@contextmanager
def semaphores(nc, prefix):
    taken = []

    def sem(name):
        taken.append(nc.alloc_semaphore(prefix + name))
        return taken[-1]

    yield sem
    nc.clear_and_free_semaphores(taken)
    nc.all_engine_barrier()


class Steps:

    def __init__(self, eng, sem, passes=None):
        self.eng, self.sem, self.n, self.passes = eng, sem, 0, passes

    def __call__(self, ins):
        ins.then_inc(self.sem, 1)
        self.n = self.n + 1
        return ins

    def wait(self):
        self.eng.wait_ge(self.sem, self.n)
        if self.passes is not None and not isinstance(self.n, int):
            self.eng.sem_inc(self.passes, 1)

    def then(self, ins):
        self(ins)
        self.wait()


def per_row(ap, n):
    return ap.unsqueeze(2).to_broadcast([ap.shape[0], ap.shape[1], n])


class Norms:

    def __init__(self, sb, sem, n):
        self.moments = sb("ln_moments", [P, n, NT, 6])
        self.mean_var = sb("ln_mean_var", [P, n, NT, 2])
        self.var_eps, self.rstd = sb("ln_var_eps", [P, n, NT]), sb("ln_rstd", [P, n, NT])
        self.half = sb("ln_half", [P, TPC])
        self.stats_ready, self.rstd_ready = sem("ln_stats_ready"), sem("ln_rstd_ready")
        self.half_ready = sem("ln_half_ready")

    def statistics(self, dve, step, k, c, src):
        tiles = range(c * TPC, (c + 1) * TPC)
        for t in tiles:
            step(dve.bn_stats(self.moments[:, k, t, :], src[:, t, :]))
        step.wait()
        for t in tiles:
            a = dve.bn_aggr(self.mean_var[:, k, t, :], self.moments[:, k, t, :])
        a.then_inc(self.stats_ready, 1)

    def apply(self, dve, k, c, src, dst):
        dve.wait_ge(self.rstd_ready, k * NCH + c + 1)
        for t in range(c * TPC, (c + 1) * TPC):
            a = dve.tensor_scalar(dst[:, t, :], src[:, t, :], self.mean_var[:, k, t, 0:1], self.rstd[:, k, t:t + 1],
                                  ALU.subtract, ALU.mult)
        return a

    def rows(self, dve, step, k, src, dst, done):
        for c in range(NCH):
            self.statistics(dve, step, k, c, src)
        for c in range(NCH):
            self.apply(dve, k, c, src, dst).then_inc(done, 1)

    def residual(self, dve, step, k, c, src, X, done):
        step.then(self.apply(dve, k, c, src, src))
        at = slice(c * TPC, (c + 1) * TPC)
        dve.tensor_tensor(X[:, at], X[:, at], src[:, at], ALU.add).then_inc(done, 1)

    def prepare(self, pool):
        pool.memset(self.half[:], -0.5).then_inc(self.half_ready, 1)

    def roots(self, pool, step, k):
        pool.wait_ge(self.half_ready, 1)
        for c in range(NCH):
            at = slice(c * TPC, (c + 1) * TPC)
            pool.wait_ge(self.stats_ready, k * NCH + c + 1)
            step.then(pool.tensor_scalar(self.var_eps[:, k, at], self.mean_var[:, k, at, 1], 1.0, EPS,
                                         ALU.mult, ALU.add))
            pool.tensor_tensor(self.rstd[:, k, at], self.var_eps[:, k, at], self.half[:], ALU.pow
                               ).then_inc(self.rstd_ready, 1)


H, D = 16, 8
PARTS = 3
BLOCKS = 6
FEAT = 2 * D
KROWS = BLOCKS * FEAT
KALL = KROWS + PARTS
ZW = 1024
HU = H // 2
RING = HU
UNITS = 2 * NB
SLOTS = 4


def attention(nc, io, X, ident, results):
    with ExitStack() as ctx:
        def sb(name, shape, dt=F32):
            return ctx.enter_context(nc.sbuf_tensor(name, shape, dt))

        def psum(name, shape, dt=F32):
            return ctx.enter_context(nc.psum_tensor(name, shape, dt))

        sem = ctx.enter_context(semaphores(nc, "a_"))

        w = sb("a_w", [P, 5, E])
        vec = sb("a_vec", [P, 4])
        rowb = sb("a_rowb", [P, 2, E])
        Hn = sb("a_hn", [P, NT, E])
        Y = sb("a_y", [P, NT, E])
        hT = sb("a_hT", [P, TOK])
        TQ = sb("a_tq", [P, TOK])
        S4 = sb("a_s4", [P, 4, TOK])
        V = sb("a_v", [P, NT, H, D + 1])
        part = sb("a_part", [P, 2, PARTS, 4, S], BF16)
        rest = sb("a_rest", [P, 2, 4, S])
        QS = [sb(f"a_qs{i}", [KALL, HU, S], BF16) for i in range(SLOTS)]
        KS = [sb(f"a_ks{i}", [KALL, HU, S], BF16) for i in range(SLOTS)]
        mx = sb("a_mx", [P, 2, HU, TPB])
        mr = sb("a_mr", [TPB * HU, P])
        mp = [sb(f"a_mp{i}", [TPB * HU, PARTS, P], BF16) for i in range(2)]
        PT = sb("a_pt", [P, RING, TPB, S])
        Vb = sb("a_vb", [P, 2, TPB, H, 32])
        OU = sb("a_ou", [P, 2, 2, S])
        rden = sb("a_rden", [P, 2, 2, TPB, 4])
        O = sb("a_o", [P, TPB, E])
        OT = sb("a_ot", [P, S])
        zero = sb("a_zero", [P, ZW])

        ps1 = [psum(f"a_s1_{i}", [P, TPB, S]) for i in range(2)]
        ps2 = [psum(f"a_s2_{i}", [P, TPB, S]) for i in range(2)]
        pso = [psum(f"a_po{i}", [P, 2, S]) for i in range(2)]
        pst = psum("a_pt_", [P, 2, TPB, P])
        psm = psum("a_pm", [P, CH])

        def flat(bank):
            return bank[:].rearrange("p a b -> p (a b)")

        wide = [flat(x) for x in (ps1[0], ps1[1], ps2[0], ps2[1])]
        qbank, kbank = [flat(x) for x in ps2], [flat(x) for x in pso]

        bounce = nc.dram_tensor("a_bounce", (NB, PARTS * 4, P, S), BF16, kind="Internal").ap()
        bounced_rows = bounce.rearrange("b (c a) (d u h) t -> b c (a d) u (h t)", a=4, u=2, h=HU)

        loaded, bounced = sem("loaded"), sem("bounced")
        norms = Norms(lambda name, shape: sb("a_" + name, shape), sem, 2)
        zero_ready, cleared = sem("zero_ready"), sem("cleared")
        x_ready, x_done = sem("x_ready"), sem("x_done")
        normed, hT_psum, hT_ready = sem("normed"), sem("hT_psum"), sem("hT_ready")
        qk_psum, qk_ready = sem("qk_psum"), sem("qk_ready")
        qj_psum, qj_ready = sem("qj_psum"), sem("qj_ready")
        v_psum, v_ready, v_ones = sem("v_psum"), sem("v_ready"), sem("v_ones")
        k_ones = sem("k_ones")
        first_split, split_ready = sem("first_split"), sem("split_ready")
        stack_ready = [sem(f"stack{i}") for i in range(SLOTS)]
        vb_ready = sem("vb_ready")
        rows_psum, rows_maxed = sem("rows_psum"), sem("rows_maxed")
        maxT_psum, maxT_ready, max_rows = (
            sem("maxT_psum"), sem("maxT_ready"), [sem(f"max_rows{i}") for i in range(SLOTS)])
        cols_psum, exp_ready, pv_done = sem("cols_psum"), sem("exp_ready"), sem("pv_done")
        ou_ready, ot_psum = sem("ou_ready"), sem("ot_psum")
        o_ready, oT_psum, oT_ready, y_psum, y_ready = (
            sem("o_ready"), sem("oT_psum"), sem("oT_ready"), sem("y_psum"), sem("y_ready"))
        den_ready = sem("den_ready")
        dve_step, act_step, pool_step = sem("dve_step"), sem("act_step"), sem("pool_step")
        pool_passes, sp_passes = sem("pool_passes"), sem("sp_passes")

        NLOAD = 11

        block = ctx.enter_context(nc.Block())

        def by_batch(eng, one):
            one(0, 0)
            one(1, 1)
            with eng.Fori(1, NB // 2 - 1) as i:
                for s in range(2):
                    one(2 * i + s, s)
            one(NB - 2, 0)
            one(NB - 1, 1)

        def split(eng, step, b, s):
            src = S4[:, :, bass.ds(b * S, S)]
            step.then(eng.tensor_copy(part[:, s, 0], src))
            step.then(eng.tensor_tensor(rest[:, s], src, part[:, s, 0], ALU.subtract))
            step.then(eng.tensor_copy(part[:, s, 1], rest[:, s]))
            return eng.tensor_tensor(part[:, s, 2], rest[:, s], part[:, s, 1], ALU.subtract)

        @block.sync
        def _(sp):
            sp.dma_start(X[:], io["x"].rearrange("b (t p) e -> p (b t) e", p=P)).then_inc(x_ready, 16)
            for n, name in enumerate(("WqT", "WkT", "WvT", "WoT", "Jd")):
                sp.dma_start(w[:, n, :], io[name]).then_inc(loaded, 16)
            for n, name in enumerate(("bq", "bk")):
                sp.dma_start(vec[:, n:n + 1], io[name].unsqueeze(1)).then_inc(loaded, 16)
            sp.dma_start(vec[:, 2:3], io["lam"].unsqueeze(1).to_broadcast([P, 1])).then_inc(loaded, 16)
            for n, name in enumerate(("bv", "bo")):
                sp.dma_start(rowb[:, n, :], io[name].unsqueeze(0).to_broadcast([P, E])).then_inc(loaded, 16)
            sp.dma_start(ident[:], io["ident"]).then_inc(loaded, 16)
            sp.wait_ge(zero_ready, 1)
            cleared_rows = results.rearrange("(n p r) e -> n p (r e)", p=P, r=ZW // E)
            per_batch = cleared_rows.shape[0] // NB

            def bounce_out(b, s):
                if isinstance(b, int) and b == 0:
                    sp.wait_ge(first_split, 1)
                else:
                    sp.wait_ge(split_ready, b)
                sp.dma_start(bounce[bass.ds(b, 1)].rearrange("b c f t -> f (b c) t"),
                             part[:, s].rearrange("p c a t -> p (c a) t")).then_inc(bounced, 16)

            def stack(b, hh, s):
                q, u = 2 * s + hh, 2 * b + hh
                if not (isinstance(u, int) and u < SLOTS):
                    sp.wait_ge(cols_psum, (u - SLOTS + 1) * HU)
                    sp.sem_inc(sp_passes, 1)
                sp.wait_ge(bounced, 16 * (b + 1))
                src = bounced_rows[bass.ds(b, 1)].rearrange("b c r u x -> (b c) r u x")[:, :, hh]
                for row, n, qp, kp in ((0, 3, 0, 0), (3, 2, 1, 0), (5, 1, 2, 0)):
                    rows = slice(row * FEAT, (row + n) * FEAT)
                    sp.dma_start(QS[q][rows].rearrange("r h t -> r (h t)"),
                                 src[qp:qp + 1, 0:FEAT].to_broadcast([n, FEAT, HU * S])).then_inc(stack_ready[q], 16)
                    sp.dma_start(KS[q][rows].rearrange("r h t -> r (h t)"),
                                 src[kp:kp + n, FEAT:2 * FEAT]).then_inc(stack_ready[q], 16)

            def max_row(u, hh, q):
                sp.wait_ge(maxT_ready, u + 1)
                for c in range(PARTS):
                    sp.dma_start(QS[q][KROWS + c:KROWS + c + 1].rearrange("r h t -> r (h t)"),
                                 mp[hh][:, c, :]).then_inc(max_rows[q], 16)

            bounce_out(0, 0)
            stack(0, 0, 0)
            stack(0, 1, 0)
            bounce_out(1, 1)
            stack(1, 0, 1)
            max_row(0, 0, 0)

            def one(b, s):
                for hh in range(2):
                    u = 2 * b + hh
                    if not isinstance(u, int) or u + 3 < UNITS:
                        stack(b + 1 + hh, 1 - hh, (s + 1 + hh) % 2)
                    if not isinstance(u, int) or u + 1 < UNITS:
                        max_row(u + 1, 1 - hh, (2 * s + hh + 1) % SLOTS)
                    if hh == 0 and (not isinstance(b, int) or b + 2 < NB):
                        bounce_out(b + 2, s)
                for n in range(per_batch):
                    sp.dma_start(cleared_rows[bass.ds(per_batch * b + n, 1)].rearrange("n p x -> (n p) x"), zero[:]
                                 ).then_inc(cleared, 16)

            by_batch(sp, one)
            sp.wait_ge(cleared, 16 * per_batch * NB)

        @block.gpsimd
        def _(pool):
            step = Steps(pool, pool_step, passes=pool_passes)
            pool.memset(zero[:], 0.0).then_inc(zero_ready, 1)
            norms.prepare(pool)
            pool.memset(V[:, :, :, D:D + 1], 1.0).then_inc(v_ones, 1)
            norms.roots(pool, step, 0)
            pool.wait_ge(norms.rstd_ready, NCH)
            for q in range(SLOTS):
                pool.memset(KS[q][KROWS:KALL], 1.0).then_inc(k_ones, 1)
                pool.wait_ge(k_ones, q + 1)
            step.then(pool.memset(Vb[:], 0.0))

            def v_of(b, s):
                pool.tensor_copy(Vb[:, s, :, :, 0:D + 1], V[:, bass.ds(b * TPB, TPB)]).then_inc(vb_ready, 1)

            pool.wait_ge(qj_ready, 1)
            split(pool, step, 1, 1).then_inc(split_ready, 1)
            pool.wait_ge(v_ready, 1)
            for b in range(2):
                v_of(b, b)
            pool.wait_ge(qj_ready, NCH)
            pool.wait_ge(v_ready, NCH)

            def split_next(b, s):
                pool.wait_ge(bounced, 16 * (b - 1))
                split(pool, step, b, s).then_inc(split_ready, 1)

            def v_next(b, s):
                pool.wait_ge(pv_done, 4 * (b - 1))
                v_of(b, s)

            split_next(2, 0)
            first = step.n
            with pool.Fori(0, NB // 2 - 2) as i:
                for s in range(2):
                    step.n = first + i * 6 + 3 * s
                    split_next(2 * i + s + 3, 1 - s)
                    v_next(2 * i + s + 2, s)
            step.n = first + (NB // 2 - 2) * 6
            split_next(NB - 1, 1)
            v_next(NB - 2, 0)
            v_next(NB - 1, 1)
            norms.roots(pool, step, 1)

        @block.scalar
        def _(act):
            for c in range(NCH):
                act.wait_ge(hT_psum, c + 1)
                act.activation(hT[:, c * CH:(c + 1) * CH], wide[c], ACT.Copy).then_inc(hT_ready, 1)
            act.wait_ge(loaded, 16 * NLOAD)
            step = Steps(act, act_step)
            for c in range(NCH):
                at = slice(c * CH, (c + 1) * CH)
                for n in range(2):
                    act.wait_ge(qk_psum, 2 * c + n + 1)
                    src = (qbank, kbank)[n][c % 2]
                    if n == 0:
                        step.then(act.activation(S4[:, 0, at], src, ACT.Identity, bias=vec[:, 0:1]))
                        act.activation(TQ[:, at], S4[:, 0, at], ACT.Tanh).then_inc(qk_ready, 1)
                        act.wait_ge(qk_ready, 2 * c + 1)
                        step(act.activation(S4[:, 0, at], S4[:, 0, at], ACT.Copy, scale=float(D) ** -0.5))
                    else:
                        step(act.activation(S4[:, 2, at], src, ACT.Identity, bias=vec[:, 1:2]))
                        act.activation(S4[:, 3, at], src, ACT.Tanh, bias=vec[:, 1:2]).then_inc(qk_ready, 1)
                act.wait_ge(qj_psum, c + 1)
                act.activation(S4[:, 1, at], psm[:], ACT.Copy, scale=vec[:, 2:3]).then_inc(qj_ready, 1)

            def evacuate(u, hh):
                act.wait_ge(pv_done, 2 * u + 2)
                act.activation(OU[:, hh], pso[hh][:], ACT.Copy).then_inc(ou_ready, 1)

            def transposed(b):
                act.wait_ge(oT_psum, b + 1)
                act.activation(OT[:], psm[:, 0:S], ACT.Copy).then_inc(oT_ready, 1)

            def one(b, s):
                for hh in range(2):
                    u = 2 * b + hh
                    first = isinstance(u, int) and u == 0
                    for h in range(HU):
                        act.wait_ge(cols_psum, u * HU + h + 1)
                        if not first:
                            act.wait_ge(pv_done, 2 * u - 1 + h // 4)
                        act.activation(PT[:, h], ps2[h % 2][:], ACT.Exp).then_inc(exp_ready, 1)
                        if h == 3 and not first:
                            evacuate(u - 1, 1 - hh)
                        if h == 7 and hh == 0 and not (isinstance(b, int) and b == 0):
                            transposed(b - 1)

            step.wait()
            by_batch(act, one)
            evacuate(UNITS - 1, 1)
            transposed(NB - 1)

        @block.vector
        def _(dve):
            step = Steps(dve, dve_step)
            dve.wait_ge(x_ready, 16)
            norms.rows(dve, step, 0, X, Hn, normed)
            dve.wait_ge(loaded, 16 * NLOAD)
            dve.wait_ge(v_ones, 1)
            for c in range(NCH):
                dve.wait_ge(v_psum, c + 1)
                dve.tensor_tensor(V[:, c * TPC:(c + 1) * TPC, :, 0:D],
                                  ps1[c % 2][:].rearrange("p a (t h d) -> p (a t) h d", h=H, d=D),
                                  rowb[:, 0, :].rearrange("p (h d) -> p h d", d=D).unsqueeze(1)
                                  .to_broadcast([P, TPC, H, D]), ALU.add).then_inc(v_ready, 1)
                if c == 0:
                    dve.wait_ge(qj_ready, 1)
                    split(dve, step, 0, 0).then_inc(first_split, 1)

            def maxima(u, hh, h):
                dve.wait_ge(rows_psum, u * HU + h + 1)
                dve.tensor_reduce(mx[:, hh, h, :], ps1[h % 2][:], AX.X, ALU.max, negate=True).then_inc(rows_maxed, 1)

            def split_max(u, hh):
                dve.wait_ge(maxT_psum, u + 1)
                src = psm[0:TPB * HU, 0:P]
                step.then(dve.tensor_copy(mp[hh][:, 0], src))
                step.then(dve.tensor_tensor(mr[:], src, mp[hh][:, 0], ALU.subtract))
                step.then(dve.tensor_copy(mp[hh][:, 1], mr[:]))
                dve.tensor_tensor(mp[hh][:, 2], mr[:], mp[hh][:, 1], ALU.subtract).then_inc(maxT_ready, 1)

            def normalise(u, hh):
                dve.wait_ge(ot_psum, u + 1)
                src = pst[:].rearrange("p g t (h c) -> p g t h c", c=32)
                dve.reciprocal(rden[:, hh], src[:, :, :, :, D]).then_inc(den_ready, 1)
                dve.wait_ge(den_ready, u + 1)
                for g in range(2):
                    m = dve.tensor_tensor(
                        O[:].rearrange("p t (g h d) -> p g t h d", g=4, d=D)[:, 2 * hh + g],
                        src[:, g, :, :, 0:D], rden[:, hh, g].unsqueeze(3).to_broadcast([P, TPB, 4, D]), ALU.mult)
                m.then_inc(o_ready, 1)

            def project(b):
                dve.wait_ge(y_psum, b + 1)
                dve.tensor_tensor(Y[:, bass.ds(b * TPB, TPB)],
                                  psm[:, S:2 * S].rearrange("p (t e) -> p t e", e=E),
                                  rowb[:, 1:2, :].to_broadcast([P, TPB, E]), ALU.add).then_inc(y_ready, 1)

            for h in range(HU):
                maxima(0, 0, h)
            split_max(0, 0)
            for h in range(HU):
                maxima(1, 1, h)
            first = step.n

            def one(b, s):
                for hh in range(2):
                    u = 2 * b + hh
                    fixed = isinstance(u, int)
                    step.n = first + u * 3
                    for h in range(HU):
                        if not fixed or u + 2 < UNITS:
                            maxima(u + 2, hh, h)
                        if h == 0 and (not fixed or u + 1 < UNITS):
                            split_max(u + 1, 1 - hh)
                        if h == 6 and hh == 1 and (not fixed or b > 0):
                            project(b - 1)
                        if h == 5 and (not fixed or u > 0):
                            normalise(u - 1, 1 - hh)

            by_batch(dve, one)
            step.n = first + (UNITS - 1) * 3
            dve.wait_ge(y_ready, NB - 1)
            for c in range(NCH - 1):
                norms.statistics(dve, step, 1, c, Y)
            normalise(UNITS - 1, 1)
            norms.residual(dve, step, 1, 0, Y, X, x_done)
            norms.residual(dve, step, 1, 1, Y, X, x_done)
            project(NB - 1)
            norms.residual(dve, step, 1, 2, Y, X, x_done)
            dve.wait_ge(y_ready, NB)
            norms.statistics(dve, step, 1, NCH - 1, Y)
            norms.residual(dve, step, 1, NCH - 1, Y, X, x_done)

        @block.tensor
        def _(pe):
            pe.wait_ge(loaded, 16 * NLOAD)
            for c in range(NCH):
                pe.wait_ge(normed, c + 1)
                for j in range(TPC):
                    t = pe.transpose(wide[c][:, j * P:(j + 1) * P], Hn[:, c * TPC + j, :], ident[:])
                t.then_inc(hT_psum, 1)
            for c in range(NCH):
                at = slice(c * CH, (c + 1) * CH)
                pe.wait_ge(hT_ready, NCH if c == 0 else c + 1)
                if c >= 2:
                    pe.wait_ge(qk_ready, 2 * (c - 1))
                for n in range(2):
                    pe.matmul((qbank, kbank)[n][c % 2], w[:, n, :], hT[:, at],
                              start=True, stop=True).then_inc(qk_psum, 1)
                if c >= 2:
                    pe.wait_ge(v_ready, c - 1)
                for j in range(TPC):
                    v = pe.matmul(ps1[c % 2][:].rearrange("p a b -> p (a b)")[:, j * P:(j + 1) * P],
                                  hT[:, (c * TPC + j) * P:(c * TPC + j + 1) * P], w[:, 2, :], start=True, stop=True)
                v.then_inc(v_psum, 1)
                pe.wait_ge(qk_ready, 2 * c + 1)
                if c >= 1:
                    pe.wait_ge(qj_ready, c)
                pe.matmul(psm[:], w[:, 4, :], TQ[:, at], start=True, stop=True).then_inc(qj_psum, 1)

            def by_rows(u, q, k, h):
                if h == 0:
                    pe.wait_ge(stack_ready[q], 16 * 6 * (k + 1))
                if not (isinstance(u, int) and u == 0 and h < 2):
                    pe.wait_ge(rows_maxed, u * HU + h - 1)
                for it in range(TPB):
                    m = pe.matmul(ps1[h % 2][:, it], QS[q][0:KROWS, h, it * P:(it + 1) * P],
                                  KS[q][0:KROWS, h, :], start=True, stop=True)
                m.then_inc(rows_psum, 1)

            def by_columns(u, q, h):
                if not (isinstance(u, int) and u == 0 and h < 2):
                    pe.wait_ge(exp_ready, u * HU + h - 1)
                for jt in range(TPB):
                    m = pe.matmul(ps2[h % 2][:, jt], KS[q][:, h, jt * P:(jt + 1) * P], QS[q][:, h, :],
                                  start=True, stop=True)
                m.then_inc(cols_psum, 1)

            def pv(u, hh, s, g):
                pe.wait_ge(exp_ready, u * HU + 4 * g + 4)
                if g == 0 and not (isinstance(u, int) and u < 2):
                    pe.wait_ge(ou_ready, u - 1)
                for jt in range(TPB):
                    for k in range(4):
                        m = pe.matmul(pso[hh][32 * k:32 * k + 32, g, :], Vb[:, s, jt, HU * hh + 4 * g + k, :],
                                      PT[:, 4 * g + k, jt, :], start=(jt == 0), stop=(jt == TPB - 1))
                m.then_inc(pv_done, 1)

            def max_transposed(u, hh):
                pe.wait_ge(rows_maxed, (u + 1) * HU)
                pe.transpose(psm[0:TPB * HU, 0:P], mx[:, hh].rearrange("p h t -> p (h t)"), ident[:]
                             ).then_inc(maxT_psum, 1)

            def to_rows(u, hh):
                pe.wait_ge(ou_ready, u + 1)
                if not (isinstance(u, int) and u == 0):
                    pe.wait_ge(o_ready, u)
                for g in range(2):
                    for it in range(TPB):
                        m = pe.transpose(pst[:, g, it, :], OU[:, hh, g, it * P:(it + 1) * P], ident[:])
                m.then_inc(ot_psum, 1)

            def o_transposed(b):
                pe.wait_ge(o_ready, 2 * b + 2)
                for it in range(TPB):
                    m = pe.transpose(psm[:, it * P:(it + 1) * P], O[:, it, :], ident[:])
                m.then_inc(oT_psum, 1)

            def project(b):
                pe.wait_ge(oT_ready, b + 1)
                for it in range(TPB):
                    m = pe.matmul(psm[:, S + it * P:S + (it + 1) * P], OT[:, it * P:(it + 1) * P], w[:, 3, :],
                                  start=True, stop=True)
                m.then_inc(y_psum, 1)

            pe.wait_ge(v_ready, NCH)
            pe.wait_ge(qj_ready, NCH)
            pe.wait_ge(qk_ready, 2 * NCH)
            for h in range(HU):
                by_rows(0, 0, 0, h)
            max_transposed(0, 0)
            for h in range(HU):
                by_rows(1, 1, 0, h)
            pe.wait_ge(k_ones, SLOTS)

            def one(b, s, turn):
                for hh in range(2):
                    u, q = 2 * b + hh, 2 * s + hh
                    fixed = isinstance(u, int)
                    pe.wait_ge(max_rows[q], 16 * PARTS * (turn + 1))
                    pe.wait_ge(vb_ready, b + 1)
                    for h in range(HU):
                        by_columns(u, q, h)
                        if not fixed or u + 2 < UNITS:
                            by_rows(u + 2, (q + 2) % SLOTS, turn + s, h)
                        if h == 0 and (not fixed or u + 1 < UNITS):
                            if hh == 0 and (not fixed or b > 1):
                                pe.wait_ge(y_ready, b - 1)
                            if hh == 1 and (not fixed or b > 0):
                                pe.wait_ge(oT_ready, b)
                            max_transposed(u + 1, 1 - hh)
                        if h == 1 and (not fixed or u > 0):
                            pv(u - 1, 1 - hh, s if hh else 1 - s, 1)
                        if h == 4 and hh == 1 and (not fixed or b > 0):
                            if not fixed or u + 1 < UNITS:
                                pe.wait_ge(maxT_ready, u + 2)
                            project(b - 1)
                        if h == 4 and (not fixed or u > 0):
                            to_rows(u - 1, 1 - hh)
                        if h == 5:
                            pv(u, hh, s, 0)
                        if h == 6 and hh == 0 and (not fixed or b > 0):
                            pe.wait_ge(maxT_ready, u + 2)
                            o_transposed(b - 1)

            one(0, 0, 0)
            one(1, 1, 0)
            with pe.Fori(1, NB // 2 - 1) as i:
                for s in range(2):
                    one(2 * i + s, s, i)
            one(NB - 2, 0, NB // 2 - 1)
            one(NB - 1, 1, NB // 2 - 1)
            pv(UNITS - 1, 1, 1, 1)
            to_rows(UNITS - 1, 1)
            o_transposed(NB - 1)
            project(NB - 1)


NE, TOPK, CAP, FF = 64, 8, 160, 384
FT = FF // P
GE = 4
NG = NE // GE
SLOTS_G = 4
GC = GE * CAP // P
GR = GE * CAP
NSLOT = NE * CAP
ROWW = E + NE
NZ = TOK * TOPK
ROUNDS = CAP // 8
CAP_BITS = CAP.bit_length()
SHIFT = 2 ** (CAP_BITS - 1)
FEPS = 1.1920928955078125e-07


def load_group(eng, io, g, W1, W2, loaded):
    eng.dma_start(W1[:], io["w1T"][bass.ds(g, 1)].rearrange("g h e f -> (g h) e f")).then_inc(loaded, 16)
    eng.dma_start(W2[:], io["w2T"][bass.ds(g, 1)].rearrange("g p e j h -> (g p) e j h")).then_inc(loaded, 16)


def route(nc, io, X, ident, rows, slots, tab, ST, W1, W2):
    with ExitStack() as ctx:
        def sb(name, shape, dt=F32):
            return ctx.enter_context(nc.sbuf_tensor("r_" + name, shape, dt))

        def psum(name, shape, dt=F32):
            return ctx.enter_context(nc.psum_tensor("r_" + name, shape, dt))

        sem = ctx.enter_context(semaphores(nc, "r_"))

        Hn = sb("hn", [P, NT, E])
        hT = sb("hT", [P, TOK])
        wg = sb("wg", [P, NE])
        w1, w2 = sb("w1", [P, 2 * FF]), sb("w2", [P, FT, E])
        G, R, M, C = (sb(n, [P, NT, NE]) for n in ("g", "r", "m", "c"))
        Wt = sb("wt", [P, NT, NE])
        top = sb("top", [P, NT, TOPK])
        small = sb("small", [P, 4, NT])
        one = sb("one", [P, 1])
        basei, base = sb("basei", [P, NT], I32), sb("base", [P, NT])
        key = sb("key", [P, NT // 2, 2, NE])
        keyT = sb("keyT", [P, TOK // 2])
        m8 = [sb(f"m8_{i}", [P, 8]) for i in range(2)]
        early = sb("early", [P, CAP])
        late = sb("late", [P, SHIFT + CAP])
        moved, joined, final = sb("moved", [P, CAP]), sb("joined", [P, CAP]), sb("final", [NE, CAP])
        nearly, nearly_i = sb("nearly", [P, 1]), sb("nearly_i", [P, 1], I32)
        bits, bits_i = sb("bits", [P, CAP_BITS]), sb("bits_i", [P, CAP_BITS], I32)
        flat_slots = sb("flat", [NSLOT // P, P])
        dest = sb("dest", [P, NG, GC])
        silu, linear = sb("silu", [P, 2, CH]), sb("linear", [P, 2, CH])
        act_in = sb("act_in", [P, 2, FT, CH])

        pl = psum("pl", [P, NT, NE])
        pt = [psum(f"pt{i}", [P, CH]) for i in range(2)]
        pu = [psum(f"pu{i}", [P, CH]) for i in range(3)]
        pd = psum("pd", [P, CH])

        loaded, prefetched = sem("loaded"), sem("prefetched")
        norms, normed = Norms(sb, sem, 1), sem("normed")
        hT_psum, hT_ready = sem("hT_psum"), sem("hT_ready")
        logits_psum, centred, exp_ready = sem("logits_psum"), sem("centred"), sem("exp_ready")
        base_ready, picked = sem("base_ready"), sem("picked")
        key_ready, keyT_psum = sem("key_ready"), sem("keyT_psum")
        final_ready, slots_out, slots_in, slots_psum = (
            sem("final_ready"), sem("slots_out"), sem("slots_in"), sem("slots_psum"))
        weights_ready, rows_out = sem("weights_ready"), sem("rows_out")
        up_psum, silu_ready, gated, down_psum, down_read = (
            sem("up_psum"), sem("silu_ready"), sem("gated"), sem("down_psum"), sem("down_read"))
        dve_step, dve_passes, pool_step = sem("dve_step"), sem("dve_passes"), sem("pool_step")

        pairs = [(pu[0], pu[1]), (pu[2], pt[1])]

        block = ctx.enter_context(nc.Block())

        @block.sync
        def _(sp):
            for dst, src in ((wg, "wgT"), (w1, "sw1T")):
                sp.dma_start(dst[:], io[src]).then_inc(loaded, 16)
            sp.dma_start(w2[:], io["sw2T"]).then_inc(loaded, 16)
            for g in range(2):
                load_group(sp, io, g, W1[g], W2[g], prefetched)
            out = rows.rearrange("(t p) c -> p t c", p=P)
            sp.wait_ge(normed, NCH)
            sp.dma_start(out[:, :, 0:E], Hn[:]).then_inc(rows_out, 16)
            sp.wait_ge(weights_ready, 1)
            sp.dma_start(out[:, :, E:ROWW], Wt[:]).then_inc(rows_out, 16)
            sp.wait_ge(final_ready, 1)
            sp.dma_start(slots.rearrange("(e c) -> e c", c=CAP), final[:]).then_inc(slots_out, 16)
            sp.wait_ge(slots_out, 16)
            sp.dma_start(flat_slots[:], slots.rearrange("(n p) -> n p", p=P)).then_inc(slots_in, 16)
            sp.wait_ge(rows_out, 32)
            sp.wait_ge(slots_in, 16)
            sp.wait_ge(prefetched, 64)

        @block.gpsimd
        def _(pool):
            step = Steps(pool, pool_step)
            norms.prepare(pool)
            step(pool.memset(one[:], 1.0))
            step.then(pool.iota(basei[:], pattern=[[8 - 8 * P, NT]], base=NZ + 1, channel_multiplier=-8))
            pool.tensor_copy(base[:], basei[:]).then_inc(base_ready, 1)
            norms.roots(pool, step, 0)
            for n in range(NCH * FT):
                c, j = n // FT, n % FT
                pool.wait_ge(silu_ready, n + 1)
                if c > 1 and j == 0:
                    pool.wait_ge(down_psum, c - 1)
                pool.tensor_tensor(act_in[:, c % 2, j, :], silu[:, n % 2], linear[:, n % 2], ALU.mult
                                   ).then_inc(gated, 1)
            pool.wait_ge(picked, 1)
            step.then(pool.tensor_tensor(Wt[:], G[:], M[:], ALU.mult))
            pool.tensor_tensor(Wt[:], Wt[:], per_row(small[:, 2], NE), ALU.mult).then_inc(weights_ready, 1)

        @block.scalar
        def _(act):
            for c in range(NCH):
                act.wait_ge(hT_psum, c + 1)
                act.activation(hT[:, c * CH:(c + 1) * CH], pt[c % 2][:], ACT.Copy).then_inc(hT_ready, 1)
            act.wait_ge(centred, 1)
            act.activation(R[:], G[:], ACT.Exp).then_inc(exp_ready, 1)
            for c in range(NCH):
                for j in range(FT):
                    n = c * FT + j
                    act.wait_ge(up_psum, n + 1)
                    if n > 1:
                        act.wait_ge(gated, n - 1)
                    act.activation(silu[:, n % 2], pairs[n % 2][0][:], ACT.Silu)
                    act.activation(linear[:, n % 2], pairs[n % 2][1][:], ACT.Copy).then_inc(silu_ready, 1)
                act.wait_ge(down_psum, c + 1)
                act.activation(ST[:, c * CH:(c + 1) * CH], pd[:], ACT.Copy).then_inc(down_read, 1)

        @block.vector
        def _(dve):
            v = dve
            step = Steps(dve, dve_step)
            norms.rows(dve, step, 0, X, Hn, normed)
            dve.wait_ge(logits_psum, 1)
            step.then(v.tensor_reduce(small[:, 0], pl[:], AX.X, ALU.max))
            v.tensor_tensor(G[:], pl[:], per_row(small[:, 0], NE), ALU.subtract).then_inc(centred, 1)
            dve.wait_ge(exp_ready, 1)
            step.then(v.tensor_reduce(small[:, 1], R[:], AX.X, ALU.add))
            step.then(v.reciprocal(small[:, 2], small[:, 1]))
            step.then(v.tensor_tensor(G[:], R[:], per_row(small[:, 2], NE), ALU.mult))
            for t in range(NT):
                step(v.max(top[:, t, :], G[:, t, :]))
            step.wait()
            for t in range(NT):
                step(v.match_replace(R[:, t, :], top[:, t, :], G[:, t, :], -1.0))
            step(v.tensor_reduce(small[:, 0], top[:], AX.X, ALU.add))
            step.wait()
            step(v.tensor_scalar(M[:], R[:], 0.0, None, ALU.is_lt))
            step.then(v.tensor_scalar(small[:, 1], small[:, 0], FEPS, None, ALU.max))
            v.reciprocal(small[:, 2], small[:, 1]).then_inc(picked, 1)
            dve.wait_ge(base_ready, 1)
            flat = "p t e -> p (t e)"
            step.then(v.tensor_tensor_scan(C[:].rearrange(flat), one[:].to_broadcast([P, NT * NE]),
                                           M[:].rearrange(flat), 0.0, ALU.mult, ALU.add))
            step.then(v.tensor_tensor(C[:], per_row(base[:], NE), C[:], ALU.subtract))
            v.tensor_tensor(key[:].rearrange("p j h e -> p h j e"), C[:].rearrange("p (h j) e -> p h j e", h=2),
                            M[:].rearrange("p (h j) e -> p h j e", h=2), ALU.mult).then_inc(key_ready, 1)
            dve.wait_ge(keyT_psum, 1)
            step.then(v.tensor_copy(keyT[:], pl[:].rearrange(flat)))

            halves = [keyT[:, i * (TOK // 4):(i + 1) * (TOK // 4)] for i in range(2)]
            behind = late[:, SHIFT:]
            first = step.n
            with dve.Fori(0, ROUNDS) as i:
                done = first + 6 * i
                dve.wait_ge(dve_step, done - 2)
                dve.sem_inc(dve_passes, 1)
                step(v.max(m8[0][:], halves[0]))
                dve.wait_ge(dve_step, done)
                dve.sem_inc(dve_passes, 1)
                step(v.max(m8[1][:], halves[1]))
                dve.wait_ge(dve_step, done + 1)
                step(v.tensor_copy(early[:, bass.ds(8 * i, 8)], m8[0][:]))
                step(v.match_replace(halves[0], m8[0][:], halves[0], 0.0))
                dve.wait_ge(dve_step, done + 2)
                step(v.tensor_copy(late[:, bass.ds(8 * i + SHIFT, 8)], m8[1][:]))
                step(v.match_replace(halves[1], m8[1][:], halves[1], 0.0))
            step.n = first + 6 * ROUNDS
            step.then(v.memset(late[:, 0:SHIFT], 0.0))

            def join(n, early, dst):
                rows_ = slice(0, n)
                step.then(v.tensor_scalar(moved[rows_], early, 0.0, None, ALU.is_gt))
                step.then(v.tensor_reduce(nearly[rows_], moved[rows_], AX.X, ALU.add))
                step.then(v.tensor_copy(nearly_i[rows_], nearly[rows_]))
                for b in range(CAP_BITS):
                    step(v.tensor_single_scalar(bits_i[rows_, b:b + 1], nearly_i[rows_], b, ALU.logical_shift_right))
                step.wait()
                step.then(v.tensor_single_scalar(bits_i[rows_], bits_i[rows_], 1, ALU.bitwise_and))
                step.then(v.tensor_copy(bits[rows_], bits_i[rows_]))
                for b in range(CAP_BITS):
                    at = slice(SHIFT - 2 ** b, SHIFT - 2 ** b + CAP)
                    step.then(v.tensor_tensor(moved[rows_], late[rows_, at], behind[rows_], ALU.subtract))
                    step.then(v.scalar_tensor_tensor(behind[rows_], moved[rows_], bits[rows_, b:b + 1], behind[rows_],
                                                     ALU.mult, ALU.add))
                return v.tensor_tensor(dst[:], early, behind[rows_], ALU.add)

            step.then(join(P, early[:], joined))
            step.then(v.tensor_copy(behind[0:NE], joined[NE:2 * NE, :]))
            join(NE, joined[0:NE, :], final).then_inc(final_ready, 1)
            dve.wait_ge(slots_psum, 1)
            keys = pd[:, 0:NG * GC].rearrange("p (g c) -> p g c", c=GC)
            step.then(v.tensor_scalar(dest[:], keys, -1.0, float(NZ), ALU.mult, ALU.add))
            step(v.tensor_copy(tab[:, :, 1, :], dest[:]))
            step.wait()
            step.then(v.tensor_scalar(dest[:], dest[:], float(NZ - 1), None, ALU.min))
            step.then(v.tensor_copy(tab[:, :, 0, :], dest[:]))
            step.then(v.tensor_single_scalar(tab[:, :, 0, :], tab[:, :, 0, :], 3, ALU.logical_shift_right))

        @block.tensor
        def _(pe):
            pe.wait_ge(loaded, 16 * 3)
            for c in range(NCH):
                pe.wait_ge(normed, c + 1)
                if c >= 2:
                    pe.wait_ge(hT_ready, c - 1)
                for j in range(TPC):
                    t = pe.transpose(pt[c % 2][:, j * P:(j + 1) * P], Hn[:, c * TPC + j, :], ident[:])
                t.then_inc(hT_psum, 1)
            pe.wait_ge(hT_ready, NCH)
            for t in range(NT):
                m = pe.matmul(pl[:, t, :], hT[:, t * P:(t + 1) * P], wg[:], start=True, stop=True)
            m.then_inc(logits_psum, 1)
            for c in range(NCH):
                at = slice(c * CH, (c + 1) * CH)
                for j in range(FT):
                    n = c * FT + j
                    if n > 1:
                        pe.wait_ge(silu_ready, n - 1)
                    pe.matmul(pairs[n % 2][0][:], w1[:, FF + j * P:FF + (j + 1) * P], hT[:, at],
                              start=True, stop=True)
                    pe.matmul(pairs[n % 2][1][:], w1[:, j * P:(j + 1) * P], hT[:, at],
                              start=True, stop=True).then_inc(up_psum, 1)
                if c == 1:
                    pe.wait_ge(key_ready, 1)
                    flat = pl[:].rearrange("p t e -> p (t e)")
                    for j in range(NT // 2):
                        m = pe.transpose(flat[:, j * P:(j + 1) * P], key[:, j].rearrange("p h e -> p (h e)"), ident[:])
                    m.then_inc(keyT_psum, 1)
                pe.wait_ge(gated, (c + 1) * FT)
                if c:
                    pe.wait_ge(down_read, c)
                for j in range(FT):
                    m = pe.matmul(pd[:], w2[:, j, :], act_in[:, c % 2, j, :], start=(j == 0), stop=(j == FT - 1))
                m.then_inc(down_psum, 1)
            pe.wait_ge(down_read, NCH)
            pe.wait_ge(slots_in, 16)
            pe.transpose(pd[:, 0:NSLOT // P], flat_slots[:], ident[0:NSLOT // P, 0:NSLOT // P]).then_inc(slots_psum, 1)


def experts(nc, io, ident, rows, results, tab, W1, W2):
    with ExitStack() as ctx:
        def sb(name, shape, dt=F32):
            return ctx.enter_context(nc.sbuf_tensor("e_" + name, shape, dt))

        def psum(name, shape, dt=F32):
            return ctx.enter_context(nc.psum_tensor("e_" + name, shape, dt))

        sem = ctx.enter_context(semaphores(nc, "e_"))

        idx_in, idx_out = ([sb(f"{n}{i}", [P, GC], I32) for i in range(SLOTS_G)] for n in ("idx_in", "idx_out"))
        G = [sb(f"g{i}", [P, GC, ROWW]) for i in range(SLOTS_G)]
        GT = [sb(f"gt{i}", [P, GR]) for i in range(2)]
        own = sb("own", [P, GC, GE])
        wsel = sb("wsel", [P, GC, GE])
        wrow = [sb(f"wrow{i}", [P, GC]) for i in range(2)]
        silu = sb("silu", [P, 2, FT, CAP])
        A = sb("a", [P, 2, FT, CAP])
        D_ = sb("d", [P, GR])
        out = [sb(f"out{i}", [P, GC, E]) for i in range(2)]

        px1 = [psum(f"px1_{i}", [P, FT, CAP]) for i in range(2)]
        px2 = [psum(f"px2_{i}", [P, FT, CAP]) for i in range(2)]
        pd = [psum(f"pd{i}", [P, 2, CAP]) for i in range(2)]
        pt = psum("pt", [P, 8, P])

        loaded = [sem("loaded0"), sem("loaded1")]
        own_ready = sem("own_ready")
        idx_ready, weighed = sem("idx_ready"), sem("weighed")
        gathered = [sem(f"gathered{i}") for i in range(SLOTS_G)]
        in_psum, in_ready = sem("in_psum"), sem("in_ready")
        up_psum, silu_ready, gated, down_psum, down_ready = (
            sem("up_psum"), sem("silu_ready"), sem("gated"), sem("down_psum"), sem("down_ready"))
        out_psum, out_ready, scattered = sem("out_psum"), sem("out_ready"), [sem("scattered0"), sem("scattered1")]
        dve_step, pool_passes = sem("dve_step"), sem("pool_passes")

        block = ctx.enter_context(nc.Block())

        def groups(eng, one):
            for g in range(SLOTS_G):
                one(g, g, 0)
            with eng.Fori(1, NG // SLOTS_G - 1) as i:
                for s in range(SLOTS_G):
                    one(SLOTS_G * i + s, s, i)
            for g in range(NG - SLOTS_G, NG):
                one(g, g % SLOTS_G, g // SLOTS_G)

        @block.sync
        def _(sp):
            sp.dma_start(own[:], io["own"]).then_inc(own_ready, 16)
            with sp.Fori(0, NG // 2 - 1) as i:
                for s in range(2):
                    sp.wait_ge(down_psum, GE * (2 * i + s + 1))
                    load_group(sp, io, 2 * i + s + 2, W1[s], W2[s], loaded[s])

        @block.gpsimd
        def _(pool):
            def indices(dst, g, which, count):
                pool.tensor_copy(dst[:], tab[:, bass.ds(g, 1), which].rearrange("p g c -> p (g c)")
                                 ).then_inc(idx_ready, 1)
                pool.wait_ge(idx_ready, count + 1)
                pool.sem_inc(pool_passes, 1)

            def gather(g, s, k, count):
                if not isinstance(g, int) or g >= SLOTS_G:
                    pool.wait_ge(in_psum, g - SLOTS_G + 1)
                    pool.wait_ge(weighed, g - SLOTS_G + 1)
                indices(idx_in[s], g, 0, count)
                for c in range(GC):
                    pool.indirect_dma_start(G[s][:, c, :], None, rows,
                                            bass.IndirectOffsetOnAxis(ap=idx_in[s][:, c:c + 1], axis=0)
                                            ).then_inc(gathered[s], 16)

            def scatter(g, s, k, count):
                if not isinstance(g, int) or g >= SLOTS_G:
                    pool.wait_ge(scattered[s % 2], 16 * GC * (2 * k + s // 2 - 1))
                indices(idx_out[s], g, 1, count)
                pool.wait_ge(out_ready, g + 1)
                pool.sem_inc(pool_passes, 1)
                for c in range(GC):
                    pool.indirect_dma_start(results, bass.IndirectOffsetOnAxis(ap=idx_out[s][:, c:c + 1], axis=0),
                                            out[s % 2][:, c, :], None, bounds_check=NZ - 1, oob_is_err=False
                                            ).then_inc(scattered[s % 2], 16)

            lead = SLOTS_G - 1
            for g in range(lead):
                gather(g, g, 0, g)

            def one(g, s, k):
                ahead = not isinstance(g, int) or g + lead < NG
                if ahead:
                    gather(g + lead, (s + lead) % SLOTS_G, k + (s + lead) // SLOTS_G, 2 * g + lead)
                scatter(g, s, k, 2 * g + lead + 1 if ahead else g + NG)

            groups(pool, one)
            for s in range(2):
                pool.wait_ge(scattered[s], 16 * GC * NG // 2)

        @block.scalar
        def _(act):
            def turned(g, s):
                act.wait_ge(in_psum, g + 1)
                act.activation(GT[s % 2][:], pt[:, 0:GC].rearrange("p c r -> p (c r)"), ACT.Copy).then_inc(in_ready, 1)

            def silus(g, e, first):
                n = GE * g + e
                act.wait_ge(up_psum, n + 1)
                if not (first and e < 2):
                    act.wait_ge(gated, n - 1)
                act.activation(silu[:, e % 2], px2[e % 2][:], ACT.Silu).then_inc(silu_ready, 1)

            def downs(g, j, first):
                act.wait_ge(down_psum, GE * g + 2 * j + 2)
                if not first:
                    act.wait_ge(out_psum, g)
                act.activation(D_[:, 2 * j * CAP:(2 * j + 2) * CAP], pd[j][:].rearrange("p e c -> p (e c)"),
                               ACT.Copy).then_inc(down_ready, 1)

            turned(0, 0)
            silus(0, 0, True)

            def one(g, s, k):
                first, last = isinstance(g, int) and g == 0, isinstance(g, int) and g == NG - 1
                for e in range(GE):
                    if not (last and e == 3):
                        silus(g if e < 3 else g + 1, (e + 1) % GE, first and e < 3)
                    if e == 2 and not last:
                        turned(g + 1, s + 1)
                    if e == 2:
                        downs(g, 0, first)
                downs(g, 1, first)

            groups(act, one)

        @block.vector
        def _(dve):
            v = dve
            dve.wait_ge(own_ready, 16)

            def gate(g, e, first):
                n = GE * g + e
                dve.wait_ge(silu_ready, n + 1)
                if not (first and e < 2):
                    dve.wait_ge(down_psum, n - 1)
                v.tensor_tensor(A[:, e % 2], px1[e % 2][:], silu[:, e % 2], ALU.mult).then_inc(gated, 1)

            def finish(g, s, k):
                dve.wait_ge(out_psum, g + 1)
                if not (isinstance(g, int) and g < 2):
                    dve.wait_ge(scattered[s % 2], 16 * GC * (2 * k + s // 2))
                v.tensor_tensor(out[s % 2][:], pt[:, 0:GC], per_row(wrow[s % 2][:], E), ALU.mult
                                ).then_inc(out_ready, 1)

            def weigh(g, s, k):
                dve.wait_ge(gathered[s], 16 * GC * (k + 1))
                v.tensor_tensor(wsel[:], G[s][:, :, bass.ds(E + GE * g, GE)], own[:], ALU.mult).then_inc(dve_step, 1)
                dve.wait_ge(dve_step, g + 1)
                v.tensor_reduce(wrow[s % 2][:], wsel[:], AX.X, ALU.add).then_inc(weighed, 1)

            weigh(0, 0, 0)
            gate(0, 0, True)

            def one(g, s, k):
                first, last = isinstance(g, int) and g == 0, isinstance(g, int) and g == NG - 1
                for e in range(GE):
                    if not (last and e == 3):
                        gate(g if e < 3 else g + 1, (e + 1) % GE, first and e < 3)
                    if e == 1 and not first:
                        finish(g - 1, (s - 1) % SLOTS_G, k if s else k - 1)
                    if e == 2 and not last:
                        weigh(g + 1, (s + 1) % SLOTS_G, k + (s + 1) // SLOTS_G)

            groups(dve, one)
            finish(NG - 1, SLOTS_G - 1, NG // SLOTS_G - 1)

        @block.tensor
        def _(pe):
            def turn(g, s, k):
                pe.wait_ge(gathered[s], 16 * GC * (k + 1))
                for c in range(GC):
                    m = pe.transpose(pt[:, c, :], G[s][:, c, 0:E], ident[:])
                m.then_inc(in_psum, 1)

            def up(g, s, k, e, first):
                n, slot = GE * g + e, s % 2
                if e == 0:
                    pe.wait_ge(in_ready, g + 1)
                    if not (isinstance(g, int) and g < 2):
                        pe.wait_ge(loaded[slot], 32 * (2 * k + s // 2))
                if not (first and e < 2):
                    pe.wait_ge(gated, n - 1)
                at = slice(e * CAP, (e + 1) * CAP)
                for j in range(FT):
                    pe.matmul(px2[e % 2][:, j, :], W1[slot][:, e, FF + j * P:FF + (j + 1) * P], GT[slot][:, at],
                              start=True, stop=True)
                for j in range(FT):
                    m = pe.matmul(px1[e % 2][:, j, :], W1[slot][:, e, j * P:(j + 1) * P], GT[slot][:, at],
                                  start=True, stop=True)
                m.then_inc(up_psum, 1)

            def down(g, slot, e, first):
                n = GE * g + e
                pe.wait_ge(gated, n + 1)
                if e % 2 == 0 and not first:
                    pe.wait_ge(down_ready, 2 * g - 1 + e // 2)
                for j in range(FT):
                    m = pe.matmul(pd[e // 2][:, e % 2, :], W2[slot][:, e, j, :], A[:, e % 2, j, :],
                                  start=(j == 0), stop=(j == FT - 1))
                m.then_inc(down_psum, 1)

            def turn_out(g):
                pe.wait_ge(down_ready, 2 * g + 2)
                for c in range(GC):
                    m = pe.transpose(pt[:, c, :], D_[:, c * P:(c + 1) * P], ident[:])
                m.then_inc(out_psum, 1)

            turn(0, 0, 0)
            up(0, 0, 0, 0, True)

            def one(g, s, k):
                first, last = isinstance(g, int) and g == 0, isinstance(g, int) and g == NG - 1
                after = (s + 1) % SLOTS_G, k + (s + 1) // SLOTS_G
                for e in range(GE):
                    if not (last and e == 3):
                        if e < 3:
                            up(g, s, k, e + 1, first)
                        else:
                            up(g + 1, *after, 0, False)
                    if e == 2 and not last:
                        if not first:
                            pe.wait_ge(out_ready, g)
                        turn(g + 1, *after)
                    if e == 1 and not first:
                        pe.wait_ge(in_ready, g + 1)
                        turn_out(g - 1)
                    down(g, s % 2, e, first)

            groups(pe, one)
            turn_out(NG - 1)


def combine(nc, io, X, ident, results, ST):
    with ExitStack() as ctx:
        def sb(name, shape, dt=F32):
            return ctx.enter_context(nc.sbuf_tensor("c_" + name, shape, dt))

        sem = ctx.enter_context(semaphores(nc, "c_"))
        norms = Norms(sb, sem, 1)

        Z = sb("z", [P, NT, TOPK, E])
        Y = sb("y", [P, NT, E])
        odd = sb("odd", [P, NT // 2, E])
        ps = [ctx.enter_context(nc.psum_tensor(f"c_ps{i}", [P, TPC, E], F32)) for i in range(NCH)]
        loaded = [sem(f"loaded{t}") for t in range(NT)]
        summed, sums_read, x_done = sem("summed"), sem("sums_read"), sem("x_done")
        dve_step, pool_step = sem("dve_step"), sem("pool_step")
        block = ctx.enter_context(nc.Block())

        @block.sync
        def _(sp):
            z = results.rearrange("(t p k) e -> t p k e", p=P, k=TOPK)
            for t in range(NT):
                sp.dma_start(Z[:, t], z[t]).then_inc(loaded[t], 16)

        @block.tensor
        def _(pe):
            for c in range(NCH):
                for j in range(TPC):
                    t = c * TPC + j
                    if t % 2 == 0:
                        pe.wait_ge(loaded[t], 16)
                        for k in range(TOPK):
                            pe.matmul(ps[c][:, j, :], ident[:], Z[:, t, k, :], start=(k == 0), stop=False)
                    m = pe.matmul(ps[c][:, j, :], ST[:, t * P:(t + 1) * P], ident[:], start=(t % 2 == 1), stop=True)
                m.then_inc(summed, 1)

        @block.gpsimd
        def _(pool):
            step = Steps(pool, pool_step)
            norms.prepare(pool)
            norms.roots(pool, step, 0)

        @block.scalar
        def _(act):
            for c in range(NCH):
                act.wait_ge(summed, c + 1)
                act.activation(Y[:, c * TPC:(c + 1) * TPC], ps[c][:], ACT.Copy).then_inc(sums_read, 1)

        @block.vector
        def _(dve):
            step = Steps(dve, dve_step)

            def residual(c):
                norms.residual(dve, step, 0, c, Y, X, x_done)

            for c in range(NCH):
                for t in range(c * TPC + 1, (c + 1) * TPC, 2):
                    dve.wait_ge(loaded[t], 16)
                    step(dve.tensor_reduce(odd[:, t // 2, :], Z[:, t].rearrange("p k e -> p e k"), AX.X, ALU.add))
                step.wait()
                dve.wait_ge(sums_read, c + 1)
                tiles = Y[:, c * TPC:(c + 1) * TPC].rearrange("p (t two) e -> p t two e", two=2)
                step.then(dve.tensor_tensor(tiles[:, :, 1], tiles[:, :, 1],
                                            odd[:, c * TPC // 2:(c + 1) * TPC // 2], ALU.add))
                norms.statistics(dve, step, 0, c, Y)
                if c:
                    residual(c - 1)
            residual(NCH - 1)


DI, DS, DR, DC = 256, 16, 8, 4
DH = DI // P
PAD = DC - 1
TH = TOK // 2
HB = TH // S
HCH = TH // CH
BCR = 3 * 2 * DS


def mamba(nc, io, X, ident):
    with ExitStack() as ctx:
        def sb(name, shape, dt=F32):
            return ctx.enter_context(nc.sbuf_tensor("m_" + name, shape, dt))

        def psum(name, shape, dt=F32):
            return ctx.enter_context(nc.psum_tensor("m_" + name, shape, dt))

        sem = ctx.enter_context(semaphores(nc, "m_"))

        N1, N2 = sb("n1", [P, NT, E]), sb("n2", [P, NT, E])
        sq, srw = sb("sq", [P, E]), sb("srw", [P, E])
        win = sb("win", [P, 2 * DI])
        wconv = sb("wconv", [P, DC, P])
        taps = sb("taps", [P, DC])
        wx = sb("wx", [P, DH, BCR + DR])
        wdt = sb("wdt", [DR, DI])
        wout = sb("wout", [P, DH, E])
        vec = sb("vec", [P, 16])
        alog = sb("alog", [P, DH, DS])
        expA, negA = sb("expa", [P, DH, DS]), sb("nega", [P, DH, DS])
        pick = sb("pick", [BCR, 2 * DS], BF16)
        pickf = sb("pickf", [BCR, 2 * DS])
        diagD = sb("diagd", [P, DH, P])
        gT = sb("gt", [P, NCH, CH])
        hP = sb("hp", [P, NB, PAD + S])
        U, SZ, delta, du = (sb(n, [P, DH, TOK]) for n in ("u", "sz", "delta", "du"))
        dtT = sb("dtT", [DR, TOK])
        BC = sb("bc", [BCR, TOK], BF16)
        rest = sb("rest", [BCR, CH])
        tmp = sb("tmp", [BCR, CH], BF16)
        Bn, Cn = ([sb(f"{n}{i}", [P, TH]) for i in range(2)] for n in ("bn", "cn"))
        dA = [[sb(f"da{i}{h}", [P, HB, S]) for h in range(DH)] for i in range(2)]
        dBu = [[sb(f"dbu{i}{h}", [P, TH]) for h in range(DH)] for i in range(2)]
        hst = [sb(f"h{h}", [P, TH]) for h in range(DH)]
        hC = [[sb(f"hc{i}{h}", [P, TH]) for h in range(DH)] for i in range(2)]

        acc = [psum(f"acc{i}", [P, CH]) for i in range(4)]
        pB, pC = psum("pb", [P, TH]), psum("pc", [P, TH])
        bank = [x[:] for x in acc] + [x[:, c * CH:(c + 1) * CH] for x in (pB, pC) for c in range(HCH)]
        vecs = {"g": 0, "b": 1, "sq_b": 2, "srw_b": 3, "scale": 4, "conv_b": 6, "dt_b": 8, "D": 10}

        def col(name, i=0):
            return vec[:, vecs[name] + i:vecs[name] + i + 1]

        def halves(x):
            return x.rearrange("p (h t) -> p h t", h=DH)

        loaded = sem("loaded")
        norms, n1_ready, n2_ready, x_done = Norms(sb, sem, 3), sem("n1_ready"), sem("n2_ready"), sem("x_done")
        hT_psum, gT_ready, sq_psum, hP_ready = sem("hT_psum"), sem("gT_ready"), sem("sq_psum"), sem("hP_ready")
        padded, taps_ready = sem("padded"), sem("taps_ready")
        conv_ready = sem("conv_ready")
        u_psum, u_ready, z_psum, z_ready = sem("u_psum"), sem("u_ready"), sem("z_psum"), sem("z_ready")
        dbc_psum, dt_ready, bc_read, bc_ready = sem("dbc_psum"), sem("dt_ready"), sem("bc_read"), sem("bc_ready")
        dl_psum, dl_read, e_ready, ln_ready, delta_ready = (
            sem("dl_psum"), sem("dl_read"), sem("e_ready"), sem("ln_ready"), sem("delta_ready"))
        du_ready, diag_ready, expA_ready, dA_zero = (
            sem("du_ready"), sem("diag_ready"), sem("expA_ready"), sem("dA_zero"))
        negA_ready = sem("negA_ready")
        b_psum, c_psum, b_ready, c_ready = sem("b_psum"), sem("c_psum"), sem("b_ready"), sem("c_ready")
        dA_ready, dBu_ready, h_ready, hC_ready, hC_used = (
            sem("dA_ready"), sem("dBu_ready"), sem("h_ready"), sem("hC_ready"), sem("hC_used"))
        y_gated, out_psum, out_ready = sem("y_gated"), sem("out_psum"), sem("out_ready")
        srw_psum, g_ready, tok_psum, tok_read = sem("srw_psum"), sem("g_ready"), sem("tok_psum"), sem("tok_read")
        dve_step, pool_step, act_step = sem("dve_step"), sem("pool_step"), sem("act_step")

        block = ctx.enter_context(nc.Block())
        NLOAD = 21

        def over_states(eng, one):
            one(0, 0)
            one(1, 1)
            with eng.Fori(1, DS // 2 - 1) as i:
                for s in range(2):
                    one(2 * i + s, s)
            one(DS - 2, 0)
            one(DS - 1, 1)

        def over_chunks(u, dbc, dl):
            for c in range(NCH + 2):
                if c < NCH:
                    u(c)
                if 0 < c <= NCH:
                    dbc(c - 1)
                if c > 1:
                    dl(c - 2)

        @block.sync
        def _(sp):
            for dst, src in ((sq, "sq_w"), (srw, "srw_w"), (win, "in_proj_w"), (wdt, "dt_w"), (pickf, "pick")):
                sp.dma_start(dst[:], io[src]).then_inc(loaded, 16)
            sp.dma_start(wx[:], io["x_proj"].rearrange("(h p) c -> p h c", p=P)).then_inc(loaded, 16)
            sp.dma_start(wout[:], io["out_proj_w"].rearrange("(h p) c -> p h c", p=P)).then_inc(loaded, 16)
            sp.dma_start(alog[:], io["A_log"].rearrange("(h p) c -> p h c", p=P)).then_inc(loaded, 16)
            sp.dma_start(wconv[:], io["conv_wT"][:, 0:P].unsqueeze(0).to_broadcast([P, DC, P])).then_inc(loaded, 16)
            sp.dma_start(taps[:], io["conv_w"][P:DI]).then_inc(loaded, 16)
            for n in ("g", "b", "sq_b", "srw_b"):
                sp.dma_start(col(n), io["m_" + n].unsqueeze(1)).then_inc(loaded, 16)
            sp.dma_start(col("scale"), io["res_scale"].unsqueeze(1).to_broadcast([P, 1])).then_inc(loaded, 16)
            for n in ("conv_b", "dt_b", "D"):
                for h in range(DH):
                    sp.dma_start(col(n, h), io["m_" + n][h * P:(h + 1) * P].unsqueeze(1)).then_inc(loaded, 16)
            sp.wait_ge(loaded, 16 * NLOAD)

        @block.gpsimd
        def _(pool):
            step = Steps(pool, pool_step)
            norms.prepare(pool)
            pool.memset(hP[:, :, 0:PAD], 0.0).then_inc(padded, 1)
            for i in range(2):
                for h in range(DH):
                    pool.memset(dA[i][h][:, :, 0:1], 0.0).then_inc(dA_zero, 1)
            norms.roots(pool, step, 0)
            norms.roots(pool, step, 1)
            pool.wait_ge(loaded, 16 * NLOAD)
            for h in range(DH):
                pool.tensor_scalar(diagD[:, h], ident[:], col("D", h), 1.0, ALU.mult, ALU.mult).then_inc(diag_ready, 1)
            pool.wait_ge(expA_ready, 1)
            pool.tensor_scalar(negA[:], expA[:], -1.0, 1.0, ALU.mult, ALU.mult).then_inc(negA_ready, 1)

            def delta_u(c):
                pool.wait_ge(delta_ready, c + 1)
                at = slice(c * CH, (c + 1) * CH)
                pool.tensor_tensor(du[:, :, at], delta[:, :, at], U[:, :, at], ALU.mult).then_inc(du_ready, 1)

            for c in range(HCH):
                delta_u(c)
            pool.wait_ge(du_ready, HCH)
            for hf in range(2):
                def one(n, s):
                    m = hf * DS + n
                    for h in range(DH):
                        k = m * DH + h
                        pool.wait_ge(b_ready, m + 1)
                        if not (isinstance(m, int) and m < 2):
                            pool.wait_ge(h_ready, k - 2 * DH + 1)
                        pool.tensor_tensor(dBu[s][h][:], du[:, h, hf * TH:(hf + 1) * TH], Bn[s][:], ALU.mult
                                           ).then_inc(dBu_ready, 1)
                    if hf == 0 and isinstance(n, int) and n == 0:
                        for c in range(HCH, NCH):
                            delta_u(c)
                        pool.wait_ge(du_ready, NCH)

                over_states(pool, one)
            norms.roots(pool, step, 2)

        @block.scalar
        def _(act):
            step = Steps(act, act_step)
            act.wait_ge(loaded, 16 * NLOAD)
            step.then(act.activation(pick[:], pickf[:], ACT.Copy))
            for c in range(NCH):
                act.wait_ge(hT_psum, c + 1)
                act.activation(gT[:, c], bank[c % 2], ACT.Identity, bias=col("b"), scale=col("g")
                               ).then_inc(gT_ready, 1)

            def u(c):
                at = slice(c * CH, (c + 1) * CH)
                act.wait_ge(u_psum, DH * c + 1)
                act.activation(U[:, 0, at], bank[4 + 2 * (c % 2)], ACT.Silu, bias=col("conv_b", 0)
                               ).then_inc(u_ready, 1)
                act.wait_ge(conv_ready, c + 1)
                act.activation(U[:, 1, at], dBu[0][c % 2][:, 0:CH], ACT.Silu).then_inc(u_ready, 1)

            def dt(c):
                act.wait_ge(dbc_psum, c + 1)
                act.activation(dtT[:, c * CH:(c + 1) * CH], bank[c % 2][BCR:BCR + DR, :], ACT.Copy
                               ).then_inc(dt_ready, 1)

            def dl(c):
                at = slice(c * CH, (c + 1) * CH)
                for h in range(DH):
                    act.wait_ge(dl_psum, DH * c + h + 1)
                    act.activation(delta[:, h, at], bank[2 + h], ACT.Identity, bias=col("dt_b", h)
                                   ).then_inc(act_step, 1)
                    act.activation(du[:, h, at], bank[2 + h], ACT.Abs, bias=col("dt_b", h)).then_inc(dl_read, 1)

            over_chunks(u, dt, dl)
            act.wait_ge(dl_read, DH * NCH)
            for c in range(NCH):
                at = slice(c * CH, (c + 1) * CH)
                act.activation(du[:, :, at], du[:, :, at], ACT.Exp, scale=-1.0).then_inc(e_ready, 1)
            act.activation(expA[:], alog[:], ACT.Exp).then_inc(expA_ready, 1)
            for c in range(NCH):
                act.wait_ge(e_ready, c + 1)
                act.activation(halves(hC[c // 2][c % 2][:]), du[:, :, c * CH:(c + 1) * CH], ACT.Ln, bias=1.0
                               ).then_inc(ln_ready, 1)
            for i in range(DH * NCH):
                c, h = i // DH, i % DH
                act.wait_ge(z_psum, i + 1)
                act.activation(SZ[:, h, c * CH:(c + 1) * CH], bank[4 + i % 4], ACT.Silu).then_inc(z_ready, 1)
            act.wait_ge(dA_zero, 2 * DH)
            act.wait_ge(negA_ready, 1)
            for hf in range(2):
                act.wait_ge(delta_ready, HCH * (hf + 1))

                def one(n, s):
                    m = hf * DS + n
                    early = isinstance(m, int) and m < 2
                    act.wait_ge(b_psum, m + 1)
                    if not early:
                        act.wait_ge(dBu_ready, DH * (m - 1))
                    act.activation(Bn[s][:], pB[:], ACT.Copy).then_inc(b_ready, 1)
                    for h in range(DH):
                        k = m * DH + h
                        if not early:
                            act.wait_ge(h_ready, k - 2 * DH + 1)
                        act.activation(dA[s][h][:, :, 1:S],
                                       delta[:, h, hf * TH:(hf + 1) * TH].rearrange("p (b t) -> p b t", t=S)[:, :, 1:S],
                                       ACT.Exp, scale=negA[:, h, bass.ds(n, 1)]).then_inc(dA_ready, 1)
                    act.wait_ge(c_psum, m + 1)
                    if isinstance(m, int) and m == 0:
                        act.wait_ge(delta_ready, NCH)
                    if not early:
                        act.wait_ge(hC_ready, DH * (m - 1))
                    act.activation(Cn[s][:], pC[:], ACT.Copy).then_inc(c_ready, 1)

                over_states(act, one)
            for c in range(NCH):
                act.wait_ge(out_psum, c + 1)
                act.activation(gT[:, c], bank[c], ACT.Copy).then_inc(out_ready, 1)

        @block.vector
        def _(dve):
            v = dve
            step = Steps(dve, dve_step)
            norms.rows(dve, step, 0, X, N1, n1_ready)
            for c in range(NCH):
                dve.wait_ge(n1_ready, c + 1)
                norms.statistics(dve, step, 1, c, N1)
            for c in range(NCH):
                norms.apply(dve, 1, c, N1, N2).then_inc(n2_ready, 1)
            dve.wait_ge(loaded, 16 * NLOAD)
            v.tensor_tensor(wconv[:], wconv[:], win[:, 0:P].unsqueeze(1).to_broadcast([P, DC, P]), ALU.mult
                            ).then_inc(taps_ready, 1)
            for c in range(NCH):
                dve.wait_ge(sq_psum, c + 1)
                dve.wait_ge(padded, 1)
                v.scalar_tensor_tensor(hP[:, 2 * c:2 * c + 2, PAD:PAD + S],
                                       bank[2 + c % 2].rearrange("p (b t) -> p b t", t=S), col("sq_b"),
                                       gT[:, c].rearrange("p (b t) -> p b t", t=S), ALU.add, ALU.add
                                       ).then_inc(hP_ready, 1)

            def convolve(c):
                dve.wait_ge(u_psum, DH * (c + 1))
                if c > 1:
                    dve.wait_ge(u_ready, DH * (c - 1))
                raw = bank[4 + 2 * (c % 2) + 1].rearrange("p (b t) -> p b t", t=S)
                u = dBu[0][c % 2][:, 0:CH].rearrange("p (b t) -> p b t", t=S)
                step.then(v.tensor_scalar(u, raw, taps[:, DC - 1:DC], col("conv_b", 1), ALU.mult, ALU.add))
                for k in range(DC - 1):
                    back = DC - 1 - k
                    x = v.scalar_tensor_tensor(u[:, :, back:], raw[:, :, 0:S - back], taps[:, k:k + 1],
                                               u[:, :, back:], ALU.mult, ALU.add)
                    if k < DC - 2:
                        step.then(x)
                x.then_inc(conv_ready, 1)

            def b_and_c(c):
                at = slice(c * CH, (c + 1) * CH)
                dve.wait_ge(dbc_psum, c + 1)
                dve.wait_ge(dt_ready, c + 1)
                step.then(v.tensor_copy(BC[:, at], bank[c % 2][0:BCR, :]))
                v.tensor_tensor(rest[:], bank[c % 2][0:BCR, :], BC[:, at], ALU.subtract).then_inc(bc_read, 1)
                dve.wait_ge(bc_read, c + 1)
                step(v.tensor_copy(BC[32:64, at], rest[32:64, :]))
                step.then(v.tensor_copy(tmp[64:96, :], rest[64:96, :]))
                v.tensor_tensor(BC[64:96, at], rest[64:96, :], tmp[64:96, :], ALU.subtract).then_inc(bc_ready, 1)
                dve.wait_ge(bc_ready, c + 1)

            over_chunks(convolve, b_and_c, lambda c: None)
            lost = [halves(x[:]) for x in (*hst, *Cn)]
            for c in range(NCH):
                at = slice(c * CH, (c + 1) * CH)
                dve.wait_ge(e_ready, c + 1)
                step.then(v.tensor_scalar(lost[c], du[:, :, at], 1.0, -1.0, ALU.add, ALU.add))
                step.then(v.tensor_tensor(lost[c], du[:, :, at], lost[c], ALU.subtract))
            for c in range(NCH):
                at = slice(c * CH, (c + 1) * CH)
                dve.wait_ge(ln_ready, c + 1)
                step.then(v.tensor_tensor(lost[c], lost[c], halves(hC[c // 2][c % 2][:]), ALU.add))
                v.scalar_tensor_tensor(delta[:, :, at], delta[:, :, at], 0.0, lost[c], ALU.max, ALU.add
                                       ).then_inc(delta_ready, 1)
            dve.wait_ge(delta_ready, NCH)
            for hf in range(2):
                def one(n, s):
                    m = hf * DS + n
                    early = isinstance(m, int) and m < 2
                    for h in range(DH):
                        k = m * DH + h
                        dve.wait_ge(dA_ready, k + 1)
                        dve.wait_ge(dBu_ready, k + 1)
                        if not (isinstance(m, int) and m < 1):
                            dve.wait_ge(hC_ready, k - DH + 1)
                        v.tensor_tensor_scan(hst[h][:], dA[s][h][:].rearrange("p b t -> p (b t)"), dBu[s][h][:], 0.0,
                                             ALU.mult, ALU.add).then_inc(h_ready, 1)
                    for h in range(DH):
                        k = m * DH + h
                        dve.wait_ge(h_ready, k + 1)
                        dve.wait_ge(c_ready, m + 1)
                        if not early:
                            dve.wait_ge(hC_used, k - 2 * DH + 1)
                        v.tensor_tensor(hC[s][h][:], hst[h][:], Cn[s][:], ALU.mult).then_inc(hC_ready, 1)

                over_states(dve, one)
                dve.wait_ge(hC_used, DS * DH * (hf + 1))
                dve.wait_ge(z_ready, DH * NCH)
                for h in range(DH):
                    for c in range(HCH):
                        at = slice(hf * TH + c * CH, hf * TH + (c + 1) * CH)
                        v.tensor_tensor(SZ[:, h, at], SZ[:, h, at], acc[2 * h + c][:], ALU.mult).then_inc(y_gated, 1)

            def gate(c):
                dve.wait_ge(srw_psum, c + 1)
                v.scalar_tensor_tensor(U[:, 0, c * CH:(c + 1) * CH], bank[4 + c], col("srw_b"), gT[:, c],
                                       ALU.add, ALU.mult).then_inc(g_ready, 1)

            gate(0)
            for c in range(NCH):
                if c + 1 < NCH:
                    gate(c + 1)
                at = slice(c * TPC, (c + 1) * TPC)
                dve.wait_ge(tok_psum, c + 1)
                v.scalar_tensor_tensor(N2[:, at], bank[c].rearrange("p (t e) -> p t e", e=E), col("scale"), N1[:, at],
                                       ALU.mult, ALU.add).then_inc(tok_read, 1)
                dve.wait_ge(tok_read, c + 1)
                norms.statistics(dve, step, 2, c, N2)
                if c:
                    norms.residual(dve, step, 2, c - 1, N2, X, x_done)
            norms.residual(dve, step, 2, NCH - 1, N2, X, x_done)

        @block.tensor
        def _(pe):
            pe.wait_ge(loaded, 16 * NLOAD)

            def turn(c):
                pe.wait_ge(n2_ready, c + 1)
                if c > 1:
                    pe.wait_ge(gT_ready, c - 1)
                for j in range(TPC):
                    m = pe.transpose(bank[c % 2][:, j * P:(j + 1) * P], N2[:, c * TPC + j, :], ident[:])
                m.then_inc(hT_psum, 1)

            turn(0)
            for c in range(NCH):
                if c + 1 < NCH:
                    turn(c + 1)
                pe.wait_ge(gT_ready, c + 1)
                if c > 1:
                    pe.wait_ge(hP_ready, c - 1)
                pe.matmul(bank[2 + c % 2], sq[:], gT[:, c], start=True, stop=True).then_inc(sq_psum, 1)
            pe.wait_ge(taps_ready, 1)

            def u(c):
                pe.wait_ge(hP_ready, c + 1)
                first, second = (bank[4 + 2 * (c % 2) + j].rearrange("p (b t) -> p b t", t=S) for j in range(DH))
                if c > 1:
                    pe.wait_ge(u_ready, DH * (c - 2) + 1)
                for k in range(DC):
                    m = pe.matmul(first, wconv[:, k, :], hP[:, 2 * c:2 * c + 2, k:k + S],
                                  start=(k == 0), stop=(k == DC - 1))
                m.then_inc(u_psum, 1)
                if c > 1:
                    pe.wait_ge(conv_ready, c - 1)
                pe.matmul(second, win[:, P:DI], hP[:, 2 * c:2 * c + 2, PAD:PAD + S], start=True, stop=True
                          ).then_inc(u_psum, 1)

            def dbc(c):
                pe.wait_ge(u_ready, DH * (c + 1))
                pe.wait_ge(gT_ready, NCH)
                if c > 1:
                    pe.wait_ge(bc_read, c - 1)
                for h in range(DH):
                    m = pe.matmul(bank[c % 2][0:BCR + DR, :], wx[:, h, :], U[:, h, c * CH:(c + 1) * CH],
                                  start=(h == 0), stop=(h == DH - 1))
                m.then_inc(dbc_psum, 1)

            def dl(c):
                pe.wait_ge(dt_ready, c + 1)
                pe.wait_ge(hP_ready, NCH)
                for h in range(DH):
                    if c:
                        pe.wait_ge(dl_read, DH * (c - 1) + h + 1)
                    pe.matmul(bank[2 + h], wdt[:, h * P:(h + 1) * P], dtT[:, c * CH:(c + 1) * CH],
                              start=True, stop=True).then_inc(dl_psum, 1)

            over_chunks(u, dbc, dl)
            pe.wait_ge(u_ready, DH * NCH)
            for i in range(DH * NCH):
                c, h = i // DH, i % DH
                if i > 3:
                    pe.wait_ge(z_ready, i - 3)
                pe.matmul(bank[4 + i % 4].rearrange("p (b t) -> p b t", t=S), win[:, DI + h * P:DI + (h + 1) * P],
                          hP[:, 2 * c:2 * c + 2, PAD:PAD + S], start=True, stop=True).then_inc(z_psum, 1)
            pe.wait_ge(bc_ready, NCH)
            pe.wait_ge(dl_read, DH * NCH)
            pe.wait_ge(diag_ready, DH)
            pe.wait_ge(z_ready, DH * NCH)
            for hf in range(2):
                def spread(n, hf=hf):
                    m = hf * DS + n
                    for p, row, read, done in ((pB, 0, b_ready, b_psum), (pC, DS, c_ready, c_psum)):
                        if not (isinstance(m, int) and m == 0):
                            pe.wait_ge(read, m)
                        for c in range(HCH):
                            x = pe.matmul(p[:, c * CH:(c + 1) * CH],
                                          pick[:, bass.ds(n + row, 1)].to_broadcast([BCR, P]),
                                          BC[:, hf * TH + c * CH:hf * TH + (c + 1) * CH], start=True, stop=True)
                        x.then_inc(done, 1)

                def add(n, s, last=False):
                    for h in range(DH):
                        pe.wait_ge(hC_ready, (hf * DS + n) * DH + h + 1)
                        for c in range(HCH):
                            x = pe.matmul(acc[2 * h + c][:], ident[:], hC[s][h][:, c * CH:(c + 1) * CH],
                                          start=False, stop=last)
                        x.then_inc(hC_used, 1)

                def one(n, s):
                    first, last = isinstance(n, int) and n == 0, isinstance(n, int) and n == DS - 1
                    if first and hf == 0:
                        spread(0)
                    if not last:
                        spread(n + 1)
                    elif hf == 0:
                        spread(0, hf=1)
                    if first:
                        if hf:
                            pe.wait_ge(y_gated, DH * HCH)
                        for h in range(DH):
                            for c in range(HCH):
                                pe.matmul(acc[2 * h + c][:], diagD[:, h],
                                          U[:, h, hf * TH + c * CH:hf * TH + (c + 1) * CH], start=True, stop=False)
                    else:
                        add(n - 1, 1 - s)

                over_states(pe, one)
                add(DS - 1, 1, last=True)
            pe.wait_ge(y_gated, 2 * DH * HCH)
            pe.wait_ge(b_ready, 2 * DS)
            pe.wait_ge(c_ready, 2 * DS)

            def project(c):
                for h in range(DH):
                    m = pe.matmul(bank[c], wout[:, h, :], SZ[:, h, c * CH:(c + 1) * CH],
                                  start=(h == 0), stop=(h == DH - 1))
                m.then_inc(out_psum, 1)

            def turn_back(c):
                pe.wait_ge(g_ready, c + 1)
                for j in range(TPC):
                    t = c * TPC + j
                    m = pe.transpose(bank[c][:, j * P:(j + 1) * P], U[:, 0, t * P:(t + 1) * P], ident[:])
                m.then_inc(tok_psum, 1)

            project(0)
            for c in range(NCH):
                if c + 1 < NCH:
                    project(c + 1)
                pe.wait_ge(out_ready, c + 1)
                pe.matmul(bank[4 + c], srw[:], gT[:, c], start=True, stop=True).then_inc(srw_psum, 1)
                if c:
                    turn_back(c - 1)
            turn_back(NCH - 1)


RE, RH = 8, 512
NR = RE - 1
RT = RH // P
XW = E + 4
TILES = NT + NR
NROW = TILES * P
ALPHA = 2.0


def switch(nc, io, X, ident, xs, ys, out):
    with ExitStack() as ctx:
        def sb(name, shape, dt=F32):
            return ctx.enter_context(nc.sbuf_tensor("s_" + name, shape, dt))

        def psum(name, shape, dt=F32):
            return ctx.enter_context(nc.psum_tensor("s_" + name, shape, dt))

        sem = ctx.enter_context(semaphores(nc, "s_"))

        R4, Y = sb("r4", [P, NT, XW]), sb("y", [P, NT, E])
        Hn = R4[:, :, 0:E]
        hT, ST = sb("hT", [P, TOK]), sb("st", [P, TOK])
        rw = sb("rw", [P, RE])
        sug, sd = sb("sug", [P, 2, RH]), sb("sd", [P, RT, E])
        UG = sb("ug", [P, NR, 2, RH])
        DW = sb("dw", [P, NR, RT, E])
        zero = sb("zero", [P, TILES * XW])
        pr = [sb(f"pr{i}", [P, NT, RE]) for i in range(5)]
        small = sb("small", [P, 4, NT])
        rev = sb("rev", [P, RE])
        revi = sb("revi", [P, RE], I32)
        jrow, ji = sb("jrow", [P, TILES]), sb("ji", [P, TILES], I32)
        hot = sb("hot", [P, NT, RE], BF16)
        tri, ones = sb("tri", [P, P], BF16), sb("ones", [P, P], BF16)
        carry = sb("carry", [P, RE, NT])
        tot, inc, exc = (sb(n, [P, RE, NT]) for n in ("tot", "inc", "exc"))
        cnt = sb("cnt", [P, 6, RE])
        cnti = sb("cnti", [P, RE], I32)
        ge = sb("ge", [P, TILES, NR - 1])
        eidf, eid = sb("eidf", [P, TILES]), sb("eid", [P, TILES], I32)
        posf, pos = sb("posf", [P, NT]), sb("pos", [P, NT], I32)
        sgate = sb("sgate", [P, 2, CH])
        sact = sb("sact", [P, 2, RT, CH])
        xt = [sb(f"xt{i}", [P, XW]) for i in range(4)]
        xT = [sb(f"xT{i}", [P, P]) for i in range(2)]
        gl = [sb(f"gl{i}", [P, RH]) for i in range(2)]
        hid = [sb(f"hid{i}", [P, RH]) for i in range(2)]
        hidT = [sb(f"hidT{i}", [P, RT, P]) for i in range(2)]
        yt = [sb(f"yt{i}", [P, E]) for i in range(2)]
        back = sb("back", [P, NT, E])

        pu = [psum(f"pu{i}", [P, CH]) for i in range(2)]
        pg = [psum(f"pg{i}", [P, CH]) for i in range(2)]
        ph, px_, py_, pr_ = psum("ph", [P, RT, P]), psum("px", [P, CH]), psum("py", [P, CH]), psum("pr", [P, CH])
        px, py = px_[:, 0:P], py_[:, 0:E]
        back_bank = [ph[:].rearrange("p a b -> p (a b)"), px_[:], py_[:], pu[0][:]]

        routed_loaded = sem("routed_loaded")
        loaded, cleared, zero_ready = sem("loaded"), sem("cleared"), sem("zero_ready")
        norms, normed = Norms(sb, sem, 2), sem("normed")
        hT_psum, hT_ready = sem("hT_psum"), sem("hT_ready")
        logits_psum, centred, exp_ready, const_ready = (
            sem("logits_psum"), sem("centred"), sem("exp_ready"), sem("const_ready"))
        hot_ready, counts_psum, pos_ready, eid_ready = (
            sem("hot_ready"), sem("counts_psum"), sem("pos_ready"), sem("eid_ready"))
        sorted_ = sem("sorted")
        sh_psum, sh_silu, sh_gated, sd_psum, sd_read = (
            sem("sh_psum"), sem("sh_silu"), sem("sh_gated"), sem("sd_psum"), sem("sd_read"))
        x_in = [sem(f"x_in{i}") for i in range(4)]
        xT_psum, xT_ready, ug_psum, silu_ready, hid_ready = (
            sem("xT_psum"), sem("xT_ready"), sem("ug_psum"), sem("silu_ready"), sem("hid_ready"))
        hT2_psum, hT2_ready, y_psum, y_ready, y_out = (
            sem("hT2_psum"), sem("hT2_ready"), sem("y_psum"), sem("y_ready"), [sem("y_out0"), sem("y_out1")])
        zrow_out, returned, shared_psum, final_ready, out_done = (
            sem("zrow_out"), [sem(f"returned{i}") for i in range(NCH)], sem("shared_psum"),
            sem("final_ready"), sem("out_done"))
        dve_step, pool_step = sem("dve_step"), sem("pool_step")

        block = ctx.enter_context(nc.Block())

        @block.sync
        def _(sp):
            sp.dma_start(rw[:], io["router_w"]).then_inc(loaded, 16)
            sp.dma_start(sug[:], io["sug"]).then_inc(loaded, 16)
            sp.dma_start(sd[:], io["sdw"]).then_inc(loaded, 16)
            sp.dma_start(UG[:], io["ug"]).then_inc(routed_loaded, 16)
            sp.dma_start(DW[:], io["dw"]).then_inc(routed_loaded, 16)
            sp.wait_ge(zero_ready, 1)
            sp.dma_start(xs.rearrange("(p r) c -> p (r c)", p=P), zero[:]).then_inc(cleared, 16)
            sp.dma_start(ys[NROW:NROW + 1, :], zero[0:1, 0:E]).then_inc(zrow_out, 16)
            sp.wait_ge(sorted_, 16 * NT)
            src = xs.rearrange("(t p) c -> t p c", p=P)
            dst = ys[0:NROW].rearrange("(t p) c -> t p c", p=P)

            def load(j, s):
                sp.dma_start(xt[s][:], src[bass.ds(j, 1)].rearrange("t p c -> (t p) c")).then_inc(x_in[s], 16)

            def store(j, s):
                sp.wait_ge(y_ready, j + 1)
                sp.dma_start(dst[bass.ds(j, 1)].rearrange("t p c -> (t p) c"), yt[s][:]).then_inc(y_out[s], 16)

            for j in range(4):
                load(j, j)
            with sp.Fori(0, (TILES - 4) // 4) as i:
                for s in range(4):
                    sp.wait_ge(hid_ready, 4 * i + s + 1)
                    load(4 * i + s + 4, s)
                    store(4 * i + s, s % 2)
            done = (TILES - 4) // 4 * 4
            for j in range(done, TILES):
                if j + 4 < TILES:
                    sp.wait_ge(hid_ready, j + 1)
                    load(j + 4, j % 4)
                store(j, j % 2)
            by_tile = out.rearrange("b (t p) e -> p (b t) e", p=P)
            for c in range(NCH):
                sp.wait_ge(final_ready, c + 1)
                sp.dma_start(by_tile[:, c * TPC:(c + 1) * TPC], X[:, c * TPC:(c + 1) * TPC]).then_inc(out_done, 16)
            sp.wait_ge(out_done, 16 * NCH)

        @block.gpsimd
        def _(pool):
            step = Steps(pool, pool_step)
            pool.memset(zero[:], 0.0).then_inc(zero_ready, 1)
            norms.prepare(pool)
            step.then(pool.iota(revi[:], pattern=[[-1, RE]], base=RE, channel_multiplier=0))
            step.then(pool.iota(ji[:], pattern=[[1, TILES]], base=0, channel_multiplier=0))
            step.then(pool.tensor_copy(rev[:], revi[:]))
            step.then(pool.tensor_copy(jrow[:], ji[:]))
            step.then(pool.memset(ones[:], 1.0))
            step.then(pool.affine_select(out=tri[:], in_=ones[:], compare_op=ALU.is_gt, fill=0.0, base=0,
                                         pattern=[[1, P]], channel_multiplier=-1))
            step.then(pool.memset(carry[:], 1.0))
            pool.memset(carry[:, :, 0:1], 0.0).then_inc(const_ready, 1)
            pool.wait_ge(const_ready, 1)
            norms.roots(pool, step, 0)
            pool.wait_ge(pos_ready, 1)
            pool.wait_ge(cleared, 16)
            for t in range(NT):
                pool.indirect_dma_start(xs, bass.IndirectOffsetOnAxis(ap=pos[:, t:t + 1], axis=0), R4[:, t, :], None,
                                        bounds_check=NROW - 1, oob_is_err=False).then_inc(sorted_, 16)
            pool.wait_ge(y_out[0], 16 * ((TILES + 1) // 2))
            pool.wait_ge(y_out[1], 16 * (TILES // 2))
            pool.wait_ge(zrow_out, 16)
            for t in range(NT):
                pool.indirect_dma_start(back[:, t, :], None, ys, bass.IndirectOffsetOnAxis(ap=pos[:, t:t + 1], axis=0)
                                        ).then_inc(returned[t // TPC], 16)
            norms.roots(pool, step, 1)

        def tile_loop(eng, one):
            for j in range(3):
                one(j, j % 2)
            with eng.Fori(1, (TILES - 3) // 2) as i:
                one(2 * i + 1, 1)
                one(2 * i + 2, 0)
            one(TILES - 2, 1)
            one(TILES - 1, 0)

        @block.scalar
        def _(act):
            for c in range(NCH):
                act.wait_ge(hT_psum, c + 1)
                act.activation(hT[:, c * CH:(c + 1) * CH], pu[c % 2][:], ACT.Copy).then_inc(hT_ready, 1)
            act.wait_ge(centred, 1)
            act.activation(pr[1][:], pr[0][:], ACT.Exp).then_inc(exp_ready, 1)

            def shared_silu(c, half):
                for j in range(half * RT // 2, (half + 1) * RT // 2):
                    n = c * RT + j
                    act.wait_ge(sh_psum, n + 1)
                    if n >= 2:
                        act.wait_ge(sh_gated, n - 1)
                    act.activation(sgate[:, n % 2], pg[n % 2][:], ACT.Silu).then_inc(sh_silu, 1)

            def shared_read(c):
                act.wait_ge(sd_psum, c + 1)
                act.activation(ST[:, c * CH:(c + 1) * CH], pr_[:], ACT.Copy).then_inc(sd_read, 1)

            def shared_pair(c):
                shared_silu(c, 0)
                shared_silu(c, 1)
                shared_silu(c + 1, 0)
                shared_read(c)
                shared_silu(c + 1, 1)
                shared_read(c + 1)

            shared_pair(0)

            def turned(j, s):
                act.wait_ge(xT_psum, j + 1)
                if not (isinstance(j, int) and j < 2):
                    act.wait_ge(ug_psum, j - 1)
                act.activation(xT[s][:], px, ACT.Copy).then_inc(xT_ready, 1)

            def silu(j, s):
                act.wait_ge(ug_psum, j + 1)
                if not (isinstance(j, int) and j < 2):
                    act.wait_ge(hid_ready, j - 1)
                act.activation(gl[s][:], pg[s][:], ACT.Silu).then_inc(silu_ready, 1)

            def hidden_turned(j, s):
                act.wait_ge(hT2_psum, j + 1)
                if not (isinstance(j, int) and j < 2):
                    act.wait_ge(y_psum, j - 1)
                act.activation(hidT[s][:], ph[:], ACT.Copy).then_inc(hT2_ready, 1)

            turned(0, 0)
            turned(1, 1)
            silu(0, 0)

            def one(j, s):
                if not (isinstance(j, int) and j >= TILES - 2):
                    turned(j + 2, s)
                if not (isinstance(j, int) and j >= TILES - 1):
                    silu(j + 1, 1 - s)
                hidden_turned(j, s)

            tile_loop(act, one)
            shared_pair(2)

        @block.vector
        def _(dve):
            v = dve
            step = Steps(dve, dve_step)
            norms.rows(dve, step, 0, X, Hn, normed)
            dve.wait_ge(logits_psum, 1)
            lg = pr_[:, 0:NT * RE].rearrange("p (t e) -> p t e", e=RE)
            step.then(v.tensor_reduce(small[:, 0], lg, AX.X, ALU.max))
            v.tensor_tensor(pr[0][:], lg, per_row(small[:, 0], RE), ALU.subtract).then_inc(centred, 1)
            dve.wait_ge(exp_ready, 1)
            step.then(v.tensor_reduce(small[:, 1], pr[1][:], AX.X, ALU.add))
            step.then(v.reciprocal(small[:, 2], small[:, 1]))
            step.then(v.tensor_tensor(pr[0][:], pr[1][:], per_row(small[:, 2], RE), ALU.mult))
            step.then(v.tensor_reduce(small[:, 3], pr[0][:], AX.X, ALU.max))
            step.then(v.tensor_tensor(pr[1][:], pr[0][:], per_row(small[:, 3], RE), ALU.is_equal))
            dve.wait_ge(const_ready, 1)
            revb = rev[:].unsqueeze(1).to_broadcast([P, NT, RE])
            step.then(v.tensor_tensor(pr[2][:], pr[1][:], revb, ALU.mult))
            step.then(v.tensor_reduce(small[:, 0], pr[2][:], AX.X, ALU.max))
            step.then(v.tensor_tensor(pr[3][:], revb, per_row(small[:, 0], RE), ALU.is_equal))
            step(v.tensor_scalar(R4[:, :, E:XW], small[:, 3].unsqueeze(2).to_broadcast([P, NT, XW - E]), ALPHA, None,
                                 ALU.mult))
            v.tensor_copy(hot[:], pr[3][:]).then_inc(hot_ready, 1)
            dve.wait_ge(counts_psum, 1)
            before = pr_[:, 0:NT * RE].rearrange("p (t e) -> p t e", e=RE)
            totals = pr_[:, NT * RE:2 * NT * RE].rearrange("p (t e) -> p e t", e=RE)
            step.then(v.tensor_copy(tot[:], totals))
            flat = "p e t -> p (e t)"
            step.then(v.tensor_tensor_scan(inc[:].rearrange(flat), carry[:].rearrange(flat), tot[:].rearrange(flat),
                                           0.0, ALU.mult, ALU.add))
            step.then(v.tensor_tensor(exc[:], inc[:], tot[:], ALU.subtract))
            step.then(v.tensor_scalar(cnti[:], inc[:, :, NT - 1], float(P - 1), None, ALU.add))
            step.then(v.tensor_single_scalar(cnti[:], cnti[:], 7, ALU.logical_shift_right))
            step.then(v.tensor_copy(cnt[:, 0], cnti[:]))
            step.then(v.memset(cnt[:, 1], 1.0))
            step.then(v.tensor_tensor_scan(cnt[:, 2], cnt[:, 1], cnt[:, 0], 0.0, ALU.mult, ALU.add))
            step.then(v.tensor_tensor(cnt[:, 3], cnt[:, 2], cnt[:, 0], ALU.subtract))
            step.then(v.tensor_scalar(cnt[:, 4], cnt[:, 3], float(P), None, ALU.mult))
            step.then(v.tensor_tensor(pr[0][:], before, exc[:].rearrange("p e t -> p t e"), ALU.add))
            step.then(v.tensor_tensor(pr[1][:], pr[0][:], cnt[:, 4:5].to_broadcast([P, NT, RE]), ALU.add))
            step.then(v.memset(pr[1][:, :, NR:RE], float(NROW)))
            step.then(v.tensor_tensor(pr[2][:], pr[1][:], pr[3][:], ALU.mult))
            step.then(v.tensor_reduce(posf[:], pr[2][:], AX.X, ALU.add))
            v.tensor_copy(pos[:], posf[:]).then_inc(pos_ready, 1)
            step.then(v.tensor_tensor(ge[:], per_row(jrow[:], NR - 1),
                                      cnt[:, 2:3, 0:NR - 1].to_broadcast([P, TILES, NR - 1]), ALU.is_ge))
            step.then(v.tensor_reduce(eidf[:], ge[:], AX.X, ALU.add))
            v.tensor_copy(eid[:], eidf[:]).then_inc(eid_ready, 1)

            def shared(c):
                for j in range(RT):
                    n = c * RT + j
                    dve.wait_ge(sh_silu, n + 1)
                    if c >= 2 and j == 0:
                        dve.wait_ge(sd_psum, c - 1)
                    v.tensor_tensor(sact[:, c % 2, j], sgate[:, n % 2], pu[n % 2][:], ALU.mult).then_inc(sh_gated, 1)

            shared(0)
            shared(1)

            def gate4(j, s4, k4):
                s = s4 % 2
                dve.wait_ge(silu_ready, j + 1)
                dve.wait_ge(x_in[s4], 16 * (k4 + 1))
                if not (isinstance(j, int) and j < 2):
                    dve.wait_ge(hT2_psum, j - 1)
                v.scalar_tensor_tensor(hid[s][:], pu[s][:], xt[s4][:, E:E + 1], gl[s][:], ALU.mult, ALU.mult
                                       ).then_inc(hid_ready, 1)

            def result(j, s, k, first=False):
                dve.wait_ge(y_psum, j + 1)
                if not first:
                    dve.wait_ge(y_out[s], 16 * k)
                v.tensor_copy(yt[s][:], py).then_inc(y_ready, 1)

            gate4(0, 0, 0)
            gate4(1, 1, 0)
            gate4(2, 2, 0)
            result(0, 0, 0, True)
            gate4(3, 3, 0)
            result(1, 1, 0, True)
            with dve.Fori(1, TILES // 4) as i:
                for s4 in range(4):
                    gate4(4 * i + s4, s4, i)
                    result(4 * i + s4 - 2, s4 % 2, 2 * i + s4 // 2 - 1)
            for j in range(TILES // 4 * 4, TILES):
                gate4(j, j % 4, j // 4)
                result(j - 2, j % 2, j // 2 - 1)
            for j in (TILES - 2, TILES - 1):
                result(j, j % 2, j // 2)

            def add_up(c):
                dve.wait_ge(returned[c], 16 * TPC)
                dve.wait_ge(shared_psum, c + 1)
                step.then(v.tensor_tensor(Y[:, c * TPC:(c + 1) * TPC], back[:, c * TPC:(c + 1) * TPC],
                                          back_bank[c].rearrange("p (t e) -> p t e", e=E), ALU.add))
                norms.statistics(dve, step, 1, c, Y)

            shared(2)
            shared(3)
            add_up(0)
            add_up(1)
            norms.residual(dve, step, 1, 0, Y, X, final_ready)
            add_up(2)
            norms.residual(dve, step, 1, 1, Y, X, final_ready)
            add_up(3)
            norms.residual(dve, step, 1, 2, Y, X, final_ready)
            norms.residual(dve, step, 1, 3, Y, X, final_ready)

        @block.tensor
        def _(pe):
            pe.wait_ge(loaded, 16 * 3)
            for c in range(NCH + 1):
                if c < NCH:
                    pe.wait_ge(normed, c + 1)
                    if c >= 2:
                        pe.wait_ge(hT_ready, c - 1)
                    for j in range(TPC):
                        m = pe.transpose(pu[c % 2][:, j * P:(j + 1) * P], Hn[:, c * TPC + j, :], ident[:])
                    m.then_inc(hT_psum, 1)
                if c:
                    pe.wait_ge(hT_ready, c)
                    for t in range((c - 1) * TPC, c * TPC):
                        m = pe.matmul(pr_[:, t * RE:(t + 1) * RE], hT[:, t * P:(t + 1) * P], rw[:],
                                      start=True, stop=True)
            m.then_inc(logits_psum, 1)

            def shared_up(c, tiles):
                at = slice(c * CH, (c + 1) * CH)
                for j in tiles:
                    n = c * RT + j
                    if n >= 2:
                        pe.wait_ge(sh_gated, n - 1)
                    pe.matmul(pg[n % 2][:], sug[:, 1, j * P:(j + 1) * P], hT[:, at], start=True, stop=True)
                    pe.matmul(pu[n % 2][:], sug[:, 0, j * P:(j + 1) * P], hT[:, at], start=True, stop=True
                              ).then_inc(sh_psum, 1)

            def shared_down(c):
                pe.wait_ge(sh_gated, (c + 1) * RT)
                if c:
                    pe.wait_ge(sd_read, c)
                else:
                    pe.wait_ge(pos_ready, 1)
                for j in range(RT):
                    m = pe.matmul(pr_[:], sd[:, j, :], sact[:, c % 2, j, :], start=(j == 0), stop=(j == RT - 1))
                m.then_inc(sd_psum, 1)

            def turn_back(c):
                pe.wait_ge(sd_read, c + 1)
                for j in range(TPC):
                    m = pe.transpose(back_bank[c][:, j * P:(j + 1) * P],
                                     ST[:, (c * TPC + j) * P:(c * TPC + j + 1) * P], ident[:])
                m.then_inc(shared_psum, 1)

            shared_up(0, [0])
            pe.wait_ge(hot_ready, 1)
            pe.wait_ge(const_ready, 1)
            hots = hot[:].rearrange("p t e -> p (t e)")
            pe.matmul(pr_[:, 0:NT * RE], tri[:], hots, start=True, stop=True)
            pe.matmul(pr_[:, NT * RE:2 * NT * RE], ones[:], hots, start=True, stop=True).then_inc(counts_psum, 1)
            shared_up(0, range(1, RT))
            shared_up(1, range(RT // 2))
            shared_down(0)
            shared_up(1, range(RT // 2, RT))
            shared_down(1)

            def turn(j, s4, k4):
                pe.wait_ge(x_in[s4], 16 * (k4 + 1))
                if not (isinstance(j, int) and j == 0):
                    pe.wait_ge(xT_ready, j)
                pe.transpose(px, xt[s4][:, 0:E], ident[:]).then_inc(xT_psum, 1)

            def up(j, s):
                e = pe.value_load(eid[0:1, bass.ds(j, 1)], min_val=0, max_val=NR - 1)
                pe.wait_ge(xT_ready, j + 1)
                if not (isinstance(j, int) and j < 2):
                    pe.wait_ge(hid_ready, j - 1)
                pe.matmul(pg[s][:], xT[s][:], UG[:, bass.ds(e, 1), 1, :].rearrange("p a h -> p (a h)"),
                          start=True, stop=True)
                pe.matmul(pu[s][:], xT[s][:], UG[:, bass.ds(e, 1), 0, :].rearrange("p a h -> p (a h)"),
                          start=True, stop=True).then_inc(ug_psum, 1)

            def hidden(j, s):
                pe.wait_ge(hid_ready, j + 1)
                if not (isinstance(j, int) and j == 0):
                    pe.wait_ge(hT2_ready, j)
                for i in range(RT):
                    m = pe.transpose(ph[:, i, :], hid[s][:, i * P:(i + 1) * P], ident[:])
                m.then_inc(hT2_psum, 1)

            def down(j, s):
                e = pe.value_load(eid[0:1, bass.ds(j, 1)], min_val=0, max_val=NR - 1)
                pe.wait_ge(hT2_ready, j + 1)
                if not (isinstance(j, int) and j == 0):
                    pe.wait_ge(y_ready, j)
                for i in range(RT):
                    m = pe.matmul(py, hidT[s][:, i, :], DW[:, bass.ds(e, 1), i, :].rearrange("p a h -> p (a h)"),
                                  start=(i == 0), stop=(i == RT - 1))
                m.then_inc(y_psum, 1)

            pe.wait_ge(routed_loaded, 32)
            pe.wait_ge(eid_ready, 1)
            pe.wait_ge(sh_gated, 2 * RT)

            def one(j, s4, k4):
                last = isinstance(j, int)
                if not (last and j >= TILES - 2):
                    turn(j + 2, (s4 + 2) % 4, k4 + (s4 + 2) // 4)
                if not (last and j >= TILES - 1):
                    up(j + 1, (s4 + 1) % 2)
                if not (last and j == 0):
                    down(j - 1, (s4 + 1) % 2)
                hidden(j, s4 % 2)

            turn(0, 0, 0)
            turn(1, 1, 0)
            up(0, 0)
            for j in range(4):
                one(j, j, 0)
            with pe.Fori(1, TILES // 4) as i:
                for s4 in range(4):
                    one(4 * i + s4, s4, i)
            for j in range(TILES // 4 * 4, TILES):
                one(j, j % 4, j // 4)
            down(TILES - 1, (TILES - 1) % 2)
            pe.wait_ge(hid_ready, TILES)
            shared_up(2, range(RT))
            shared_up(3, range(RT // 2))
            shared_down(2)
            shared_up(3, range(RT // 2, RT))
            pe.wait_ge(y_ready, TILES)
            turn_back(0)
            turn_back(1)
            shared_down(3)
            turn_back(2)
            turn_back(3)


def sandwich(nc, io, out):
    rows = nc.dram_tensor("expert_rows", (TOK, ROWW), F32, kind="Internal").ap()
    results = nc.dram_tensor("pick_results", (NZ, E), F32, kind="Internal").ap()
    slots = nc.dram_tensor("expert_slots", (NSLOT,), F32, kind="Internal").ap()
    xs = nc.dram_tensor("sorted_rows", (NROW, XW), F32, kind="Internal").ap()
    ys = nc.dram_tensor("sorted_results", (NROW + 1, E), F32, kind="Internal").ap()
    with ExitStack() as ctx:
        X = ctx.enter_context(nc.sbuf_tensor("X", [P, NT, E], F32))
        ident = ctx.enter_context(nc.sbuf_tensor("identity", [P, P], F32))
        attention(nc, io, X, ident, results)
        with ExitStack() as ffn:
            ST = ffn.enter_context(nc.sbuf_tensor("shared_T", [P, TOK], F32))
            tab = ffn.enter_context(nc.sbuf_tensor("row_table", [P, NG, 2, GC], I32))
            W1 = [ffn.enter_context(nc.sbuf_tensor(f"w1_{i}", [P, GE, 2 * FF], F32)) for i in range(2)]
            W2 = [ffn.enter_context(nc.sbuf_tensor(f"w2_{i}", [P, GE, FT, E], F32)) for i in range(2)]
            route(nc, io, X, ident, rows, slots, tab, ST, W1, W2)
            experts(nc, io, ident, rows, results, tab, W1, W2)
            combine(nc, io, X, ident, results, ST)
        mamba(nc, io, X, ident)
        switch(nc, io, X, ident, xs, ys, out)


def kernel(**inputs):
    import numpy as np
    import concourse.bacc as bacc
    from concourse.bass_utils import run_bass_kernel_spmd

    a = {name: np.asarray(value) for name, value in inputs.items()}

    def attn(name):
        return a["L0_attn_" + name]

    def moe(name):
        return a["L0_ffn_" + name]

    def mix(name):
        return a["L1_attn_" + name]

    def sw(name):
        return a["L1_ffn_" + name]

    def by_feature(w):
        return w.reshape(w.shape[:-1] + (H, D)).swapaxes(-1, -2).reshape(w.shape)

    Jd = np.zeros((E, E), np.float32)
    for h in range(H):
        Jd[h::H, h::H] = attn("J_attn")[h]
    own = np.zeros((P, GC, GE), np.float32)
    for r in range(GR):
        own[r % P, r // P, r // CAP] = 1
    bc_rows = 2 * DS
    pick = np.zeros((3 * bc_rows, bc_rows), np.float32)
    for r in range(3 * bc_rows):
        pick[r, r % bc_rows] = 1
    xp = mix("x_proj_w")
    arrays = dict(
        x=attn("x"), ident=np.eye(P, dtype=np.float32),
        WqT=by_feature(attn("Wq").T), WkT=by_feature(attn("Wk").T), WvT=attn("Wv").T, WoT=attn("Wo").T, Jd=Jd,
        bq=by_feature(attn("bq")), bk=by_feature(attn("bk")), bv=attn("bv"), bo=attn("bo"),
        lam=attn("lambda_attn").reshape(1),
        wgT=moe("wg").T, sw1T=moe("shared_w1").T, sw2T=moe("shared_w2").T.reshape(FT, P, E).transpose(1, 0, 2),
        w1T=moe("expert_w1").reshape(NG, GE, 2 * FF, E).transpose(0, 3, 1, 2),
        w2T=moe("expert_w2").reshape(NG, GE, E, FT, P).transpose(0, 4, 1, 3, 2), own=own,
        sq_w=mix("sq_w"), srw_w=mix("srw_w"), in_proj_w=mix("in_proj_w"), dt_w=mix("dt_w"), pick=pick,
        x_proj=np.concatenate([xp[:, DR:]] * 3 + [xp[:, :DR]], 1), out_proj_w=mix("out_proj_w"),
        A_log=mix("A_log"), conv_w=mix("conv_w"), conv_wT=mix("conv_w").T, m_g=mix("ln_g"),
        m_b=mix("ln_b"), m_sq_b=mix("sq_b"),
        m_srw_b=mix("srw_b"), res_scale=mix("res_scale"), m_conv_b=mix("conv_b"), m_dt_b=mix("dt_b"), m_D=mix("D"),
        router_w=sw("router_w"), sug=np.stack([sw("shared_up_w"), sw("shared_gate_w")], 1),
        sdw=sw("shared_down_w").reshape(RT, P, E).transpose(1, 0, 2),
        ug=np.stack([sw("up_w"), sw("gate_w")], 1).transpose(2, 0, 1, 3),
        dw=sw("down_w").reshape(NR, RT, P, E).transpose(2, 0, 1, 3))

    nc = bacc.Bacc("TRN2", target_bir_lowering=False, num_devices=1)
    io, fed = {}, {}
    for name, array in arrays.items():
        fed[f"in_{name}_dram"] = np.ascontiguousarray(array)
        io[name] = nc.dram_tensor(f"in_{name}_dram", array.shape, mybir.dt.from_np(array.dtype),
                                  kind="ExternalInput").ap()
    out = nc.dram_tensor("out_dram", (NB, S, E), F32, kind="ExternalOutput").ap()
    sandwich(nc, io, out)
    r = run_bass_kernel_spmd(nc, [fed], core_ids=[0])
    return r.results[0]["out_dram"]
```
